# Optimizing a Trainium2 kernel written in Bass

```python
import numpy as np
import jax
import jax.numpy as jnp

def _softmax(x, axis=-1):
    return jax.nn.softmax(x, axis=axis)

def _gelu(x):
    return jax.nn.gelu(x, approximate=True)

def _silu(x):
    return jax.nn.silu(x)

def _sigmoid(x):
    return jax.nn.sigmoid(x)

def _layernorm(x, axis=-1, eps=1e-05):
    m = jnp.mean(x, axis=axis, keepdims=True)
    v = jnp.var(x, axis=axis, keepdims=True)
    return (x - m) / jnp.sqrt(v + eps)

def _scatter_add(tgt, idx, src, axis=0):
    return tgt.at[idx].add(src)

def _segment_sum(src, seg, n):
    return jax.ops.segment_sum(src, seg, n)
kernel_name = 'mk_gnn_preln_d2_gnn_r8_c546da'

def setup_inputs(seed: int=0):
    np.random.seed(seed)
    _w = jnp.asarray

    def _rec_inputs():
        import jax
        import jax.numpy as jnp
        _gk = jax.random.key(seed)
        x = -1.857e-05 + 0.05 * jax.random.normal(jax.random.fold_in(_gk, 1), (12500, 128), jnp.float32)
        src = jax.random.randint(jax.random.fold_in(_gk, 2), (200000,), 0, 12500, jnp.int32)
        dst = jnp.minimum((12500 * jax.random.uniform(jax.random.fold_in(_gk, 3), (200000,)) ** 2.0).astype(jnp.int32), 99999)
        _o = jnp.argsort(dst, stable=True)
        src = src[_o]
        dst = dst[_o]
        edge_type_200 = jax.random.randint(jax.random.fold_in(_gk, 13), (200000,), 0, 200, jnp.int32)
        edge_weight = jax.random.uniform(jax.random.fold_in(_gk, 14), (200000,), jnp.float32, 0.0, 0.999998)
        return (x, src, dst, edge_type_200, edge_weight)
    x, src, dst, edge_type_200, edge_weight = _rec_inputs()

    def _L0_gnn_setup():
        import jax, jax.numpy as jnp
        import numpy as np
        N_NODES = 12500
        N_REL = 200
        D = 128
        L = 2
        E = 62500

        def segment_softmax(e, idx, num_segments):
            m = jax.ops.segment_max(e, idx, num_segments=num_segments)
            m = jnp.where(jnp.isfinite(m), m, 0.0)
            ex = jnp.exp(e - m[idx])
            s = jax.ops.segment_sum(ex, idx, num_segments=num_segments)
            return ex / (s[idx] + 1e-16)
        key = jax.random.key(seed)
        ks = jax.random.split(key, 16)
        s = 0.05
        return {'entity_emb': jax.random.normal(ks[0], (N_NODES, D), jnp.float32) * s, 'rel_emb': jax.random.normal(ks[1], (N_REL, D), jnp.float32) * s, 'edge_conf': jax.random.uniform(ks[2], (E,), jnp.float32), 'Wv_w': jax.random.normal(ks[3], (L, D, D), jnp.float32) * s, 'Wv_b': jax.random.normal(ks[4], (L, D), jnp.float32) * s, 'W0_w': jax.random.normal(ks[5], (L, D, D), jnp.float32) * s, 'W0_b': jax.random.normal(ks[6], (L, D), jnp.float32) * s, 'A1_w': jax.random.normal(ks[7], (L, 3 * D, D), jnp.float32) * s, 'A1_b': jax.random.normal(ks[8], (L, D), jnp.float32) * s, 'A2_w': jax.random.normal(ks[9], (L, D), jnp.float32) * s, 'A2_b': jax.random.normal(ks[10], (L,), jnp.float32) * s, 'G_w': jax.random.normal(ks[11], (L,), jnp.float32) * s, 'G_b': jax.random.normal(ks[12], (L,), jnp.float32) * s, 'edge_index': jax.random.randint(ks[13], (2, E), 0, N_NODES, jnp.int64 if jax.config.jax_enable_x64 else jnp.int32), 'edge_type': jax.random.randint(ks[14], (E,), 0, N_REL, jnp.int64 if jax.config.jax_enable_x64 else jnp.int32)}
    _L0_gnn_all = _L0_gnn_setup()
    _L0_gnn_in = {k: v for k, v in _L0_gnn_all.items() if k in ('rel_emb', 'Wv_w', 'Wv_b', 'W0_w', 'W0_b', 'A1_w', 'A1_b', 'A2_w', 'A2_b', 'G_w', 'G_b')}
    del _L0_gnn_all

    def _L1_gnn_setup():
        import jax, jax.numpy as jnp
        import numpy as np
        N, D, E, OUT = (12500, 128, 75000, 128)
        key = jax.random.key(seed)
        k1, k2, k3, k4, k5 = jax.random.split(key, 5)
        x = jax.random.normal(k1, (N, D), dtype=jnp.float32)
        W = jax.random.normal(k2, (D, OUT), dtype=jnp.float32) * (1.0 / np.sqrt(D))
        b = jax.random.normal(k3, (OUT,), dtype=jnp.float32) * 0.01
        edge_src = jax.random.randint(k4, (E,), 0, N, dtype=jnp.int32)
        edge_dst = jnp.sort(jax.random.randint(k5, (E,), 0, N, dtype=jnp.int32))
        return {'x': x, 'W': W, 'b': b, 'edge_src': edge_src, 'edge_dst': edge_dst}
    _L1_gnn_all = _L1_gnn_setup()
    _L1_gnn_in = {k: v for k, v in _L1_gnn_all.items() if k in ('W', 'b')}
    del _L1_gnn_all
    return {'x': x, 'src': src, 'dst': dst, 'edge_type_200': edge_type_200, 'edge_weight': edge_weight, 'L0_gnn_rel_emb': _L0_gnn_in['rel_emb'], 'L0_gnn_Wv_w': _L0_gnn_in['Wv_w'], 'L0_gnn_Wv_b': _L0_gnn_in['Wv_b'], 'L0_gnn_W0_w': _L0_gnn_in['W0_w'], 'L0_gnn_W0_b': _L0_gnn_in['W0_b'], 'L0_gnn_A1_w': _L0_gnn_in['A1_w'], 'L0_gnn_A1_b': _L0_gnn_in['A1_b'], 'L0_gnn_A2_w': _L0_gnn_in['A2_w'], 'L0_gnn_A2_b': _L0_gnn_in['A2_b'], 'L0_gnn_G_w': _L0_gnn_in['G_w'], 'L0_gnn_G_b': _L0_gnn_in['G_b'], 'L1_gnn_W': _L1_gnn_in['W'], 'L1_gnn_b': _L1_gnn_in['b']}

def reference(x, src, dst, edge_type_200, edge_weight, L0_gnn_rel_emb, L0_gnn_Wv_w, L0_gnn_Wv_b, L0_gnn_W0_w, L0_gnn_W0_b, L0_gnn_A1_w, L0_gnn_A1_b, L0_gnn_A2_w, L0_gnn_A2_b, L0_gnn_G_w, L0_gnn_G_b, L1_gnn_W, L1_gnn_b):
    import jax
    import jax.numpy as jnp

    def _L0_gnn_ref(entity_emb, rel_emb, edge_conf, Wv_w, Wv_b, W0_w, W0_b, A1_w, A1_b, A2_w, A2_b, G_w, G_b, edge_index, edge_type):
        import jax, jax.numpy as jnp
        import numpy as np
        N_NODES = 12500
        N_REL = 200
        D = 128
        L = 2
        E = 62500

        def segment_softmax(e, idx, num_segments):
            m = jax.ops.segment_max(e, idx, num_segments=num_segments)
            m = jnp.where(jnp.isfinite(m), m, 0.0)
            ex = jnp.exp(e - m[idx])
            s = jax.ops.segment_sum(ex, idx, num_segments=num_segments)
            return ex / (s[idx] + 1e-16)
        src = edge_index[0]
        dst = edge_index[1]
        n = entity_emb.shape[0]
        x = entity_emb
        rf = rel_emb[edge_type]
        for l in range(Wv_w.shape[0]):
            xj = x[src]
            xi = x[dst]
            attn_in = jnp.concatenate([xj, rf, xi], axis=-1)
            h = jax.nn.leaky_relu(attn_in @ A1_w[l] + A1_b[l], negative_slope=0.2)
            e = h @ A2_w[l] + A2_b[l]
            alpha = segment_softmax(e, dst, n)
            gate = jax.nn.sigmoid(edge_conf * G_w[l] + G_b[l])
            base_msg = (xj @ Wv_w[l] + Wv_b[l]) * rf
            msg = (alpha * gate)[:, None] * base_msg
            agg = jax.ops.segment_sum(msg, dst, num_segments=n)
            x = jax.nn.relu(agg + x @ W0_w[l] + W0_b[l])
        return x

    def _L1_gnn_ref(x, W, b, edge_src, edge_dst):
        import jax, jax.numpy as jnp
        import numpy as np
        N, D, E, OUT = (12500, 128, 75000, 128)
        n = x.shape[0]
        neigh_sum = jax.ops.segment_sum(x[edge_src], edge_dst, num_segments=n)
        deg = jax.ops.segment_sum(jnp.ones((edge_dst.shape[0],), x.dtype), edge_dst, num_segments=n)
        neigh_mean = neigh_sum / jnp.maximum(deg, 1.0)[:, None]
        h = x + neigh_mean
        return jax.nn.relu(h @ W + b)
    edge_index = jnp.stack([src, dst])
    h = jnp.maximum(_layernorm(x, axis=-1), 0.0)
    x = x + _L0_gnn_ref(h, L0_gnn_rel_emb, edge_weight, L0_gnn_Wv_w, L0_gnn_Wv_b, L0_gnn_W0_w, L0_gnn_W0_b, L0_gnn_A1_w, L0_gnn_A1_b, L0_gnn_A2_w, L0_gnn_A2_b, L0_gnn_G_w, L0_gnn_G_b, edge_index, edge_type_200)
    h = jnp.maximum(_layernorm(x, axis=-1), 0.0)
    x = x + _L1_gnn_ref(h, L1_gnn_W, L1_gnn_b, src, dst)
    return x

_drawn_inputs = setup_inputs


def setup_inputs(seed=0):
    import zlib

    import numpy as np

    out = dict(_drawn_inputs(seed))
    spreads = {}
    factors = {'edge_weight': 8.0,
     'L0_gnn_rel_emb': 8.0,
     'L0_gnn_Wv_w': 8.0,
     'L0_gnn_Wv_b': 8.0,
     'L0_gnn_A1_w': 8.0,
     'L0_gnn_A1_b': 8.0,
     'L0_gnn_A2_w': 8.0,
     'L0_gnn_A2_b': 8.0,
     'L0_gnn_G_w': 8.0,
     'L0_gnn_G_b': 8.0,
     'L1_gnn_b': 7.795}
    for name, (base, spread) in spreads.items():
        noise = np.random.default_rng([zlib.crc32(name.encode()), seed]).standard_normal(out[name].shape)
        drawn = base * np.exp(spread * noise) if base else spread * noise
        out[name] = jnp.asarray(drawn.astype(out[name].dtype))
    for name, factor in factors.items():
        out[name] = (out[name] * factor).astype(out[name].dtype)
    return out
```

```python
from contextlib import ExitStack

import concourse.bass as bass
from concourse import mybir

F32 = mybir.dt.float32
BF16 = mybir.dt.bfloat16
I32 = mybir.dt.int32
ALU = mybir.AluOpType
ACT = mybir.ActivationFunctionType
AX = mybir.AxisListType
ENG = mybir.EngineType

P = 128
D = 128
NODES = 12500
EDGES = 200000
RELS = 200
LAYERS = 2
BLOCKS = -(-NODES // P)
FULL_BLOCKS = NODES // P
TAIL_NODES = NODES - FULL_BLOCKS * P
EDGE_TILES = -(-EDGES // P)
FULL_TILES = EDGES // P
TAIL_EDGES = EDGES - FULL_TILES * P
CHUNKS = -(-(EDGE_TILES + BLOCKS - 1) // P)
STEPS = CHUNKS * P
BATCH = 16
GROUP = 4
GPB = BATCH // GROUP
NBATCH = STEPS // BATCH
PAD_DST = BLOCKS * P
AW = D + 1
NEG = -1.0e30
EPS = 1e-5


class Kit:

    def __init__(self, nc, stack, tag=""):
        self.nc, self.stack, self.tag = nc, stack, tag
        self.sems = []

    def sb(self, name, shape, dt=F32):
        return self.stack.enter_context(self.nc.sbuf_tensor(self.tag + name, shape, dt))

    def ps(self, name, shape):
        size = 1
        for n in shape[1:]:
            size *= n
        bank = self.stack.enter_context(self.nc.psum_tensor(self.tag + name, [P, 512], F32))
        flat = bank[0:shape[0], 0:size]
        if len(shape) == 3:
            return flat.rearrange("p (a b) -> p a b", a=shape[1])
        return flat

    def sem(self, name):
        self.sems.append(self.stack.enter_context(self.nc.semaphore(self.tag + name)))
        return self.sems[-1]

    def gather_sem(self, root, name):
        return root.stack.enter_context(self.nc.semaphore(self.tag + name))

    def block(self):
        self.stack.callback(self.clear)
        return self.stack.enter_context(self.nc.Block())

    def clear(self):
        with self.nc.Block() as block:
            @block.gpsimd
            def _(pool):
                for sem in self.sems:
                    pool.sem_clear(sem)


def over_partitions(ap):
    return ap.partition_broadcast(P)


def row(ap):
    return ap.rearrange("(a n) -> a n", a=1)


def make_constants(nc, C):
    with ExitStack() as st:
        K = Kit(nc, st, "c_")
        iota_i = K.sb("iota_i", [P, P], I32)
        part_i = K.sb("part_i", [P, 2], I32)
        filled = K.sem("filled")
        made = K.sem("made")
        block = K.block()

        @block.gpsimd
        def _(pool):
            pool.memset(C.ident[:, :], 0.0).then_inc(filled, 1)
            pool.wait_ge(filled, 1)
            pool.affine_select(out=C.ident[:, :], in_=C.ident[:, :], compare_op=ALU.not_equal, fill=1.0,
                               base=0, pattern=[[-1, P]], channel_multiplier=1).then_inc(made, 1)
            pool.memset(C.ones[:, :], 1.0).then_inc(made, 1)
            pool.iota(iota_i[:, :], [[1, P]], 0, 0).then_inc(made, 1)
            pool.iota(part_i[:, :], [[P, 2]], 0, 1).then_inc(made, 1)

        @block.vector
        def _(dve):
            dve.wait_ge(made, 4)
            dve.tensor_copy(C.iota_free[:, :], iota_i[:, :])
            dve.tensor_copy(C.iota_part[:, :], part_i[:, :])


def plan_steps(nc, C, src, dst, etype, weight, gw, gb):
    with ExitStack() as st:
        K = Kit(nc, st, "p_")
        edges = K.sb("edges", [P, CHUNKS, 4, P], I32)
        steps = K.sb("steps", [P, CHUNKS, 4, P], I32)
        ends_f = K.sb("ends_f", [P, 2, CHUNKS])
        start_i = K.sb("start_i", [P, BLOCKS + 1], I32)
        start = K.sb("start", [P, BLOCKS + 1])
        below = K.sb("below", [P, 2, BLOCKS])
        count = K.sb("count", [P, 2, BLOCKS])
        npair = K.sb("npair", [P, BLOCKS])
        pair_end = K.sb("pair_end", [P, BLOCKS])
        shift = K.sb("shift", [P, BLOCKS])
        step_i = K.sb("step_i", [P, CHUNKS], I32)
        step_f = K.sb("step_f", [P, CHUNKS])
        table = K.sb("table", [P, CHUNKS, BLOCKS])
        facts = K.sb("facts", [P, 4, CHUNKS])
        tile_i = K.sb("tile_i", [P, CHUNKS], I32)
        base = K.sb("base", [P, CHUNKS])
        dst_g = K.sb("dst_g", [P, CHUNKS, P])
        dst_b = K.sb("dst_b", [P, CHUNKS, P])
        src_f = K.sb("src_f", [P, CHUNKS, P])
        masks = K.sb("masks", [P, CHUNKS, 3, P])
        rows = K.sb("rows", [P, CHUNKS, 2, P], BF16)
        col_i = K.sb("col_i", [P, 2, P], I32)
        col_f = K.sb("col_f", [P, 2, P])
        wcol = K.sb("wcol", [P, 2, P])
        gf = K.sb("gf", [P, 2, 3, P])
        gwb = K.sb("gwb", [P, 2 * LAYERS])
        facts_t = K.sb("facts_t", [4 * CHUNKS, P])
        now = K.sb("now", [NBATCH, 4, BATCH])
        nxt = K.sb("nxt", [NBATCH, 3, BATCH])
        flags = K.sb("flags", [NBATCH, 4, BATCH])
        ag = K.sb("ag", [NBATCH, 2, BATCH])
        blk_i = K.sb("blk_i", [NBATCH, BATCH], I32)
        zero = K.sb("zero", [4, BATCH])
        count_ps = K.ps("count_ps", [P, 2 * BLOCKS])
        facts_ps = K.ps("facts_ps", [4 * CHUNKS, P])
        turned_ps = [K.ps(f"turned_ps{i}", [P, 3, P]) for i in range(2)]
        first_ps = [K.ps(f"first_ps{i}", [P, P]) for i in range(2)]

        padded = K.sem("padded")
        loaded = K.sem("loaded")
        stored = K.sem("stored")
        counted = K.sem("counted")
        link = K.sem("link")
        summed = K.sem("summed")
        facts_ready = K.sem("facts_ready")
        facts_turned = K.sem("facts_turned")
        facts_copied = K.sem("facts_copied")
        facts_stored = K.sem("facts_stored")
        facts_back = K.sem("facts_back")
        gathered = K.gather_sem(C.root, "gathered")
        rows_ready = K.sem("rows_ready")
        rows_stored = K.sem("rows_stored")
        turned = K.sem("turned")
        copied = K.sem("copied")
        first_done = K.sem("first_done")
        gated = K.sem("gated")
        selected = K.sem("selected")
        gate_in = K.sem("gate_in")
        cols_stored = [K.sem(f"cols_stored{i}") for i in range(2)]
        last_ready = K.sem("last_ready")
        block = K.block()

        full_c = FULL_TILES // P
        rest = FULL_TILES - full_c * P
        fields = [src, dst, etype, weight.bitcast(I32)]

        @block.gpsimd
        def _(pool):
            pool.memset(edges[:, full_c:CHUNKS, :, :], 0).then_inc(padded, 1)
            pool.wait_ge(padded, 1)
            pool.memset(edges[:, full_c:CHUNKS, 1, :], PAD_DST).then_inc(padded, 1)
            pool.memset(zero[:, :], 0.0).then_inc(padded, 1)
            pool.iota(start_i[:, :], [[P, BLOCKS + 1]], 0, 0).then_inc(counted, 1)
            pool.iota(step_i[:, :], [[P, CHUNKS]], 0, 1).then_inc(counted, 1)
            pool.wait_ge(facts_ready, 1)
            pool.wait_ge(stored, 16)
            for c in range(CHUNKS):
                pool.indirect_dma_start(steps[:, c, :, :].rearrange("p f e -> p (f e)"), None, C.edge_tab,
                                        bass.IndirectOffsetOnAxis(ap=tile_i[:, c:c + 1], axis=0)
                                        ).then_inc(gathered, 16)

        @block.sync
        def _(sp):
            sp.wait_ge(padded, 3)
            for f, a in enumerate(fields):
                sp.dma_start(edges[:, 0:full_c, f, :],
                             a[0:full_c * P * P].rearrange("(c p e) -> p c e", p=P, e=P)).then_inc(loaded, 16)
                sp.dma_start(edges[0:rest, full_c, f, :],
                             a[full_c * P * P:FULL_TILES * P].rearrange("(p e) -> p e", e=P)).then_inc(loaded, 16)
                sp.dma_start(edges[rest:rest + 1, full_c, f, 0:TAIL_EDGES],
                             row(a[FULL_TILES * P:EDGES])).then_inc(loaded, 16)
            for i in range(LAYERS):
                sp.dma_start(gwb[:, 2 * i:2 * i + 1], over_partitions(row(gw[i:i + 1]))).then_inc(gate_in, 16)
                sp.dma_start(gwb[:, 2 * i + 1:2 * i + 2], over_partitions(row(gb[i:i + 1]))).then_inc(gate_in, 16)
            sp.dma_start(C.facts_tab[:, STEPS:STEPS + BATCH], zero[:, :]).then_inc(facts_stored, 16)
            sp.wait_ge(loaded, 16 * 3 * len(fields))
            sp.dma_start(C.edge_tab.rearrange("(c p) w -> p c w", p=P),
                         edges[:, :, :, :].rearrange("p c f e -> p c (f e)")).then_inc(stored, 16)
            sp.wait_ge(facts_copied, 1)
            for f in range(4):
                sp.dma_start(row(C.facts_tab[f, 0:STEPS]).rearrange("a (c p) -> (a c) p", p=P),
                             facts_t[f * CHUNKS:(f + 1) * CHUNKS, :]).then_inc(facts_stored, 16)
            sp.wait_ge(facts_stored, 16 * 5)
            for f in range(4):
                sp.dma_start(now[:, f, :], C.facts_tab[f, 0:STEPS].rearrange("(b j) -> b j", j=BATCH)
                             ).then_inc(facts_back, 16)
            for f in range(3):
                sp.dma_start(nxt[:, f, :], C.facts_tab[f, 1:STEPS + 1].rearrange("(b j) -> b j", j=BATCH)
                             ).then_inc(facts_back, 16)
            sp.wait_ge(rows_ready, 1)
            sp.dma_start(C.row_tab.rearrange("(c p) w -> p c w", p=P),
                         rows[:, :, :, :].rearrange("p c f e -> p c (f e)")).then_inc(rows_stored, 16)
            sp.dma_start(C.mask_tab.rearrange("(c p) w -> p c w", p=P),
                         masks[:, :, :, :].rearrange("p c f e -> p c (f e)")).then_inc(rows_stored, 16)
            bpc = P // BATCH
            for c in range(CHUNKS):
                sp.wait_ge(copied, 3 * (c + 1))
                sp.wait_ge(gated, LAYERS * (c + 1))
                sp.wait_ge(selected, c + 1)
                done = cols_stored[c % 2]
                bs = slice(c * bpc, (c + 1) * bpc)
                sp.dma_start(C.index_tab[bs, :, :].rearrange("b p j -> p b j"),
                             col_i[:, c % 2, :].rearrange("p (b j) -> p b j", j=BATCH)).then_inc(done, 16)
                sp.dma_start(C.dst_tab[bs, :, :].rearrange("b p j -> p b j"),
                             col_f[:, c % 2, :].rearrange("p (b j) -> p b j", j=BATCH)).then_inc(done, 16)
                for f in range(3):
                    sp.dma_start(C.gate_tab[bs, :, f, :].rearrange("b p j -> p b j"),
                                 gf[:, c % 2, f, :].rearrange("p (b j) -> p b j", j=BATCH)).then_inc(done, 16)
            sp.wait_ge(last_ready, 1)
            sp.dma_start(C.carry_tab.rearrange("b f j -> b (f j)"),
                         ag[:, :, :].rearrange("b f j -> b (f j)")).then_inc(rows_stored, 16)
            sp.dma_start(C.block_tab, blk_i[:, :]).then_inc(rows_stored, 16)
            sp.wait_ge(rows_stored, 64)
            for n in range(2):
                sp.wait_ge(cols_stored[n], 16 * 5 * ((CHUNKS + 1 - n) // 2))

        @block.tensor
        def _(pe):
            pe.wait_ge(summed, 1)
            pe.matmul(count_ps[:, :], C.ones[:, :], below[:, :, :].rearrange("p f b -> p (f b)"),
                      start=True, stop=True).then_inc(turned, 1)
            pe.wait_ge(facts_ready, 2)
            pe.transpose(facts_ps[:, :], facts[:, :, :].rearrange("p f c -> p (f c)"), C.ident[:, :]
                         ).then_inc(facts_turned, 1)
            pe.wait_ge(rows_ready, 1)
            for c in range(CHUNKS):
                if c >= 2:
                    pe.wait_ge(copied, 3 * (c - 1))
                pe.transpose(turned_ps[c % 2][:, 0, :], src_f[:, c, :], C.ident[:, :])
                pe.transpose(turned_ps[c % 2][:, 1, :], dst_b[:, c, :], C.ident[:, :])
                pe.transpose(turned_ps[c % 2][:, 2, :], steps[:, c, 3, :].bitcast(F32), C.ident[:, :]
                             ).then_inc(turned, 1)
                pe.wait_ge(copied, 3 * (c + 1))
                if c >= 2:
                    pe.wait_ge(selected, c - 1)
                pe.matmul(first_ps[c % 2][:, :], C.ones[0:1, :], col_f[0:1, c % 2, :],
                          start=True, stop=True).then_inc(first_done, 1)

        @block.scalar
        def _(act):
            act.wait_ge(gate_in, 16 * 2 * LAYERS)
            for c in range(CHUNKS):
                act.wait_ge(copied, 3 * (c + 1))
                if c >= 2:
                    act.wait_ge(cols_stored[c % 2], 16 * 5 * (c // 2))
                for i in range(LAYERS):
                    act.activation(gf[:, c % 2, i, :], wcol[:, c % 2, :], ACT.Sigmoid,
                                   scale=gwb[:, 2 * i:2 * i + 1], bias=gwb[:, 2 * i + 1:2 * i + 2]
                                   ).then_inc(gated, 1)

        @block.vector
        def _(dve):
            chain = [0]

            def done(ins):
                chain[0] += 1
                ins.then_inc(link, 1)
                dve.wait_ge(link, chain[0])

            dve.wait_ge(counted, 2)
            dve.wait_ge(loaded, 16 * 3 * len(fields))
            dve.tensor_copy(start[:, :], start_i[:, :])
            dve.tensor_copy(step_f[:, :], step_i[:, :])
            dve.tensor_copy(ends_f[:, 0, :], edges[:, :, 1, 0])
            done(dve.tensor_copy(ends_f[:, 1, :], edges[:, :, 1, P - 1]))
            for f, (at, e) in enumerate(((0, 1), (1, 0))):
                for c in range(CHUNKS):
                    edge = ends_f[:, e, c:c + 1]
                    if c == 0:
                        done(dve.tensor_scalar(below[:, f, :], start[:, at:at + BLOCKS], edge, None, ALU.is_gt))
                    else:
                        done(dve.scalar_tensor_tensor(out=below[:, f, :], in0=start[:, at:at + BLOCKS],
                                                      scalar=edge, in1=below[:, f, :], op0=ALU.is_gt, op1=ALU.add))
            dve.sem_inc(summed, 1)
            dve.wait_ge(turned, 1)
            done(dve.tensor_copy(count[:, :, :].rearrange("p f b -> p (f b)"), count_ps[:, :]))
            done(dve.tensor_tensor(npair[:, :], count[:, 1, :], count[:, 0, :], ALU.subtract))
            done(dve.tensor_tensor_scan(pair_end[:, :], C.ones[:, 0:BLOCKS], npair[:, :], 0.0, ALU.mult, ALU.add))
            done(dve.tensor_tensor(shift[:, :], count[:, 0, :], pair_end[:, :], ALU.subtract))
            done(dve.tensor_tensor(shift[:, :], shift[:, :], npair[:, :], ALU.add))
            grid = [P, CHUNKS, BLOCKS]
            done(dve.tensor_tensor(table[:, :, :], pair_end[:, :].unsqueeze(1).to_broadcast(grid),
                                   step_f[:, :].unsqueeze(2).to_broadcast(grid), ALU.is_le))
            done(dve.tensor_reduce(facts[:, 3, :], table[:, :, :], AX.X, ALU.add))
            done(dve.tensor_scalar(base[:, :], facts[:, 3, :], float(P), None, ALU.mult))
            done(dve.tensor_tensor(table[:, :, :], start[:, 0:BLOCKS].unsqueeze(1).to_broadcast(grid),
                                   base[:, :].unsqueeze(2).to_broadcast(grid), ALU.is_equal))
            done(dve.tensor_tensor(table[:, :, :], table[:, :, :],
                                   shift[:, :].unsqueeze(1).to_broadcast(grid), ALU.mult))
            done(dve.tensor_reduce(facts[:, 0, :], table[:, :, :], AX.X, ALU.add))
            done(dve.tensor_tensor(facts[:, 0, :], facts[:, 0, :], step_f[:, :], ALU.add))
            done(dve.tensor_scalar(facts[:, 0, :], facts[:, 0, :], float(EDGE_TILES - 1), None, ALU.min))
            dve.tensor_copy(tile_i[:, :], facts[:, 0, :]).then_inc(facts_ready, 1)
            dve.wait_ge(gathered, 16 * CHUNKS)
            dve.tensor_copy(src_f[:, :, :], steps[:, :, 0, :])
            done(dve.tensor_copy(dst_g[:, :, :], steps[:, :, 1, :]))
            dve.tensor_copy(facts[:, 1, :], dst_g[:, :, 0])
            dve.tensor_copy(facts[:, 2, :], dst_g[:, :, P - 1]).then_inc(facts_ready, 1)
            done(dve.tensor_tensor(dst_b[:, :, :], dst_g[:, :, :],
                                   base[:, :].unsqueeze(2).to_broadcast([P, CHUNKS, P]), ALU.subtract))
            dve.tensor_copy(rows[:, :, 0, :], steps[:, :, 2, :])
            dve.tensor_copy(rows[:, :, 1, :], dst_b[:, :, :])
            dve.memset(masks[:, :, 0, 0:1], 0.0)
            dve.memset(masks[:, :, 1, P - 1:P], 0.0)
            dve.tensor_tensor(masks[:, :, 0, 1:P], dst_g[:, :, 1:P], dst_g[:, :, 0:P - 1], ALU.not_equal)
            dve.tensor_tensor(masks[:, :, 1, 0:P - 1], dst_g[:, :, 0:P - 1], dst_g[:, :, 1:P], ALU.not_equal)
            done(dve.tensor_tensor(masks[:, :, 2, :], dst_g[:, :, :],
                                   dst_g[:, :, 0:1].to_broadcast([P, CHUNKS, P]), ALU.not_equal))
            flat = masks[:, :, :, :].rearrange("p c f e -> p (c f e)")
            dve.tensor_scalar(flat, flat, NEG, None, ALU.mult).then_inc(rows_ready, 1)
            dve.wait_ge(facts_turned, 1)
            dve.tensor_copy(facts_t[:, :], facts_ps[:, :]).then_inc(facts_copied, 1)
            for c in range(CHUNKS):
                dve.wait_ge(turned, c + 2)
                if c >= 2:
                    dve.wait_ge(cols_stored[c % 2], 16 * 5 * (c // 2))
                    dve.wait_ge(gated, LAYERS * (c - 1))
                dve.tensor_copy(col_i[:, c % 2, :], turned_ps[c % 2][:, 0, :]).then_inc(copied, 1)
                dve.tensor_copy(col_f[:, c % 2, :], turned_ps[c % 2][:, 1, :]).then_inc(copied, 1)
                dve.tensor_copy(wcol[:, c % 2, :], turned_ps[c % 2][:, 2, :]).then_inc(copied, 1)
                dve.wait_ge(first_done, c + 1)
                dve.tensor_scalar(gf[:, c % 2, 2, :], first_ps[c % 2][:, :], C.iota_part[:, 0:1], None,
                                  ALU.is_equal).then_inc(selected, 1)
            dve.wait_ge(facts_back, 16 * 7)
            same, goes, one = flags[:, 0, :], flags[:, 1, :], flags[:, 2, :]
            dve.tensor_copy(blk_i[:, :], now[:, 3, :])
            dve.tensor_tensor(same, now[:, 0, :], nxt[:, 0, :], ALU.is_equal)
            dve.tensor_tensor(goes, now[:, 2, :], nxt[:, 1, :], ALU.is_equal)
            dve.tensor_tensor(one, now[:, 1, :], now[:, 2, :], ALU.is_equal)
            done(dve.tensor_tensor(flags[:, 3, :], now[:, 0, :], nxt[:, 0, :], ALU.not_equal))
            done(dve.tensor_tensor(goes, goes, flags[:, 3, :], ALU.mult))
            done(dve.tensor_tensor(one, one, goes, ALU.mult))
            done(dve.tensor_tensor(same, same, one, ALU.max))
            dve.tensor_scalar(ag[:, 0, :], same, -NEG, NEG, ALU.mult, ALU.add)
            dve.tensor_scalar(ag[:, 1, :], goes, -NEG, NEG, ALU.mult, ALU.add).then_inc(last_ready, 1)


def load_node_rows(sp, acc, x, sem):
    sp.dma_start(acc[:, 0:FULL_BLOCKS, 0:D], x[0:FULL_BLOCKS * P, :].rearrange("(i p) d -> p i d", p=P)
                 ).then_inc(sem, 16)
    sp.dma_start(acc[0:TAIL_NODES, FULL_BLOCKS, 0:D], x[FULL_BLOCKS * P:NODES, :]).then_inc(sem, 16)


def layer_norm(nc, C, tag, x, skip):
    with ExitStack() as st:
        K = Kit(nc, st, tag)
        stats = K.sb("stats", [P, BLOCKS, 6])
        mv = K.sb("mv", [P, BLOCKS, 2])
        dev = K.sb("dev", [P, BLOCKS])
        rstd = K.sb("rstd", [P, BLOCKS])
        other = K.sb("other", [P, BLOCKS if skip else 1, D])
        loaded = K.sem("loaded")
        ready = K.sem("ready")
        added = K.sem("added")
        counted = K.sem("counted")
        aggregated = K.sem("aggregated")
        shifted = K.sem("shifted")
        rooted = K.sem("rooted")
        inverted = K.sem("inverted")
        scaled = K.sem("scaled")
        clipped = K.sem("clipped")
        stored = K.sem("stored")
        acc = C.acc
        block = K.block()

        @block.gpsimd
        def _(pool):
            if skip:
                pool.memset(other[:, FULL_BLOCKS, :], 0.0).then_inc(ready, 1)
            else:
                pool.memset(acc[:, FULL_BLOCKS:BLOCKS + 1, :], 0.0).then_inc(ready, 1)

        @block.sync
        def _(sp):
            sp.wait_ge(ready, 1)
            load_node_rows(sp, other if skip else acc, x, loaded)
            if skip:
                sp.wait_ge(added, BLOCKS)
                sp.dma_start(C.skip_tab.rearrange("(i p) d -> p i d", p=P), other[:, :, :]).then_inc(stored, 16)
                sp.wait_ge(clipped, BLOCKS)
                sp.dma_start(C.h_tab.rearrange("(i p) d -> p i d", p=P), acc[:, 0:BLOCKS, 0:D]).then_inc(stored, 16)
                sp.wait_ge(stored, 32)

        @block.vector
        def _(dve):
            dve.wait_ge(loaded, 32)
            tgt = other if skip else acc
            with dve.Fori(0, BLOCKS, 1) as i:
                if skip:
                    dve.tensor_tensor(other[:, bass.ds(i, 1), :], other[:, bass.ds(i, 1), :],
                                      acc[:, bass.ds(i, 1), 0:D], ALU.add).then_inc(added, 1)
                    dve.wait_ge(added, i + 1)
                dve.bn_stats(stats[:, bass.ds(i, 1), :].rearrange("p a s -> p (a s)"),
                             tgt[:, bass.ds(i, 1), 0:D].rearrange("p a d -> p (a d)")).then_inc(counted, 1)
            dve.wait_ge(counted, BLOCKS)
            for i in range(BLOCKS):
                dve.bn_aggr(mv[:, i, :], stats[:, i, :]).then_inc(aggregated, 1)
            dve.wait_ge(aggregated, BLOCKS)
            dve.tensor_scalar(dev[:, :], mv[:, :, 1], EPS, None, ALU.add).then_inc(shifted, 1)
            dve.wait_ge(rooted, 1)
            dve.reciprocal(rstd[:, :], dev[:, :]).then_inc(inverted, 1)
            dve.wait_ge(inverted, 1)
            with dve.Fori(0, BLOCKS, 1) as i:
                dve.tensor_scalar(acc[:, bass.ds(i, 1), 0:D], tgt[:, bass.ds(i, 1), 0:D],
                                  mv[:, bass.ds(i, 1), 0:1].rearrange("p a b -> p (a b)"),
                                  rstd[:, bass.ds(i, 1)], ALU.subtract, ALU.mult).then_inc(scaled, 1)

        @block.scalar
        def _(act):
            act.wait_ge(shifted, 1)
            act.activation(dev[:, :], dev[:, :], ACT.Sqrt).then_inc(rooted, 1)
            with act.Fori(0, BLOCKS, 1) as i:
                act.wait_ge(scaled, i + 1)
                act.activation(acc[:, bass.ds(i, 1), 0:D], acc[:, bass.ds(i, 1), 0:D], ACT.Relu
                               ).then_inc(clipped, 1)


def split3(dve, scratch, src, hi, mid, lo, done):
    done(dve.tensor_copy(hi, src))
    done(dve.tensor_tensor(scratch, src, hi, ALU.subtract))
    done(dve.tensor_copy(mid, scratch))
    done(dve.tensor_tensor(lo, scratch, mid, ALU.subtract))


def relation_tables(nc, C, layer, rel_emb, a1w, a1b, a2w, a2b):
    with ExitStack() as st:
        K = Kit(nc, st, f"r{layer}_")
        rel = K.sb("rel", [P, 2, D])
        rel_t = K.sb("rel_t", [P, 2, P])
        w = K.sb("w", [P, D])
        b = K.sb("b", [P, D])
        tab = K.sb("tab", [P, 2, D])
        scratch = K.sb("scratch", [P, 2, D])
        t_ps = K.ps("t_ps", [P, 2, P])
        r_ps = K.ps("r_ps", [P, 2, D])
        cleared = K.sem("cleared")
        loaded = K.sem("loaded")
        turned = K.sem("turned")
        copied = K.sem("copied")
        product = K.sem("product")
        link = K.sem("link")
        block = K.block()

        @block.gpsimd
        def _(pool):
            pool.memset(rel[:, :, :], 0.0).then_inc(cleared, 1)
            pool.memset(C.a2_slide[:, :], 0.0).then_inc(cleared, 1)

        @block.sync
        def _(sp):
            sp.wait_ge(cleared, 2)
            sp.dma_start(rel[:, 0, :], rel_emb[0:P, :]).then_inc(loaded, 16)
            sp.dma_start(rel[0:RELS - P, 1, :], rel_emb[P:RELS, :]).then_inc(loaded, 16)
            sp.dma_start(w[:, :], a1w[layer, D:2 * D, :]).then_inc(loaded, 16)
            sp.dma_start(b[:, :], over_partitions(row(a1b[layer, :]))).then_inc(loaded, 16)
            sp.dma_start(C.a2_slide[:, BATCH - 1:BATCH], a2w[layer, :].rearrange("(d a) -> d a", a=1)
                         ).then_inc(loaded, 16)
            sp.dma_start(C.a2_bias[:, :], over_partitions(row(a2b[layer:layer + 1]))).then_inc(loaded, 16)
            sp.wait_ge(loaded, 96)

        @block.tensor
        def _(pe):
            pe.wait_ge(loaded, 96)
            for c in range(2):
                pe.transpose(t_ps[:, c, :], rel[:, c, :], C.ident[:, :]).then_inc(turned, 1)
            pe.wait_ge(copied, 1)
            for c in range(2):
                pe.matmul(r_ps[:, c, :], rel_t[:, c, :], w[:, :], start=True, stop=True).then_inc(product, 1)

        @block.vector
        def _(dve):
            chain = [0]

            def done(ins):
                chain[0] += 1
                ins.then_inc(link, 1)
                dve.wait_ge(link, chain[0])

            dve.wait_ge(turned, 2)
            dve.tensor_copy(rel_t[:, :, :], t_ps[:, :, :]).then_inc(copied, 1)
            dve.wait_ge(loaded, 96)
            split3(dve, scratch[:, :, :], rel[:, :, :],
                   *(C.gate_rel[:, :, s, :] for s in range(3)), done)
            dve.wait_ge(product, 2)
            done(dve.tensor_tensor(tab[:, :, :], r_ps[:, :, :],
                                   b[:, :].unsqueeze(1).to_broadcast([P, 2, D]), ALU.add))
            split3(dve, scratch[:, :, :], tab[:, :, :],
                   *(C.rel_tab[:, :, s, :] for s in range(3)), done)


def node_tables(nc, C, layer, a1w, wv, bv, w0, b0):
    with ExitStack() as st:
        K = Kit(nc, st, f"n{layer}_")
        w = K.sb("w", [P, 4, D])
        bias = K.sb("bias", [P, 4, D])
        x_now = K.sb("x_now", [P, 2, D])
        xt = K.sb("xt", [P, 2, P])
        out = K.sb("out", [P, 2, 4, D])
        rest = K.sb("rest", [P, 1, D])
        xt_ps = [K.ps(f"xt_ps{i}", [P, P]) for i in range(2)]
        out_ps = [K.ps(f"out_ps{i}", [P, 4 * D]) for i in range(2)]
        cleared = K.sem("cleared")
        loaded = K.sem("loaded")
        staged = K.sem("staged")
        turned = K.sem("turned")
        copied = K.sem("copied")
        projected = K.sem("projected")
        biased = K.sem("biased")
        split = K.sem("split")
        split_step = K.sem("split_step")
        passed = K.sem("passed")
        stored = [K.sem(f"stored{i}") for i in range(2)]
        block = K.block()
        own = C.own_tab.rearrange("(i p) d -> i p d", p=P)
        sources = C.source_tab.rearrange("(i p) d -> i p d", p=P)

        @block.sync
        def _(sp):
            sp.wait_ge(cleared, 1)
            sp.dma_start(w[:, 0, :], a1w[layer, 0:D, :]).then_inc(loaded, 16)
            sp.dma_start(w[:, 1, :], wv[layer, :, :]).then_inc(loaded, 16)
            sp.dma_start(w[:, 2, :], a1w[layer, 2 * D:3 * D, :]).then_inc(loaded, 16)
            sp.dma_start(w[:, 3, :], w0[layer, :, :]).then_inc(loaded, 16)
            sp.dma_start(bias[:, 1, :], over_partitions(row(bv[layer, :]))).then_inc(loaded, 16)
            sp.dma_start(bias[:, 3, :], over_partitions(row(b0[layer, :]))).then_inc(loaded, 16)
            with sp.Fori(0, BLOCKS // 2) as pair:
                i = pair * 2
                for n in range(2):
                    sp.wait_ge(biased, i + (n + 3))
                    sp.dma_start(sources[bass.ds(i + n, 1), :, :].rearrange("a p d -> (a p) d"),
                                 out[:, n, 0:2, :].rearrange("p f d -> p (f d)")).then_inc(stored[n], 16)
                    sp.dma_start(own[bass.ds(i + n, 1), :, :].rearrange("a p d -> (a p) d"),
                                 out[:, n, 3, :]).then_inc(stored[n], 16)
            for n in range(2):
                sp.wait_ge(stored[n], 32 * (BLOCKS // 2))

        @block.gpsimd
        def _(pool):
            pool.sem_inc(split, 2)
            pool.memset(bias[:, :, :], 0.0).then_inc(cleared, 1)
            pool.memset(C.node_q[:, BLOCKS, :, :], 0.0)
            with pool.Fori(0, BLOCKS // 2) as pair:
                i = pair * 2
                for n in range(2):
                    wait_alone(pool, biased, i + (n + 3), passed)
                    q = out[:, n, 2:3, :]
                    hi, mid, lo = (C.node_q[:, bass.ds(i + n, 1), s, :] for s in range(3))
                    pool.tensor_copy(hi, q).then_inc(split_step, 1)
                    wait_alone(pool, split_step, i * 3 + (3 * n + 1), passed)
                    pool.tensor_tensor(rest[:, :, :], q, hi, ALU.subtract).then_inc(split_step, 1)
                    wait_alone(pool, split_step, i * 3 + (3 * n + 2), passed)
                    pool.tensor_copy(mid, rest[:, :, :]).then_inc(split_step, 1)
                    wait_alone(pool, split_step, i * 3 + (3 * n + 3), passed)
                    pool.tensor_tensor(lo, rest[:, :, :], mid, ALU.subtract).then_inc(split, 1)

        @block.tensor
        def _(pe):
            pe.sem_inc(projected, 2)
            pe.wait_ge(loaded, 96)
            pe.wait_ge(staged, 1)
            pe.transpose(xt_ps[0][:, :], x_now[:, 0, :], C.ident[:, :]).then_inc(turned, 1)
            with pe.Fori(0, BLOCKS // 2) as pair:
                i = pair * 2
                for n in range(2):
                    pe.wait_ge(staged, i + (n + 2))
                    pe.transpose(xt_ps[1 - n][:, :], x_now[:, 1 - n, :], C.ident[:, :]).then_inc(turned, 1)
                    pe.wait_ge(copied, i + (n + 1))
                    pe.wait_ge(biased, i + (n + 1))
                    pe.matmul(out_ps[n][:, :], xt[:, n, :], w[:, :, :].rearrange("p f d -> p (f d)"),
                              start=True, stop=True).then_inc(projected, 1)

        @block.scalar
        def _(act):
            act.activation(x_now[:, 0, :], C.acc[:, 0, 0:D], ACT.Copy).then_inc(staged, 1)
            with act.Fori(0, BLOCKS // 2) as pair:
                i = pair * 2
                for n in range(2):
                    act.activation(x_now[:, 1 - n, :], C.acc[:, bass.ds(i + (n + 1), 1), 0:D]
                                   .rearrange("p a d -> p (a d)"), ACT.Copy).then_inc(staged, 1)
                    act.wait_ge(turned, i + (n + 1))
                    act.wait_ge(projected, i + (n + 1))
                    act.activation(xt[:, n, :], xt_ps[n][:, :], ACT.Copy).then_inc(copied, 1)

        @block.vector
        def _(dve):
            dve.sem_inc(biased, 2)
            dve.wait_ge(loaded, 96)

            def emit(i):
                for n in range(2):
                    dve.wait_ge(projected, i + (n + 3))
                    waits(dve, stored[n], i * 16)
                    dve.wait_ge(split, i + (n + 1))
                    dve.tensor_tensor(out[:, n, :, :], out_ps[n][:, :].rearrange("p (f d) -> p f d", d=D),
                                      bias[:, :, :], ALU.add).then_inc(biased, 1)

            emit(0)
            with dve.Fori(1, BLOCKS // 2) as pair:
                emit(pair * 2)


def fetch_blocks(engine, tab, at):
    _, vals = engine.bass.values_load_multi_w_load_instructions(
        tab[0:1, at:at + GROUP], engines=[engine.engine], min_val=0, max_val=BLOCKS,
        skip_runtime_bounds_check_because="plan_steps counts at most BLOCKS pair ends")
    return vals


def waits(engine, sem, value):
    if not isinstance(value, int) or value > 0:
        engine.wait_ge(sem, value)


def wait_alone(engine, sem, value, passed):
    if isinstance(value, int):
        waits(engine, sem, value)
        return
    engine.wait_ge(sem, value)
    engine.sem_inc(passed, 1)


def run_batches(engine, emit):
    for k0 in (0, 2):
        for par in range(2):
            k = k0 + par
            emit(k0, par, True, k >= 1, k >= 2)
    with engine.Fori(2, NBATCH // 2) as pair:
        for par in range(2):
            emit(pair * 2, par, True, True, True)
    emit(NBATCH, 0, False, True, True)
    emit(NBATCH, 1, False, False, True)


def attention(nc, C, layer):
    with ExitStack() as st:
        K = Kit(nc, st, f"a{layer}_")
        index = K.sb("index", [P, 2, BATCH], I32)
        blk_q = K.sb("blk_q", [1, 2, BATCH], I32)
        blk_acc = K.sb("blk_acc", [1, 2, BATCH], I32)
        gate = K.sb("gate", [P, 2, 2, BATCH])
        mask = K.sb("mask", [BATCH, 2, 3, P])
        carry_tab = K.sb("carry_tab", [1, 2, 2, BATCH])
        dstc = K.sb("dstc", [P, 2, BATCH])
        row_sb = K.sb("row_sb", [P, 2, GROUP, 2, P], BF16)
        got = K.sb("got", [P, 2, GROUP, 2, D])
        hot = K.sb("hot", [P, 2, 3, GROUP, P], BF16)
        lrelu = K.sb("lrelu", [P, 2, GROUP, P])
        sel = K.sb("sel", [P, 2, GROUP, P])
        msg = K.sb("msg", [P, 2, BATCH, AW])
        logit = K.sb("logit", [BATCH, P])
        before = K.sb("before", [BATCH, P])
        after = K.sb("after", [BATCH, P])
        top = K.sb("top", [BATCH, P])
        diff = K.sb("diff", [BATCH, P])
        prob = K.sb("prob", [BATCH, P])
        last = K.sb("last", [1, BATCH])
        carried = K.sb("carried", [1, 2, BATCH + 1])
        carried_c = K.sb("carried_c", [BATCH, 1])
        delta = K.sb("delta", [BATCH, 1])
        diag = K.sb("diag", [BATCH, BATCH])
        wgt = K.sb("wgt", [P, 2, 2, BATCH])
        shrink_log = K.sb("shrink_log", [P, BATCH])
        shrink = K.sb("shrink", [P, 2, BATCH])
        z_ps = [K.ps(f"z_ps{i}", [P, GROUP * P]) for i in range(2)]
        rel_ps = [K.ps(f"rel_ps{i}", [P, GROUP * P]) for i in range(2)]
        logit_ps = K.ps("logit_ps", [BATCH, P])
        small_ps = K.ps("small_ps", [P, 4, BATCH])
        sum_ps = [K.ps(f"sum_ps{i}", [P, 2, 2 * P]) for i in range(2)]

        index_in = [K.sem(f"index_in{i}") for i in range(2)]
        norm_in = [K.sem(f"norm_in{i}") for i in range(2)]
        sums_in = [K.sem(f"sums_in{i}") for i in range(2)]
        rows_in = [K.sem(f"rows_in{i}") for i in range(2)]
        got_in = [K.gather_sem(C.root, f"got_in{i}") for i in range(2 * GROUP)]
        cleared = K.sem("cleared")
        passed = K.sem("passed")
        hot_ready = K.sem("hot_ready")
        z_ready = K.sem("z_ready")
        rel_ready = K.sem("rel_ready")
        z_scaled = K.sem("z_scaled")
        lrelu_ready = K.sem("lrelu_ready")
        logit_ready = K.sem("logit_ready")
        msg_ready = K.sem("msg_ready")
        sel_ready = K.sem("sel_ready")
        msg_scaled = K.sem("msg_scaled")
        pair_summed = K.sem("pair_summed")
        step_added = K.sem("step_added")
        norm_step = K.sem("norm_step")
        norm_turned = K.sem("norm_turned")
        prob_ready = K.sem("prob_ready")
        shrink_ready = K.sem("shrink_ready")
        NS = 13
        block = K.block()

        @block.sync
        def _(sp):
            def emit(k0, par, logits, norm, sums):
                k = k0 + par
                if logits:
                    waits(sp, msg_ready, k * GPB - GPB)
                    sp.dma_start(index[:, par, :], C.index_tab[bass.ds(k, 1), :, :]
                                 .rearrange("b p j -> (b p) j")).then_inc(index_in[par], 16)
                    sp.dma_start(blk_q[0:1, par, :], C.block_tab[bass.ds(k, 1), :]).then_inc(index_in[par], 16)
                if norm:
                    q = 1 - par
                    waits(sp, norm_step, k * NS - 2 * NS)
                    g = C.gate_tab[bass.ds(k - 1, 1), :, :, :].rearrange("b p f j -> (b p) f j")
                    sp.dma_start(gate[:, q, 0, :], g[:, layer, :]).then_inc(norm_in[q], 16)
                    sp.dma_start(gate[:, q, 1, :], g[:, 2, :]).then_inc(norm_in[q], 16)
                    sp.dma_start(mask[:, q, :, :].rearrange("s f e -> s (f e)"),
                                 C.mask_tab[bass.ds(k * BATCH - BATCH, BATCH), :]).then_inc(norm_in[q], 16)
                    sp.dma_start(carry_tab[:, q, :, :].rearrange("a f j -> a (f j)"),
                                 C.carry_tab[bass.ds(k - 1, 1), :, :].rearrange("b f j -> b (f j)")
                                 ).then_inc(norm_in[q], 16)
                if sums:
                    waits(sp, step_added, k * BATCH - 3 * BATCH)
                    sp.dma_start(dstc[:, par, :], C.dst_tab[bass.ds(k - 2, 1), :, :]
                                 .rearrange("b p j -> (b p) j")).then_inc(sums_in[par], 16)
                    sp.dma_start(blk_acc[0:1, par, :], C.block_tab[bass.ds(k - 2, 1), :]).then_inc(sums_in[par], 16)
                if logits:
                    for g in range(GPB):
                        waits(sp, hot_ready, k * GPB + (g - 1))
                        sp.dma_start(row_sb[:, g % 2, :, :, :].rearrange("p s f e -> p (s f e)"),
                                     over_partitions(C.row_tab[bass.ds(k * BATCH + g * GROUP, GROUP), :]
                                                     .rearrange("(a s) w -> a (s w)", a=1))
                                     ).then_inc(rows_in[g % 2], 16)
            run_batches(sp, emit)

        @block.gpsimd
        def _(pool):
            pool.memset(carried[:, :, :], NEG).then_inc(cleared, 1)

            def emit(k0, par, logits, norm, sums):
                if not logits:
                    return
                k = k0 + par
                pool.wait_ge(index_in[par], k0 * 16 + 32)
                for g in range(GPB):
                    wait_alone(pool, msg_ready, k * GPB + (g - 1), passed)
                    for j in range(GROUP):
                        n = g % 2 * GROUP + j
                        pool.indirect_dma_start(
                            got[:, g % 2, j, :, :].rearrange("p f d -> p (f d)"), None, C.source_tab,
                            bass.IndirectOffsetOnAxis(ap=index[:, par, g * GROUP + j:g * GROUP + j + 1], axis=0)
                        ).then_inc(got_in[n], 16)
            run_batches(pool, emit)

        @block.tensor
        def _(pe):
            def emit(k0, par, logits, norm, sums):
                k = k0 + par
                q = 1 - par
                if logits:
                    wait_alone(pe, index_in[par], k0 * 16 + 32, passed)
                for g in range(GPB):
                    grp = k * GPB + g
                    if logits:
                        blk = fetch_blocks(pe, blk_q[:, par, :], g * GROUP)
                        pe.wait_ge(hot_ready, grp + 1)
                        waits(pe, lrelu_ready, grp - 1)
                        for c in range(2):
                            for s in range(3):
                                pe.matmul(z_ps[g % 2][:, :], C.rel_tab[:, c, s, :],
                                          hot[:, g % 2, c, :, :].rearrange("p j e -> p (j e)"),
                                          start=(c == 0 and s == 0), stop=False, skip_group_check=True)
                        for j in range(GROUP):
                            z = z_ps[g % 2][:, j * P:(j + 1) * P]
                            for s in range(3):
                                pe.matmul(z, C.node_q[:, bass.ds(blk[j], 1), s, :].rearrange("p a d -> p (a d)"),
                                          hot[:, g % 2, 2, j, :], start=False, stop=False, skip_group_check=True)
                            pe.wait_ge(got_in[g % 2 * GROUP + j], k0 * (16 * GPB // 2)
                                       + (par * GPB // 2 + g // 2 + 1) * 16)
                            last_mm = pe.matmul(z, got[:, g % 2, j, 0, :], C.ident[:, :], start=False,
                                                stop=True, skip_group_check=True)
                        last_mm.then_inc(z_ready, 1)
                    if norm and g == 1:
                        wait_alone(pe, norm_step, k * NS + (2 - NS), passed)
                        pe.matmul(small_ps[0:1, 0, :], before[:, P - 1:P], C.ident[0:BATCH, 0:BATCH],
                                  start=True, stop=True).then_inc(norm_turned, 1)
                    if norm and g == 2:
                        wait_alone(pe, norm_step, k * NS + (6 - NS), passed)
                        pe.matmul(small_ps[0:BATCH, 1, 0:1], carried[0:1, q, 0:BATCH], C.ones[0:1, 0:1],
                                  start=True, stop=True).then_inc(norm_turned, 1)
                    if norm and g == 3:
                        pe.wait_ge(norm_step, k * NS + (10 - NS))
                        wait_alone(pe, prob_ready, k, passed)
                        pe.matmul(small_ps[:, 2, :], prob[:, :], C.ident[0:BATCH, 0:BATCH], start=True, stop=True)
                        pe.matmul(small_ps[:, 3, :], C.ones[0:BATCH, :], diag[:, :], start=True, stop=True
                                  ).then_inc(norm_turned, 1)
                    if sums:
                        pe.wait_ge(sel_ready, grp + (1 - 2 * GPB))
                        pe.wait_ge(msg_scaled, grp + (1 - 2 * GPB))
                        for j in range(GROUP):
                            if j % 2 == 0:
                                waits(pe, step_added, k * BATCH + (g * GROUP + j - 2 * BATCH - 2))
                            mm = pe.matmul(sum_ps[j // 2][:, j % 2, 0:AW], sel[:, g % 2, j, :],
                                           msg[:, par, g * GROUP + j, :], start=True, stop=True)
                            if j % 2 == 1:
                                mm.then_inc(pair_summed, 1)
                    if logits:
                        waits(pe, msg_ready, grp - 1)
                        for j in range(GROUP):
                            for c in range(2):
                                for s in range(3):
                                    mm = pe.matmul(rel_ps[g % 2][:, j * P:(j + 1) * P], hot[:, g % 2, c, j, :],
                                                   C.gate_rel[:, c, s, :], start=(c == 0 and s == 0),
                                                   stop=(c == 1 and s == 2))
                        mm.then_inc(rel_ready, 1)
                        pe.wait_ge(lrelu_ready, grp + 1)
                        if g == 0:
                            waits(pe, norm_step, (k - 1) * NS + 1 if norm else 0)
                        for j in range(GROUP):
                            n = g * GROUP + j
                            mm = pe.matmul(logit_ps[:, :], C.a2_slide[:, BATCH - 1 - n:2 * BATCH - 1 - n],
                                           lrelu[:, g % 2, j, :], start=(n == 0), stop=(n == BATCH - 1),
                                           skip_group_check=True)
                        mm.then_inc(logit_ready, 1)
            run_batches(pe, emit)

        @block.scalar
        def _(act):
            def emit(k0, par, logits, norm, sums):
                k = k0 + par
                q = 1 - par
                for g in range(GPB):
                    if sums:
                        if g == 0:
                            act.wait_ge(norm_step, k * NS - NS)
                        for j in range(GROUP):
                            n = g * GROUP + j
                            act.activation(msg[:, par, n, 0:D], msg[:, par, n, 0:D], ACT.Copy,
                                           scale=wgt[:, par, 0, n:n + 1])
                        act.activation(msg[:, par, g * GROUP:(g + 1) * GROUP, D],
                                       wgt[:, par, 1, g * GROUP:(g + 1) * GROUP], ACT.Copy).then_inc(msg_scaled, 1)
                    if logits:
                        act.wait_ge(z_ready, k * GPB + (g + 1))
                        waits(act, logit_ready, k * GPB + (g - 1))
                        act.activation(lrelu[:, g % 2, :, :].rearrange("p j e -> p (j e)"), z_ps[g % 2][:, :],
                                       ACT.Copy, scale=0.2).then_inc(z_scaled, 1)
                    if norm and g == 2:
                        act.wait_ge(norm_step, k * NS + (10 - NS))
                        act.activation(prob[:, :], diff[:, :], ACT.Exp).then_inc(prob_ready, 1)
                    if norm and g == 3:
                        act.wait_ge(norm_step, k * NS)
                        waits(act, step_added, k * BATCH - 2 * BATCH)
                        act.activation(shrink[:, q, :], shrink_log[:, :], ACT.Exp).then_inc(shrink_ready, 1)
            run_batches(act, emit)

        @block.vector
        def _(dve):
            dve.memset(C.acc[:, :, :], 0.0).then_inc(cleared, 1)
            dve.wait_ge(cleared, 2)

            def emit(k0, par, logits, norm, sums):
                k = k0 + par
                q = 1 - par

                def step(ins, n):
                    ins.then_inc(norm_step, 1)
                    dve.wait_ge(norm_step, k * NS + (n - NS))

                for g in range(GPB):
                    grp = k * GPB + g
                    if logits:
                        dve.wait_ge(rows_in[g % 2], k0 * (16 * GPB // 2) + (par * GPB // 2 + g // 2 + 1) * 16)
                        waits(dve, rel_ready, grp - 1)
                        types = row_sb[:, g % 2, :, 0, :]
                        nodes = row_sb[:, g % 2, :, 1, :]
                        dve.tensor_scalar(hot[:, g % 2, 0, :, :], types, C.iota_part[:, 0:1], None, ALU.is_equal)
                        dve.tensor_scalar(hot[:, g % 2, 1, :, :], types, C.iota_part[:, 1:2], None, ALU.is_equal)
                        dve.tensor_scalar(hot[:, g % 2, 2, :, :], nodes, C.iota_part[:, 0:1], None, ALU.is_equal
                                          ).then_inc(hot_ready, 1)
                    if sums:
                        if g == 0:
                            dve.wait_ge(sums_in[par], k0 * 16)
                        waits(dve, pair_summed, (k * BATCH + (g * GROUP - 2 * BATCH - GROUP)) // 2
                              if isinstance(k, int) else k * (BATCH // 2) + (g * GROUP - 2 * BATCH - GROUP) // 2)
                        dve.tensor_tensor(sel[:, g % 2, :, :], C.iota_free[:, :].unsqueeze(1).to_broadcast([P, GROUP, P]),
                                          dstc[:, par, g * GROUP:(g + 1) * GROUP].unsqueeze(2).to_broadcast([P, GROUP, P]),
                                          ALU.is_equal).then_inc(sel_ready, 1)
                    if norm and g == 0:
                        dve.wait_ge(norm_in[q], k0 * 32 + 64 * par)
                        dve.wait_ge(logit_ready, k * GPB)
                        step(dve.tensor_scalar(logit[:, :], logit_ps[:, :], C.a2_bias[0:BATCH, 0:1], None,
                                               ALU.add), 1)
                    if logits:
                        dve.wait_ge(z_scaled, grp + 1)
                        act_z = lrelu[:, g % 2, :, :].rearrange("p j e -> p (j e)")
                        dve.tensor_tensor(act_z, z_ps[g % 2][:, :], act_z, ALU.max).then_inc(lrelu_ready, 1)
                    if sums:
                        blk = fetch_blocks(dve, blk_acc[:, par, :], g * GROUP)
                        if g == 0:
                            dve.wait_ge(shrink_ready, k - 1)
                        for j in range(GROUP):
                            n = g * GROUP + j
                            if j % 2 == 0:
                                dve.wait_ge(pair_summed, k * (BATCH // 2) + (n - 2 * BATCH) // 2 + 1)
                            waits(dve, step_added, k * BATCH + (n - 2 * BATCH))
                            a = C.acc[:, bass.ds(blk[j], 1), :].rearrange("p a d -> p (a d)")
                            dve.scalar_tensor_tensor(out=a, in0=a, scalar=shrink[:, par, n:n + 1],
                                                     in1=sum_ps[j // 2][:, j % 2, 0:AW], op0=ALU.mult,
                                                     op1=ALU.add).then_inc(step_added, 1)
                    if logits:
                        dve.wait_ge(rel_ready, grp + 1)
                        dve.tensor_tensor(msg[:, par, g * GROUP:(g + 1) * GROUP, 0:D], got[:, g % 2, :, 1, :],
                                          rel_ps[g % 2][:, :].rearrange("p (j d) -> p j d", d=D), ALU.mult
                                          ).then_inc(msg_ready, 1)
                    if norm and g == 0:
                        step(dve.tensor_tensor_scan(before[:, :], mask[:, q, 0, :], logit[:, :], NEG,
                                                    ALU.add, ALU.max), 2)
                        step(dve.tensor_tensor_scan(after[:, ::-1], mask[:, q, 1, ::-1], logit[:, ::-1], NEG,
                                                    ALU.add, ALU.max), 3)
                        step(dve.tensor_tensor(top[:, :], before[:, :], after[:, :], ALU.max), 4)
                    if norm and g == 1:
                        dve.tensor_copy(carried[:, q, 0:1], carried[:, par, BATCH:BATCH + 1])
                        dve.wait_ge(norm_turned, k * 3 - 2)
                        step(dve.tensor_tensor(last[:, :], small_ps[0:1, 0, :], carry_tab[:, q, 1, :], ALU.add), 5)
                        step(dve.tensor_tensor_scan(carried[:, q, 1:BATCH + 1], carry_tab[:, q, 0, :], last[:, :],
                                                    carried[:, q, 0:1], ALU.add, ALU.max), 6)
                    if norm and g == 2:
                        dve.wait_ge(norm_turned, k * 3 - 1)
                        step(dve.tensor_copy(carried_c[:, :], small_ps[0:BATCH, 1, 0:1]), 7)
                        step(dve.scalar_tensor_tensor(out=top[:, :], in0=mask[:, q, 2, :], scalar=carried_c[:, 0:1],
                                                      in1=top[:, :], op0=ALU.add, op1=ALU.max), 8)
                        step(dve.tensor_tensor(delta[:, :], carried_c[:, :], top[:, 0:1], ALU.subtract), 9)
                        dve.tensor_scalar(diag[:, :], C.ident[0:BATCH, 0:BATCH], delta[:, 0:1], None, ALU.mult)
                        step(dve.tensor_tensor(diff[:, :], logit[:, :], top[:, :], ALU.subtract), 10)
                    if norm and g == 3:
                        dve.wait_ge(norm_turned, k * 3)
                        step(dve.tensor_copy(wgt[:, q, 1, :], small_ps[:, 2, :]), 11)
                        step(dve.tensor_tensor(wgt[:, q, 0, :], wgt[:, q, 1, :], gate[:, q, 0, :], ALU.mult), 12)
                        step(dve.tensor_tensor(shrink_log[:, :], small_ps[:, 3, :], gate[:, q, 1, :], ALU.mult), 13)
            run_batches(dve, emit)


def combine(nc, C, layer):
    with ExitStack() as st:
        K = Kit(nc, st, f"m{layer}_")
        inv = K.sb("inv", [P, BLOCKS])
        own = K.sb("own", [P, 2, 7, D])
        chunk = 7
        loaded = [K.sem(f"loaded{i}") for i in range(2)]
        inverted = K.sem("inverted")
        scaled = K.sem("scaled")
        added = K.sem("added")
        clipped = K.sem("clipped")
        block = K.block()
        rounds = BLOCKS // chunk
        own_v = C.own_tab.rearrange("(r i p) d -> r p i d", p=P, i=chunk)

        @block.sync
        def _(sp):
            for r in range(rounds):
                if r >= 2:
                    sp.wait_ge(added, r - 1)
                sp.dma_start(own[:, r % 2, :, :], own_v[r]).then_inc(loaded[r % 2], 16)

        @block.vector
        def _(dve):
            dve.tensor_scalar(inv[:, :], C.acc[:, 0:BLOCKS, D], 1e-16, None, ALU.add).then_inc(inverted, 1)
            dve.wait_ge(inverted, 1)
            dve.reciprocal(inv[:, :], inv[:, :]).then_inc(inverted, 1)
            dve.wait_ge(inverted, 2)
            for r in range(rounds):
                a = C.acc[:, r * chunk:(r + 1) * chunk, 0:D]
                dve.tensor_tensor(a, a, inv[:, r * chunk:(r + 1) * chunk].unsqueeze(2)
                                  .to_broadcast([P, chunk, D]), ALU.mult).then_inc(scaled, 1)
                dve.wait_ge(scaled, r + 1)
                dve.wait_ge(loaded[r % 2], 16 * (r // 2 + 1))
                dve.tensor_tensor(a, a, own[:, r % 2, :, :], ALU.add).then_inc(added, 1)

        @block.scalar
        def _(act):
            for r in range(rounds):
                act.wait_ge(added, r + 1)
                a = C.acc[:, r * chunk:(r + 1) * chunk, 0:D]
                act.activation(a, a, ACT.Relu).then_inc(clipped, 1)


def neighbour_sums(nc, C):
    with ExitStack() as st:
        K = Kit(nc, st, "s_")
        depth = 2
        index = K.sb("index", [P, 2, BATCH], I32)
        blk = K.sb("blk", [1, 2, BATCH], I32)
        dstc = K.sb("dstc", [P, 2, BATCH])
        got = K.sb("got", [P, GPB, GROUP, AW])
        sel = K.sb("sel", [P, 2, GROUP, P])
        sum_ps = [K.ps(f"sum_ps{i}", [P, 2, 2 * P]) for i in range(2)]
        tabs_in = [K.sem(f"tabs_in{i}") for i in range(2)]
        got_in = [K.gather_sem(C.root, f"got_in{i}") for i in range(BATCH)]
        cleared = K.sem("cleared")
        passed = K.sem("passed")
        sel_ready = K.sem("sel_ready")
        pair_summed = K.sem("pair_summed")
        step_added = K.sem("step_added")
        block = K.block()

        def batches(engine, emit):
            for par in range(2):
                emit(0, par)
            with engine.Fori(1, NBATCH // 2) as pair:
                for par in range(2):
                    emit(pair * 2, par)

        @block.sync
        def _(sp):
            def emit(k0, par):
                k = k0 + par
                waits(sp, step_added, k * BATCH - BATCH)
                sp.dma_start(index[:, par, :], C.index_tab[bass.ds(k, 1), :, :]
                             .rearrange("b p j -> (b p) j")).then_inc(tabs_in[par], 16)
                sp.dma_start(dstc[:, par, :], C.dst_tab[bass.ds(k, 1), :, :]
                             .rearrange("b p j -> (b p) j")).then_inc(tabs_in[par], 16)
                sp.dma_start(blk[0:1, par, :], C.block_tab[bass.ds(k, 1), :]).then_inc(tabs_in[par], 16)
            batches(sp, emit)

        @block.gpsimd
        def _(pool):
            pool.memset(got[:, :, :, D], 1.0).then_inc(cleared, 1)

            def emit(k0, par):
                k = k0 + par
                pool.wait_ge(tabs_in[par], k0 * 24 + 48)
                for g in range(GPB):
                    wait_alone(pool, pair_summed, k * (BATCH // 2) + (g * GROUP - BATCH + GROUP) // 2, passed)
                    for j in range(GROUP):
                        n = g * GROUP + j
                        pool.indirect_dma_start(
                            got[:, g, j, 0:D], None, C.h_tab,
                            bass.IndirectOffsetOnAxis(ap=index[:, par, n:n + 1], axis=0)).then_inc(got_in[n], 16)
            batches(pool, emit)

        @block.tensor
        def _(pe):
            pe.wait_ge(cleared, 2)

            def emit(k0, par):
                k = k0 + par
                for g in range(GPB):
                    pe.wait_ge(sel_ready, k * GPB + (g + 1))
                    for j in range(GROUP):
                        n = g * GROUP + j
                        pe.wait_ge(got_in[n], k * 16 + 16)
                        if j % 2 == 0:
                            waits(pe, step_added, k * BATCH + (n - 2))
                        mm = pe.matmul(sum_ps[j // 2][:, j % 2, 0:AW], sel[:, g % 2, j, :], got[:, g, j, :],
                                       start=True, stop=True)
                        if j % 2 == 1:
                            mm.then_inc(pair_summed, 1)
            batches(pe, emit)

        @block.vector
        def _(dve):
            dve.memset(C.acc[:, :, :], 0.0).then_inc(cleared, 1)
            dve.wait_ge(cleared, 2)

            def emit(k0, par):
                k = k0 + par
                dve.wait_ge(tabs_in[par], k0 * 24 + 48)
                for g in range(GPB):
                    waits(dve, pair_summed, k * (BATCH // 2) + (g * GROUP - GROUP) // 2)
                    dve.tensor_tensor(sel[:, g % 2, :, :], C.iota_free[:, :].unsqueeze(1).to_broadcast([P, GROUP, P]),
                                      dstc[:, par, g * GROUP:(g + 1) * GROUP].unsqueeze(2).to_broadcast([P, GROUP, P]),
                                      ALU.is_equal).then_inc(sel_ready, 1)
                    vals = fetch_blocks(dve, blk[:, par, :], g * GROUP)
                    for j in range(GROUP):
                        n = g * GROUP + j
                        if j % 2 == 0:
                            dve.wait_ge(pair_summed, k * (BATCH // 2) + (n // 2 + 1))
                        waits(dve, step_added, k * BATCH + n)
                        a = C.acc[:, bass.ds(vals[j], 1), :].rearrange("p a d -> p (a d)")
                        dve.tensor_tensor(a, a, sum_ps[j // 2][:, j % 2, 0:AW], ALU.add).then_inc(step_added, 1)
            batches(dve, emit)


def finish(nc, C, w1, b1, out):
    with ExitStack() as st:
        K = Kit(nc, st, "f_")
        w = K.sb("w", [P, D])
        bias = K.sb("bias", [P, D])
        inv = K.sb("inv", [P, BLOCKS])
        h = K.sb("h", [P, BLOCKS // 2, D])
        skip = K.sb("skip", [P, BLOCKS, D])
        x_now = K.sb("x_now", [P, 2, D])
        xt = K.sb("xt", [P, 2, P])
        lin = K.sb("lin", [P, 2, D])
        xt_ps = [K.ps(f"xt_ps{i}", [P, P]) for i in range(2)]
        out_ps = [K.ps(f"out_ps{i}", [P, D]) for i in range(2)]
        loaded = K.sem("loaded")
        h_in = K.sem("h_in")
        skip_in = K.sem("skip_in")
        inverted = K.sem("inverted")
        scaled = K.sem("scaled")
        added = K.sem("added")
        staged = K.sem("staged")
        turned = K.sem("turned")
        copied = K.sem("copied")
        projected = K.sem("projected")
        biased = K.sem("biased")
        finished = K.sem("finished")
        stored = K.sem("stored")
        half = BLOCKS // 2
        h_v = C.h_tab.rearrange("(r i p) d -> r p i d", p=P, i=half)
        block = K.block()

        @block.sync
        def _(sp):
            sp.dma_start(w[:, :], w1[:, :]).then_inc(loaded, 16)
            sp.dma_start(bias[:, :], over_partitions(row(b1))).then_inc(loaded, 16)
            sp.dma_start(h[:, :, :], h_v[0]).then_inc(h_in, 16)
            sp.dma_start(skip[:, :, :], C.skip_tab.rearrange("(i p) d -> p i d", p=P)).then_inc(skip_in, 16)
            sp.wait_ge(added, 1)
            sp.dma_start(h[:, :, :], h_v[1]).then_inc(h_in, 16)
            sp.wait_ge(finished, BLOCKS)
            sp.dma_start(out[0:FULL_BLOCKS * P, :].rearrange("(i p) d -> p i d", p=P), skip[:, 0:FULL_BLOCKS, :]
                         ).then_inc(stored, 16)
            sp.dma_start(out[FULL_BLOCKS * P:NODES, :], skip[0:TAIL_NODES, FULL_BLOCKS, :]).then_inc(stored, 16)
            sp.wait_ge(stored, 32)

        @block.tensor
        def _(pe):
            pe.wait_ge(loaded, 32)
            pe.wait_ge(staged, 1)
            pe.transpose(xt_ps[0][:, :], x_now[:, 0, :], C.ident[:, :]).then_inc(turned, 1)
            with pe.Fori(0, BLOCKS // 2) as pair:
                i = pair * 2
                for n in range(2):
                    pe.wait_ge(staged, i + (n + 2))
                    pe.transpose(xt_ps[1 - n][:, :], x_now[:, 1 - n, :], C.ident[:, :]).then_inc(turned, 1)
                    pe.wait_ge(copied, i + (n + 1))
                    pe.wait_ge(biased, i + (n + 1))
                    pe.matmul(out_ps[n][:, :], xt[:, n, :], w[:, :], start=True, stop=True).then_inc(projected, 1)

        @block.scalar
        def _(act):
            act.wait_ge(added, 2)
            act.activation(x_now[:, 0, :], C.acc[:, 0, 0:D], ACT.Copy).then_inc(staged, 1)
            with act.Fori(0, BLOCKS // 2) as pair:
                i = pair * 2
                for n in range(2):
                    act.activation(x_now[:, 1 - n, :], C.acc[:, bass.ds(i + (n + 1), 1), 0:D]
                                   .rearrange("p a d -> p (a d)"), ACT.Copy).then_inc(staged, 1)
                    act.wait_ge(turned, i + (n + 1))
                    act.wait_ge(biased, i + (n + 1))
                    act.activation(xt[:, n, :], xt_ps[n][:, :], ACT.Copy).then_inc(copied, 1)

        @block.vector
        def _(dve):
            dve.sem_inc(biased, 2)
            dve.tensor_scalar(inv[:, :], C.acc[:, 0:BLOCKS, D], 1.0, None, ALU.max).then_inc(inverted, 1)
            dve.wait_ge(inverted, 1)
            dve.reciprocal(inv[:, :], inv[:, :]).then_inc(inverted, 1)
            dve.wait_ge(inverted, 2)
            for r in range(2):
                a = C.acc[:, r * half:(r + 1) * half, 0:D]
                dve.tensor_tensor(a, a, inv[:, r * half:(r + 1) * half].unsqueeze(2)
                                  .to_broadcast([P, half, D]), ALU.mult).then_inc(scaled, 1)
                dve.wait_ge(scaled, r + 1)
                dve.wait_ge(h_in, 16 * (r + 1))
                dve.tensor_tensor(a, a, h[:, :, :], ALU.add).then_inc(added, 1)
            dve.wait_ge(loaded, 32)
            dve.wait_ge(skip_in, 16)
            with dve.Fori(0, BLOCKS // 2) as pair:
                i = pair * 2
                for n in range(2):
                    dve.wait_ge(projected, i + (n + 1))
                    dve.tensor_tensor(lin[:, n, :], out_ps[n][:, :], bias[:, :], ALU.add).then_inc(biased, 1)
                    dve.wait_ge(biased, i + (n + 3))
                    s = skip[:, bass.ds(i + n, 1), :].rearrange("p a d -> p (a d)")
                    dve.scalar_tensor_tensor(out=s, in0=lin[:, n, :], scalar=0.0, in1=s, op0=ALU.max,
                                             op1=ALU.add).then_inc(finished, 1)


def gnn(nc, x, src, dst, etype, weight, rel_emb, wv, bv, w0, b0, a1w, a1b, a2w, a2b, gw, gb, w1, b1, out):
    class C:
        pass

    with ExitStack() as st:
        K = Kit(nc, st)
        C.root = K

        def dram(name, shape, dt=F32):
            return nc.dram_tensor(name, shape, dt, kind="Internal").ap()

        C.edge_tab = dram("edge_tab", [STEPS, 4 * P], I32)
        C.facts_tab = dram("facts_tab", [4, STEPS + BATCH])
        C.row_tab = dram("row_tab", [STEPS, 2 * P], BF16)
        C.mask_tab = dram("mask_tab", [STEPS, 3 * P])
        C.index_tab = dram("index_tab", [NBATCH, P, BATCH], I32)
        C.dst_tab = dram("dst_tab", [NBATCH, P, BATCH])
        C.gate_tab = dram("gate_tab", [NBATCH, P, 3, BATCH])
        C.carry_tab = dram("carry_tab", [NBATCH, 2, BATCH])
        C.block_tab = dram("block_tab", [NBATCH, BATCH], I32)
        C.source_tab = dram("source_tab", [BLOCKS * P, 2 * D])
        C.own_tab = dram("own_tab", [BLOCKS * P, D])
        C.h_tab = dram("h_tab", [BLOCKS * P, D])
        C.skip_tab = dram("skip_tab", [BLOCKS * P, D])

        C.ident = K.sb("ident", [P, P])
        C.ones = K.sb("ones", [P, P])
        C.iota_free = K.sb("iota_free", [P, P])
        C.iota_part = K.sb("iota_part", [P, 2])
        make_constants(nc, C)
        plan_steps(nc, C, src, dst, etype, weight, gw, gb)
        C.acc = K.sb("acc", [P, BLOCKS + 1, AW])
        layer_norm(nc, C, "l0_", x, False)
        with ExitStack() as att:
            A = Kit(nc, att)
            C.node_q = A.sb("node_q", [P, BLOCKS + 1, 3, D], BF16)
            C.rel_tab = A.sb("rel_tab", [P, 2, 3, D], BF16)
            C.gate_rel = A.sb("gate_rel", [P, 2, 3, D], BF16)
            C.a2_slide = A.sb("a2_slide", [P, 2 * BATCH - 1])
            C.a2_bias = A.sb("a2_bias", [P, 1])
            for layer in range(LAYERS):
                relation_tables(nc, C, layer, rel_emb, a1w, a1b, a2w, a2b)
                node_tables(nc, C, layer, a1w, wv, bv, w0, b0)
                attention(nc, C, layer)
                combine(nc, C, layer)
        layer_norm(nc, C, "l1_", x, True)
        neighbour_sums(nc, C)
        finish(nc, C, w1, b1, out)


_INS = ["x", "src", "dst", "edge_type_200", "edge_weight", "L0_gnn_rel_emb", "L0_gnn_Wv_w", "L0_gnn_Wv_b",
        "L0_gnn_W0_w", "L0_gnn_W0_b", "L0_gnn_A1_w", "L0_gnn_A1_b", "L0_gnn_A2_w", "L0_gnn_A2_b",
        "L0_gnn_G_w", "L0_gnn_G_b", "L1_gnn_W", "L1_gnn_b"]


def kernel(**inputs):
    import numpy as np
    from concourse import bacc
    from concourse.bass_utils import run_bass_kernel_spmd

    nc = bacc.Bacc("TRN2", target_bir_lowering=False, num_devices=1)
    arrays, args = {}, []
    for name in _INS:
        a = np.ascontiguousarray(inputs[name])
        arrays[f"in_{name}"] = a
        args.append(nc.dram_tensor(f"in_{name}", a.shape, mybir.dt.from_np(a.dtype), kind="ExternalInput").ap())
    args.append(nc.dram_tensor("out_0", (NODES, D), F32, kind="ExternalOutput").ap())
    gnn(nc, *args)
    r = run_bass_kernel_spmd(nc, [arrays], core_ids=[0])
    return r.results[0]["out_0"]
```

```python
from contextlib import ExitStack

import concourse.bass as bass
from concourse import mybir

F32 = mybir.dt.float32
BF16 = mybir.dt.bfloat16
I32 = mybir.dt.int32
ALU = mybir.AluOpType
ACT = mybir.ActivationFunctionType
AX = mybir.AxisListType
ENG = mybir.EngineType

P = 128
D = 128
NODES = 12500
EDGES = 200000
RELS = 200
LAYERS = 2
BLOCKS = -(-NODES // P)
FULL_BLOCKS = NODES // P
TAIL_NODES = NODES - FULL_BLOCKS * P
EDGE_TILES = -(-EDGES // P)
FULL_TILES = EDGES // P
TAIL_EDGES = EDGES - FULL_TILES * P
CHUNKS = -(-(EDGE_TILES + BLOCKS - 1) // P)
STEPS = CHUNKS * P
BATCH = 16
GROUP = 4
GPB = BATCH // GROUP
SPLITS = 3
HIGH = RELS - P
MID0 = P - HIGH
RELP = (0, 0, 0, 1, 2)
NBATCH = STEPS // BATCH
PAD_DST = BLOCKS * P
AW = D + 1
NEG = -1.0e30
EPS = 1e-5


class Kit:

    def __init__(self, nc, stack, tag=""):
        self.nc, self.stack, self.tag = nc, stack, tag
        self.sems = []

    def sb(self, name, shape, dt=F32):
        return self.stack.enter_context(self.nc.sbuf_tensor(self.tag + name, shape, dt))

    def ps(self, name, shape):
        size = 1
        for n in shape[1:]:
            size *= n
        bank = self.stack.enter_context(self.nc.psum_tensor(self.tag + name, [P, 512], F32))
        flat = bank[0:shape[0], 0:size]
        if len(shape) == 3:
            return flat.rearrange("p (a b) -> p a b", a=shape[1])
        return flat

    def sem(self, name):
        self.sems.append(self.stack.enter_context(self.nc.semaphore(self.tag + name)))
        return self.sems[-1]

    def gather_sem(self, root, name):
        return root.stack.enter_context(self.nc.semaphore(self.tag + name))

    def block(self):
        self.stack.callback(self.clear)
        return self.stack.enter_context(self.nc.Block())

    def clear(self):
        with self.nc.Block() as block:
            @block.gpsimd
            def _(pool):
                for sem in self.sems:
                    pool.sem_clear(sem)


def over_partitions(ap):
    return ap.partition_broadcast(P)


def row(ap):
    return ap.rearrange("(a n) -> a n", a=1)


def make_constants(nc, C):
    with ExitStack() as st:
        K = Kit(nc, st, "c_")
        iota_i = K.sb("iota_i", [P, P], I32)
        part_i = K.sb("part_i", [P, 1], I32)
        part = K.sb("part", [P, 3])
        link = K.sem("link")
        filled = K.sem("filled")
        made = K.sem("made")
        block = K.block()

        @block.gpsimd
        def _(pool):
            pool.memset(C.ident[:, :], 0.0).then_inc(filled, 1)
            pool.wait_ge(filled, 1)
            pool.affine_select(out=C.ident[:, :], in_=C.ident[:, :], compare_op=ALU.not_equal, fill=1.0,
                               base=0, pattern=[[-1, P]], channel_multiplier=1).then_inc(made, 1)
            pool.memset(C.ones[:, :], 1.0).then_inc(made, 1)
            pool.iota(iota_i[:, :], [[1, P]], 0, 0).then_inc(made, 1)
            pool.iota(part_i[:, :], [[0, 1]], 0, 1).then_inc(made, 1)

        @block.vector
        def _(dve):
            dve.wait_ge(made, 4)
            dve.tensor_copy(C.iota_free[:, :], iota_i[:, :])
            dve.tensor_copy(C.iota_part[:, 0:1], part_i[:, :]).then_inc(link, 1)
            dve.wait_ge(link, 1)
            p = C.iota_part[:, 0:1]
            dve.tensor_scalar(part[:, 0:1], p, float(HIGH), float(-HIGH), ALU.is_ge, ALU.mult)
            dve.tensor_scalar(part[:, 1:2], p, float(HIGH - MID0), float(HIGH), ALU.is_lt, ALU.mult)
            dve.tensor_scalar(part[:, 2:3], p, float(2 * HIGH - MID0), float(-2 * RELS), ALU.is_ge, ALU.mult
                              ).then_inc(link, 1)
            dve.wait_ge(link, 2)
            dve.tensor_tensor(part[:, 1:2], part[:, 1:2], part[:, 2:3], ALU.add).then_inc(link, 1)
            dve.wait_ge(link, 3)
            dve.scalar_tensor_tensor(out=C.iota_part[:, 1:2], in0=p, scalar=float(P), in1=part[:, 0:1],
                                     op0=ALU.add, op1=ALU.add)
            dve.scalar_tensor_tensor(out=C.iota_part[:, 2:3], in0=p, scalar=float(P - (HIGH - MID0)),
                                     in1=part[:, 1:2], op0=ALU.add, op1=ALU.add)


def plan_steps(nc, C, src, dst, etype, weight, gw, gb):
    with ExitStack() as st:
        K = Kit(nc, st, "p_")
        edges = K.sb("edges", [P, CHUNKS, 4, P], I32)
        steps = K.sb("steps", [P, CHUNKS, 4, P], I32)
        ends_f = K.sb("ends_f", [P, 2, CHUNKS])
        start_i = K.sb("start_i", [P, BLOCKS + 1], I32)
        start = K.sb("start", [P, BLOCKS + 1])
        below = K.sb("below", [P, 2, BLOCKS])
        count = K.sb("count", [P, 2, BLOCKS])
        npair = K.sb("npair", [P, BLOCKS])
        pair_end = K.sb("pair_end", [P, BLOCKS])
        shift = K.sb("shift", [P, BLOCKS])
        step_i = K.sb("step_i", [P, CHUNKS], I32)
        step_f = K.sb("step_f", [P, CHUNKS])
        table = K.sb("table", [P, CHUNKS, BLOCKS])
        facts = K.sb("facts", [P, 4, CHUNKS])
        tile_i = K.sb("tile_i", [P, CHUNKS], I32)
        base = K.sb("base", [P, CHUNKS])
        dst_g = K.sb("dst_g", [P, CHUNKS, P])
        dst_b = K.sb("dst_b", [P, CHUNKS, P])
        src_f = K.sb("src_f", [P, CHUNKS, P])
        masks = K.sb("masks", [P, CHUNKS, 3, P])
        rows = K.sb("rows", [P, CHUNKS, 2, P], BF16)
        col_i = K.sb("col_i", [P, 2, P], I32)
        col_f = K.sb("col_f", [P, 2, P])
        wcol = K.sb("wcol", [P, 2, P])
        gf = K.sb("gf", [P, 2, 3, P])
        gwb = K.sb("gwb", [P, 2 * LAYERS])
        facts_t = K.sb("facts_t", [4 * CHUNKS, P])
        now = K.sb("now", [NBATCH, 4, BATCH])
        nxt = K.sb("nxt", [NBATCH, 3, BATCH])
        flags = K.sb("flags", [NBATCH, 4, BATCH])
        ag = K.sb("ag", [NBATCH, 2, BATCH])
        blk_i = K.sb("blk_i", [NBATCH, 2, BATCH], I32)
        zero = K.sb("zero", [4, BATCH])
        count_ps = K.ps("count_ps", [P, 2 * BLOCKS])
        facts_ps = K.ps("facts_ps", [4 * CHUNKS, P])
        turned_ps = [K.ps(f"turned_ps{i}", [P, 3, P]) for i in range(2)]
        first_ps = [K.ps(f"first_ps{i}", [P, P]) for i in range(2)]

        padded = K.sem("padded")
        loaded = K.sem("loaded")
        stored = K.sem("stored")
        counted = K.sem("counted")
        link = K.sem("link")
        summed = K.sem("summed")
        facts_ready = K.sem("facts_ready")
        facts_turned = K.sem("facts_turned")
        facts_copied = K.sem("facts_copied")
        facts_stored = K.sem("facts_stored")
        facts_back = K.sem("facts_back")
        gathered = K.gather_sem(C.root, "gathered")
        rows_ready = K.sem("rows_ready")
        rows_stored = K.sem("rows_stored")
        turned = K.sem("turned")
        copied = K.sem("copied")
        first_done = K.sem("first_done")
        gated = K.sem("gated")
        selected = K.sem("selected")
        gate_in = K.sem("gate_in")
        cols_stored = [K.sem(f"cols_stored{i}") for i in range(2)]
        last_ready = K.sem("last_ready")
        block = K.block()

        full_c = FULL_TILES // P
        rest = FULL_TILES - full_c * P
        fields = [src, dst, etype, weight.bitcast(I32)]

        @block.gpsimd
        def _(pool):
            pool.memset(edges[:, full_c:CHUNKS, :, :], 0).then_inc(padded, 1)
            pool.wait_ge(padded, 1)
            pool.memset(edges[:, full_c:CHUNKS, 1, :], PAD_DST).then_inc(padded, 1)
            pool.memset(zero[:, :], 0.0).then_inc(padded, 1)
            pool.iota(start_i[:, :], [[P, BLOCKS + 1]], 0, 0).then_inc(counted, 1)
            pool.iota(step_i[:, :], [[P, CHUNKS]], 0, 1).then_inc(counted, 1)
            pool.wait_ge(facts_ready, 1)
            pool.wait_ge(stored, 16)
            for c in range(CHUNKS):
                pool.indirect_dma_start(steps[:, c, :, :].rearrange("p f e -> p (f e)"), None, C.edge_tab,
                                        bass.IndirectOffsetOnAxis(ap=tile_i[:, c:c + 1], axis=0)
                                        ).then_inc(gathered, 16)

        @block.sync
        def _(sp):
            sp.wait_ge(padded, 3)
            for f, a in enumerate(fields):
                sp.dma_start(edges[:, 0:full_c, f, :],
                             a[0:full_c * P * P].rearrange("(c p e) -> p c e", p=P, e=P)).then_inc(loaded, 16)
                sp.dma_start(edges[0:rest, full_c, f, :],
                             a[full_c * P * P:FULL_TILES * P].rearrange("(p e) -> p e", e=P)).then_inc(loaded, 16)
                sp.dma_start(edges[rest:rest + 1, full_c, f, 0:TAIL_EDGES],
                             row(a[FULL_TILES * P:EDGES])).then_inc(loaded, 16)
            for i in range(LAYERS):
                sp.dma_start(gwb[:, 2 * i:2 * i + 1], over_partitions(row(gw[i:i + 1]))).then_inc(gate_in, 16)
                sp.dma_start(gwb[:, 2 * i + 1:2 * i + 2], over_partitions(row(gb[i:i + 1]))).then_inc(gate_in, 16)
            sp.dma_start(C.facts_tab[:, STEPS:STEPS + BATCH], zero[:, :]).then_inc(facts_stored, 16)
            sp.wait_ge(loaded, 16 * 3 * len(fields))
            sp.dma_start(C.edge_tab.rearrange("(c p) w -> p c w", p=P),
                         edges[:, :, :, :].rearrange("p c f e -> p c (f e)")).then_inc(stored, 16)
            sp.wait_ge(facts_copied, 1)
            for f in range(4):
                sp.dma_start(row(C.facts_tab[f, 0:STEPS]).rearrange("a (c p) -> (a c) p", p=P),
                             facts_t[f * CHUNKS:(f + 1) * CHUNKS, :]).then_inc(facts_stored, 16)
            sp.wait_ge(facts_stored, 16 * 5)
            for f in range(4):
                sp.dma_start(now[:, f, :], C.facts_tab[f, 0:STEPS].rearrange("(b j) -> b j", j=BATCH)
                             ).then_inc(facts_back, 16)
            for f in range(3):
                sp.dma_start(nxt[:, f, :], C.facts_tab[f, 1:STEPS + 1].rearrange("(b j) -> b j", j=BATCH)
                             ).then_inc(facts_back, 16)
            sp.wait_ge(rows_ready, 1)
            sp.dma_start(C.row_tab.rearrange("(c p) w -> p c w", p=P),
                         rows[:, :, :, :].rearrange("p c f e -> p c (f e)")).then_inc(rows_stored, 16)
            sp.dma_start(C.mask_tab.rearrange("(c p) w -> p c w", p=P),
                         masks[:, :, :, :].rearrange("p c f e -> p c (f e)")).then_inc(rows_stored, 16)
            bpc = P // BATCH
            for c in range(CHUNKS):
                sp.wait_ge(copied, 3 * (c + 1))
                sp.wait_ge(gated, LAYERS * (c + 1))
                sp.wait_ge(selected, c + 1)
                done = cols_stored[c % 2]
                bs = slice(c * bpc, (c + 1) * bpc)
                sp.dma_start(C.index_tab[bs, :, :].rearrange("b p j -> p b j"),
                             col_i[:, c % 2, :].rearrange("p (b j) -> p b j", j=BATCH)).then_inc(done, 16)
                sp.dma_start(C.dst_tab[bs, :, :].rearrange("b p j -> p b j"),
                             col_f[:, c % 2, :].rearrange("p (b j) -> p b j", j=BATCH)).then_inc(done, 16)
                for f in range(3):
                    sp.dma_start(C.gate_tab[bs, :, f, :].rearrange("b p j -> p b j"),
                                 gf[:, c % 2, f, :].rearrange("p (b j) -> p b j", j=BATCH)).then_inc(done, 16)
            sp.wait_ge(last_ready, 1)
            sp.dma_start(C.carry_tab.rearrange("b f j -> b (f j)"),
                         ag[:, :, :].rearrange("b f j -> b (f j)")).then_inc(rows_stored, 16)
            sp.dma_start(C.block_tab.rearrange("b f j -> b (f j)"),
                         blk_i[:, :, :].rearrange("b f j -> b (f j)")).then_inc(rows_stored, 16)
            sp.wait_ge(rows_stored, 64)
            for n in range(2):
                sp.wait_ge(cols_stored[n], 16 * 5 * ((CHUNKS + 1 - n) // 2))

        @block.tensor
        def _(pe):
            pe.wait_ge(summed, 1)
            pe.matmul(count_ps[:, :], C.ones[:, :], below[:, :, :].rearrange("p f b -> p (f b)"),
                      start=True, stop=True).then_inc(turned, 1)
            pe.wait_ge(facts_ready, 2)
            pe.transpose(facts_ps[:, :], facts[:, :, :].rearrange("p f c -> p (f c)"), C.ident[:, :]
                         ).then_inc(facts_turned, 1)
            pe.wait_ge(rows_ready, 1)
            for c in range(CHUNKS):
                if c >= 2:
                    pe.wait_ge(copied, 3 * (c - 1))
                pe.transpose(turned_ps[c % 2][:, 0, :], src_f[:, c, :], C.ident[:, :])
                pe.transpose(turned_ps[c % 2][:, 1, :], dst_b[:, c, :], C.ident[:, :])
                pe.transpose(turned_ps[c % 2][:, 2, :], steps[:, c, 3, :].bitcast(F32), C.ident[:, :]
                             ).then_inc(turned, 1)
                pe.wait_ge(copied, 3 * (c + 1))
                if c >= 2:
                    pe.wait_ge(selected, c - 1)
                pe.matmul(first_ps[c % 2][:, :], C.ones[0:1, :], col_f[0:1, c % 2, :],
                          start=True, stop=True).then_inc(first_done, 1)

        @block.scalar
        def _(act):
            act.wait_ge(gate_in, 16 * 2 * LAYERS)
            for c in range(CHUNKS):
                act.wait_ge(copied, 3 * (c + 1))
                if c >= 2:
                    act.wait_ge(cols_stored[c % 2], 16 * 5 * (c // 2))
                for i in range(LAYERS):
                    act.activation(gf[:, c % 2, i, :], wcol[:, c % 2, :], ACT.Sigmoid,
                                   scale=gwb[:, 2 * i:2 * i + 1], bias=gwb[:, 2 * i + 1:2 * i + 2]
                                   ).then_inc(gated, 1)

        @block.vector
        def _(dve):
            chain = [0]

            def done(ins):
                chain[0] += 1
                ins.then_inc(link, 1)
                dve.wait_ge(link, chain[0])

            dve.wait_ge(counted, 2)
            dve.wait_ge(loaded, 16 * 3 * len(fields))
            dve.tensor_copy(start[:, :], start_i[:, :])
            dve.tensor_copy(step_f[:, :], step_i[:, :])
            dve.tensor_copy(ends_f[:, 0, :], edges[:, :, 1, 0])
            done(dve.tensor_copy(ends_f[:, 1, :], edges[:, :, 1, P - 1]))
            for f, (at, e) in enumerate(((0, 1), (1, 0))):
                for c in range(CHUNKS):
                    edge = ends_f[:, e, c:c + 1]
                    if c == 0:
                        done(dve.tensor_scalar(below[:, f, :], start[:, at:at + BLOCKS], edge, None, ALU.is_gt))
                    else:
                        done(dve.scalar_tensor_tensor(out=below[:, f, :], in0=start[:, at:at + BLOCKS],
                                                      scalar=edge, in1=below[:, f, :], op0=ALU.is_gt, op1=ALU.add))
            dve.sem_inc(summed, 1)
            dve.wait_ge(turned, 1)
            done(dve.tensor_copy(count[:, :, :].rearrange("p f b -> p (f b)"), count_ps[:, :]))
            done(dve.tensor_tensor(npair[:, :], count[:, 1, :], count[:, 0, :], ALU.subtract))
            done(dve.tensor_tensor_scan(pair_end[:, :], C.ones[:, 0:BLOCKS], npair[:, :], 0.0, ALU.mult, ALU.add))
            done(dve.tensor_tensor(shift[:, :], count[:, 0, :], pair_end[:, :], ALU.subtract))
            done(dve.tensor_tensor(shift[:, :], shift[:, :], npair[:, :], ALU.add))
            grid = [P, CHUNKS, BLOCKS]
            done(dve.tensor_tensor(table[:, :, :], pair_end[:, :].unsqueeze(1).to_broadcast(grid),
                                   step_f[:, :].unsqueeze(2).to_broadcast(grid), ALU.is_le))
            done(dve.tensor_reduce(facts[:, 3, :], table[:, :, :], AX.X, ALU.add))
            done(dve.tensor_scalar(base[:, :], facts[:, 3, :], float(P), None, ALU.mult))
            done(dve.tensor_tensor(table[:, :, :], start[:, 0:BLOCKS].unsqueeze(1).to_broadcast(grid),
                                   base[:, :].unsqueeze(2).to_broadcast(grid), ALU.is_equal))
            done(dve.tensor_tensor(table[:, :, :], table[:, :, :],
                                   shift[:, :].unsqueeze(1).to_broadcast(grid), ALU.mult))
            done(dve.tensor_reduce(facts[:, 0, :], table[:, :, :], AX.X, ALU.add))
            done(dve.tensor_tensor(facts[:, 0, :], facts[:, 0, :], step_f[:, :], ALU.add))
            done(dve.tensor_scalar(facts[:, 0, :], facts[:, 0, :], float(EDGE_TILES - 1), None, ALU.min))
            dve.tensor_copy(tile_i[:, :], facts[:, 0, :]).then_inc(facts_ready, 1)
            dve.wait_ge(gathered, 16 * CHUNKS)
            dve.tensor_copy(src_f[:, :, :], steps[:, :, 0, :])
            done(dve.tensor_copy(dst_g[:, :, :], steps[:, :, 1, :]))
            dve.tensor_copy(facts[:, 1, :], dst_g[:, :, 0])
            dve.tensor_copy(facts[:, 2, :], dst_g[:, :, P - 1]).then_inc(facts_ready, 1)
            done(dve.tensor_tensor(dst_b[:, :, :], dst_g[:, :, :],
                                   base[:, :].unsqueeze(2).to_broadcast([P, CHUNKS, P]), ALU.subtract))
            dve.tensor_copy(rows[:, :, 0, :], steps[:, :, 2, :])
            dve.tensor_copy(rows[:, :, 1, :], dst_b[:, :, :])
            dve.memset(masks[:, :, 0, 0:1], 0.0)
            dve.memset(masks[:, :, 1, P - 1:P], 0.0)
            dve.tensor_tensor(masks[:, :, 0, 1:P], dst_g[:, :, 1:P], dst_g[:, :, 0:P - 1], ALU.not_equal)
            dve.tensor_tensor(masks[:, :, 1, 0:P - 1], dst_g[:, :, 0:P - 1], dst_g[:, :, 1:P], ALU.not_equal)
            done(dve.tensor_tensor(masks[:, :, 2, :], dst_g[:, :, :],
                                   dst_g[:, :, 0:1].to_broadcast([P, CHUNKS, P]), ALU.not_equal))
            flat = masks[:, :, :, :].rearrange("p c f e -> p (c f e)")
            dve.tensor_scalar(flat, flat, NEG, None, ALU.mult).then_inc(rows_ready, 1)
            dve.wait_ge(facts_turned, 1)
            dve.tensor_copy(facts_t[:, :], facts_ps[:, :]).then_inc(facts_copied, 1)
            for c in range(CHUNKS):
                dve.wait_ge(turned, c + 2)
                if c >= 2:
                    dve.wait_ge(cols_stored[c % 2], 16 * 5 * (c // 2))
                    dve.wait_ge(gated, LAYERS * (c - 1))
                dve.tensor_copy(col_i[:, c % 2, :], turned_ps[c % 2][:, 0, :]).then_inc(copied, 1)
                dve.tensor_copy(col_f[:, c % 2, :], turned_ps[c % 2][:, 1, :]).then_inc(copied, 1)
                dve.tensor_copy(wcol[:, c % 2, :], turned_ps[c % 2][:, 2, :]).then_inc(copied, 1)
                dve.wait_ge(first_done, c + 1)
                dve.tensor_scalar(gf[:, c % 2, 2, :], first_ps[c % 2][:, :], C.iota_part[:, 0:1], None,
                                  ALU.is_equal).then_inc(selected, 1)
            dve.wait_ge(facts_back, 16 * 7)
            same, goes, one = flags[:, 0, :], flags[:, 1, :], flags[:, 2, :]
            dve.tensor_scalar(blk_i[:, 0, :], now[:, 3, :], float(3 * D), None, ALU.mult)
            dve.tensor_scalar(blk_i[:, 1, :], now[:, 3, :], float(AW), None, ALU.mult)
            dve.tensor_tensor(same, now[:, 0, :], nxt[:, 0, :], ALU.is_equal)
            dve.tensor_tensor(goes, now[:, 2, :], nxt[:, 1, :], ALU.is_equal)
            dve.tensor_tensor(one, now[:, 1, :], now[:, 2, :], ALU.is_equal)
            done(dve.tensor_tensor(flags[:, 3, :], now[:, 0, :], nxt[:, 0, :], ALU.not_equal))
            done(dve.tensor_tensor(goes, goes, flags[:, 3, :], ALU.mult))
            done(dve.tensor_tensor(one, one, goes, ALU.mult))
            done(dve.tensor_tensor(same, same, one, ALU.max))
            dve.tensor_scalar(ag[:, 0, :], same, -NEG, NEG, ALU.mult, ALU.add)
            dve.tensor_scalar(ag[:, 1, :], goes, -NEG, NEG, ALU.mult, ALU.add).then_inc(last_ready, 1)


def load_node_rows(sp, acc, x, sem):
    sp.dma_start(acc[:, 0:FULL_BLOCKS, 0:D], x[0:FULL_BLOCKS * P, :].rearrange("(i p) d -> p i d", p=P)
                 ).then_inc(sem, 16)
    sp.dma_start(acc[0:TAIL_NODES, FULL_BLOCKS, 0:D], x[FULL_BLOCKS * P:NODES, :]).then_inc(sem, 16)


def layer_norm(nc, C, tag, x, skip):
    with ExitStack() as st:
        K = Kit(nc, st, tag)
        stats = K.sb("stats", [P, BLOCKS, 6])
        mv = K.sb("mv", [P, BLOCKS, 2])
        dev = K.sb("dev", [P, BLOCKS])
        rstd = K.sb("rstd", [P, BLOCKS])
        other = K.sb("other", [P, BLOCKS if skip else 1, D])
        loaded = K.sem("loaded")
        ready = K.sem("ready")
        added = K.sem("added")
        counted = K.sem("counted")
        aggregated = K.sem("aggregated")
        shifted = K.sem("shifted")
        rooted = K.sem("rooted")
        inverted = K.sem("inverted")
        centred = K.sem("centred")
        scaled = K.sem("scaled")
        clipped = K.sem("clipped")
        stored = K.sem("stored")
        acc = C.acc
        block = K.block()

        @block.gpsimd
        def _(pool):
            if skip:
                pool.memset(other[:, FULL_BLOCKS, :], 0.0).then_inc(ready, 1)
            else:
                pool.memset(acc[:, FULL_BLOCKS:BLOCKS + 1, :], 0.0).then_inc(ready, 1)

        @block.sync
        def _(sp):
            sp.wait_ge(ready, 1)
            load_node_rows(sp, other if skip else acc, x, loaded)
            if skip:
                sp.wait_ge(added, BLOCKS // 7)
                sp.dma_start(C.skip_tab.rearrange("(i p) d -> p i d", p=P), other[:, :, :]).then_inc(stored, 16)
                sp.wait_ge(clipped, BLOCKS // 7)
                sp.dma_start(C.h_tab.rearrange("(i p) d -> p i d", p=P), acc[:, 0:BLOCKS, 0:D]).then_inc(stored, 16)
                sp.wait_ge(stored, 32)

        per = 7

        @block.vector
        def _(dve):
            tgt = other if skip else acc
            with dve.Fori(0, BLOCKS // per) as r:
                dve.wait_ge(loaded, 32)
                part = tgt[:, bass.ds(r * per, per), 0:D]
                if skip:
                    dve.tensor_tensor(part, part, acc[:, bass.ds(r * per, per), 0:D], ALU.add).then_inc(added, 1)
                    dve.wait_ge(added, r + 1)
                for i in range(per):
                    dve.bn_stats(stats[:, bass.ds(r * per + i, 1), :].rearrange("p a s -> p (a s)"),
                                 tgt[:, bass.ds(r * per + i, 1), 0:D].rearrange("p a d -> p (a d)")
                                 ).then_inc(counted, 1)
            dve.wait_ge(counted, BLOCKS)
            for i in range(BLOCKS):
                dve.bn_aggr(mv[:, i, :], stats[:, i, :]).then_inc(aggregated, 1)
            dve.wait_ge(aggregated, BLOCKS)
            dve.tensor_scalar(dev[:, :], mv[:, :, 1], EPS, None, ALU.add).then_inc(shifted, 1)
            dve.wait_ge(rooted, 1)
            dve.reciprocal(rstd[:, :], dev[:, :]).then_inc(inverted, 1)
            dve.wait_ge(inverted, 1)
            for r in range(BLOCKS // per):
                rs = slice(r * per, (r + 1) * per)
                dve.tensor_tensor(acc[:, rs, 0:D], tgt[:, rs, 0:D], mv[:, rs, 0:1].to_broadcast([P, per, D]),
                                  ALU.subtract).then_inc(centred, 1)
                dve.wait_ge(centred, r + 1)
                dve.tensor_tensor(acc[:, rs, 0:D], acc[:, rs, 0:D],
                                  rstd[:, rs].unsqueeze(2).to_broadcast([P, per, D]), ALU.mult).then_inc(scaled, 1)

        @block.scalar
        def _(act):
            act.wait_ge(shifted, 1)
            act.activation(dev[:, :], dev[:, :], ACT.Sqrt).then_inc(rooted, 1)
            for r in range(BLOCKS // per):
                act.wait_ge(scaled, r + 1)
                part = acc[:, r * per:(r + 1) * per, 0:D]
                act.activation(part, part, ACT.Relu).then_inc(clipped, 1)


def split3(dve, scratch, src, hi, mid, lo, done):
    done(dve.tensor_copy(hi, src))
    done(dve.tensor_tensor(scratch, src, hi, ALU.subtract))
    done(dve.tensor_copy(mid, scratch))
    done(dve.tensor_tensor(lo, scratch, mid, ALU.subtract))


def relation_tables(nc, C, layer, rel_emb, a1w, a1b, a2w, a2b):
    with ExitStack() as st:
        K = Kit(nc, st, f"r{layer}_")
        rel = K.sb("rel", [P, 2, D])
        rel_t = K.sb("rel_t", [P, 2, P])
        w = K.sb("w", [P, D])
        b = K.sb("b", [P, D])
        tab = K.sb("tab", [P, 2, D])
        scratch = K.sb("scratch", [P, 2, D])
        parts = K.sb("parts", [P, 2, 2, 3, D], BF16)
        split = K.sem("split")
        packed = K.sem("packed")
        t_ps = K.ps("t_ps", [P, 2, P])
        r_ps = K.ps("r_ps", [P, 2, D])
        cleared = K.sem("cleared")
        loaded = K.sem("loaded")
        turned = K.sem("turned")
        copied = K.sem("copied")
        product = K.sem("product")
        link = K.sem("link")
        block = K.block()

        @block.gpsimd
        def _(pool):
            pool.memset(rel[:, :, :], 0.0).then_inc(cleared, 1)
            pool.memset(C.a2_slide[:, :], 0.0).then_inc(cleared, 1)
            pool.memset(C.rel_tab[:, 4, :], 0.0).then_inc(cleared, 1)
            pool.memset(C.gate_rel[:, 4, :], 0.0).then_inc(cleared, 1)

        @block.sync
        def _(sp):
            sp.wait_ge(cleared, 4)
            sp.dma_start(rel[:, 0, :], rel_emb[0:P, :]).then_inc(loaded, 16)
            sp.dma_start(rel[0:RELS - P, 1, :], rel_emb[P:RELS, :]).then_inc(loaded, 16)
            sp.dma_start(w[:, :], a1w[layer, D:2 * D, :]).then_inc(loaded, 16)
            sp.dma_start(b[:, :], over_partitions(row(a1b[layer, :]))).then_inc(loaded, 16)
            sp.dma_start(C.a2_slide[:, BATCH - 1:BATCH], a2w[layer, :].rearrange("(d a) -> d a", a=1)
                         ).then_inc(loaded, 16)
            sp.dma_start(C.a2_bias[:, :], over_partitions(row(a2b[layer:layer + 1]))).then_inc(loaded, 16)
            sp.wait_ge(split, 1)
            for n, tab in enumerate((C.gate_rel, C.rel_tab)):
                hi, mid, lo = (parts[:, n, 1, s, :] for s in range(3))
                for dst, src in ((tab[0:HIGH, 3, :], hi[0:HIGH, :]), (tab[HIGH:P, 3, :], mid[0:MID0, :]),
                                 (tab[0:HIGH - MID0, 4, :], mid[MID0:HIGH, :]),
                                 (tab[HIGH - MID0:2 * HIGH - MID0, 4, :], lo[0:HIGH, :])):
                    sp.dma_start(dst, src).then_inc(packed, 16)
            sp.wait_ge(packed, 128)

        @block.tensor
        def _(pe):
            pe.wait_ge(loaded, 96)
            for c in range(2):
                pe.transpose(t_ps[:, c, :], rel[:, c, :], C.ident[:, :]).then_inc(turned, 1)
            pe.wait_ge(copied, 1)
            for c in range(2):
                pe.matmul(r_ps[:, c, :], rel_t[:, c, :], w[:, :], start=True, stop=True).then_inc(product, 1)

        @block.vector
        def _(dve):
            chain = [0]

            def done(ins):
                chain[0] += 1
                ins.then_inc(link, 1)
                dve.wait_ge(link, chain[0])

            dve.wait_ge(turned, 2)
            dve.tensor_copy(rel_t[:, :, :], t_ps[:, :, :]).then_inc(copied, 1)
            dve.wait_ge(loaded, 96)
            split3(dve, scratch[:, :, :], rel[:, :, :], *(parts[:, 0, :, s, :] for s in range(3)), done)
            dve.wait_ge(product, 2)
            done(dve.tensor_tensor(tab[:, :, :], r_ps[:, :, :],
                                   b[:, :].unsqueeze(1).to_broadcast([P, 2, D]), ALU.add))
            split3(dve, scratch[:, :, :], tab[:, :, :], *(parts[:, 1, :, s, :] for s in range(3)), done)
            dve.tensor_copy(C.gate_rel[:, 0:3, :], parts[:, 0, 0, :, :])
            dve.tensor_copy(C.rel_tab[:, 0:3, :], parts[:, 1, 0, :, :]).then_inc(split, 1)


def node_tables(nc, C, layer, a1w, wv, bv, w0, b0):
    with ExitStack() as st:
        K = Kit(nc, st, f"n{layer}_")
        w = K.sb("w", [P, 4, D])
        bias = K.sb("bias", [P, 4, D])
        x_now = K.sb("x_now", [P, 2, D])
        xt = K.sb("xt", [P, 2, P])
        out = K.sb("out", [P, 2, 4, D])
        rest = K.sb("rest", [P, 2, D])
        xt_ps = [K.ps(f"xt_ps{i}", [P, P]) for i in range(2)]
        out_ps = [K.ps(f"out_ps{i}", [P, 4 * D]) for i in range(2)]
        cleared = K.sem("cleared")
        loaded = K.sem("loaded")
        staged = K.sem("staged")
        turned = K.sem("turned")
        copied = K.sem("copied")
        projected = K.sem("projected")
        biased = K.sem("biased")
        split_step = K.sem("split_step")
        stored = [K.sem(f"stored{i}") for i in range(2)]
        block = K.block()
        own = C.own_tab.rearrange("(i p) d -> i p d", p=P)
        sources = C.source_tab.rearrange("(i p) d -> i p d", p=P)

        @block.sync
        def _(sp):
            sp.wait_ge(cleared, 1)
            sp.dma_start(w[:, 0, :], a1w[layer, 0:D, :]).then_inc(loaded, 16)
            sp.dma_start(w[:, 1, :], wv[layer, :, :]).then_inc(loaded, 16)
            sp.dma_start(w[:, 2, :], a1w[layer, 2 * D:3 * D, :]).then_inc(loaded, 16)
            sp.dma_start(w[:, 3, :], w0[layer, :, :]).then_inc(loaded, 16)
            sp.dma_start(bias[:, 1, :], over_partitions(row(bv[layer, :]))).then_inc(loaded, 16)
            sp.dma_start(bias[:, 3, :], over_partitions(row(b0[layer, :]))).then_inc(loaded, 16)
            with sp.Fori(0, BLOCKS // 2) as pair:
                i = pair * 2
                for n in range(2):
                    sp.wait_ge(biased, i + (n + 3))
                    sp.dma_start(sources[bass.ds(i + n, 1), :, :].rearrange("a p d -> (a p) d"),
                                 out[:, n, 0:2, :].rearrange("p f d -> p (f d)")).then_inc(stored[n], 16)
                    sp.dma_start(own[bass.ds(i + n, 1), :, :].rearrange("a p d -> (a p) d"),
                                 out[:, n, 3, :]).then_inc(stored[n], 16)
            for n in range(2):
                sp.wait_ge(stored[n], 32 * (BLOCKS // 2))

        @block.gpsimd
        def _(pool):
            pool.memset(bias[:, :, :], 0.0).then_inc(cleared, 1)
            pool.memset(C.node_q[:, BLOCKS, :, :], 0.0)

        @block.tensor
        def _(pe):
            pe.sem_inc(projected, 2)
            pe.wait_ge(loaded, 96)
            pe.wait_ge(staged, 1)
            pe.transpose(xt_ps[0][:, :], x_now[:, 0, :], C.ident[:, :]).then_inc(turned, 1)
            with pe.Fori(0, BLOCKS // 2) as pair:
                i = pair * 2
                for n in range(2):
                    pe.wait_ge(staged, i + (n + 2))
                    pe.transpose(xt_ps[1 - n][:, :], x_now[:, 1 - n, :], C.ident[:, :]).then_inc(turned, 1)
                    pe.wait_ge(copied, i + (n + 1))
                    pe.wait_ge(biased, i + (n + 1))
                    pe.matmul(out_ps[n][:, :], xt[:, n, :], w[:, :, :].rearrange("p f d -> p (f d)"),
                              start=True, stop=True).then_inc(projected, 1)

        @block.scalar
        def _(act):
            act.activation(x_now[:, 0, :], C.acc[:, 0, 0:D], ACT.Copy).then_inc(staged, 1)
            with act.Fori(0, BLOCKS // 2) as pair:
                i = pair * 2
                for n in range(2):
                    act.activation(x_now[:, 1 - n, :], C.acc[:, bass.ds(i + (n + 1), 1), 0:D]
                                   .rearrange("p a d -> p (a d)"), ACT.Copy).then_inc(staged, 1)
                    act.wait_ge(turned, i + (n + 1))
                    act.wait_ge(projected, i + (n + 1))
                    act.activation(xt[:, n, :], xt_ps[n][:, :], ACT.Copy).then_inc(copied, 1)

        @block.vector
        def _(dve):
            dve.sem_inc(biased, 2)
            dve.wait_ge(loaded, 96)

            def emit(i):
                for n in range(2):
                    dve.wait_ge(projected, i + (n + 3))
                    waits(dve, stored[n], i * 16)
                    dve.tensor_tensor(out[:, n, :, :], out_ps[n][:, :].rearrange("p (f d) -> p f d", d=D),
                                      bias[:, :, :], ALU.add).then_inc(biased, 1)
                q = out[:, :, 2, :]
                hi, mid, lo = (C.node_q[:, bass.ds(i, 2), s, :] for s in range(3))
                dve.wait_ge(biased, i + 4)
                dve.tensor_copy(hi, q).then_inc(split_step, 1)
                dve.wait_ge(split_step, i * 2 + 1)
                dve.tensor_tensor(rest[:, :, :], q, hi, ALU.subtract).then_inc(split_step, 1)
                dve.wait_ge(split_step, i * 2 + 2)
                dve.tensor_copy(mid, rest[:, :, :]).then_inc(split_step, 1)
                dve.wait_ge(split_step, i * 2 + 3)
                dve.tensor_tensor(lo, rest[:, :, :], mid, ALU.subtract).then_inc(split_step, 1)

            emit(0)
            with dve.Fori(1, BLOCKS // 2) as pair:
                emit(pair * 2)


def fetch_places(engine, tab, at, most):
    _, vals = engine.bass.values_load_multi_w_load_instructions(
        tab[0:1, at:at + GROUP], engines=[engine.engine], min_val=0, max_val=most,
        skip_runtime_bounds_check_because="plan_steps counts at most BLOCKS pair ends")
    return vals


def waits(engine, sem, value):
    if not isinstance(value, int) or value > 0:
        engine.wait_ge(sem, value)


def wait_alone(engine, sem, value, passed):
    if isinstance(value, int):
        waits(engine, sem, value)
        return
    engine.wait_ge(sem, value)
    engine.sem_inc(passed, 1)


def run_batches(engine, emit):
    for k0 in (0, 2):
        for par in range(2):
            k = k0 + par
            emit(k0, par, True, k >= 1, k >= 2)
    with engine.Fori(2, NBATCH // 2) as pair:
        for par in range(2):
            emit(pair * 2, par, True, True, True)
    emit(NBATCH, 0, False, True, True)
    emit(NBATCH, 1, False, False, True)


def attention(nc, C, layer):
    with ExitStack() as st:
        K = Kit(nc, st, f"a{layer}_")
        index = K.sb("index", [P, 2, BATCH], I32)
        blk_q = K.sb("blk_q", [1, 2, BATCH], I32)
        blk_acc = K.sb("blk_acc", [1, 2, BATCH], I32)
        gate = K.sb("gate", [P, 2, 2, BATCH])
        mask = K.sb("mask", [BATCH, 2, 3, P])
        carry_tab = K.sb("carry_tab", [1, 2, 2, BATCH])
        dstc = K.sb("dstc", [P, 2, BATCH])
        row_sb = K.sb("row_sb", [P, 2, GROUP, 2, P], BF16)
        got = K.sb("got", [P, 2, GROUP, 2, D])
        hot = K.sb("hot", [P, 2, 4, GROUP, P], BF16)
        lrelu = K.sb("lrelu", [P, 2, GROUP, P])
        sel = K.sb("sel", [P, 2, GROUP, P])
        msg = K.sb("msg", [P, 2, BATCH, AW])
        logit = K.sb("logit", [BATCH, P])
        before = K.sb("before", [BATCH, P])
        after = K.sb("after", [BATCH, P])
        top = K.sb("top", [BATCH, P])
        diff = K.sb("diff", [BATCH, P])
        prob = K.sb("prob", [BATCH, P])
        last = K.sb("last", [1, BATCH])
        carried = K.sb("carried", [1, 2, BATCH + 1])
        carried_c = K.sb("carried_c", [BATCH, 1])
        delta = K.sb("delta", [BATCH, 1])
        diag = K.sb("diag", [BATCH, BATCH])
        wgt = K.sb("wgt", [P, 2, 2, BATCH])
        shrink_log = K.sb("shrink_log", [P, BATCH])
        shrink = K.sb("shrink", [P, 2, BATCH])
        z_ps = [K.ps(f"z_ps{i}", [P, GROUP * P]) for i in range(2)]
        rel_ps = [K.ps(f"rel_ps{i}", [P, GROUP * P]) for i in range(2)]
        logit_ps = K.ps("logit_ps", [BATCH, P])
        small_ps = K.ps("small_ps", [P, 4, BATCH])
        sum_ps = [K.ps(f"sum_ps{i}", [P, 2, 2 * P]) for i in range(2)]

        index_in = [K.sem(f"index_in{i}") for i in range(2)]
        norm_in = [K.sem(f"norm_in{i}") for i in range(2)]
        sums_in = [K.sem(f"sums_in{i}") for i in range(2)]
        rows_in = [K.sem(f"rows_in{i}") for i in range(2)]
        got_in = [K.gather_sem(C.root, f"got_in{i}") for i in range(2 * GROUP)]
        cleared = K.sem("cleared")
        passed = K.sem("passed")
        hot_ready = K.sem("hot_ready")
        z_ready = K.sem("z_ready")
        rel_ready = K.sem("rel_ready")
        z_scaled = K.sem("z_scaled")
        lrelu_ready = K.sem("lrelu_ready")
        logit_ready = K.sem("logit_ready")
        msg_ready = K.sem("msg_ready")
        sel_ready = K.sem("sel_ready")
        msg_scaled = K.sem("msg_scaled")
        pair_summed = K.sem("pair_summed")
        step_added = K.sem("step_added")
        norm_step = K.sem("norm_step")
        norm_turned = K.sem("norm_turned")
        prob_ready = K.sem("prob_ready")
        shrink_ready = K.sem("shrink_ready")
        NS = 13
        block = K.block()
        node_q = C.node_q[:, :, :, :].rearrange("p b s d -> p (b s d)")
        acc = C.acc[:, :, :].rearrange("p b w -> p (b w)")

        @block.sync
        def _(sp):
            def sums_tables(k, q):
                waits(sp, step_added, k * BATCH - 2 * BATCH)
                sp.dma_start(dstc[:, q, :], C.dst_tab[bass.ds(k - 1, 1), :, :]
                             .rearrange("b p j -> (b p) j")).then_inc(sums_in[q], 16)
                sp.dma_start(blk_acc[0:1, q, :], C.block_tab[bass.ds(k - 1, 1), 1, :]).then_inc(sums_in[q], 16)

            def emit(k0, par, logits, norm, sums):
                k = k0 + par
                if logits:
                    waits(sp, msg_ready, k * GPB - GPB)
                    sp.dma_start(index[:, par, :], C.index_tab[bass.ds(k, 1), :, :]
                                 .rearrange("b p j -> (b p) j")).then_inc(index_in[par], 16)
                    sp.dma_start(blk_q[0:1, par, :], C.block_tab[bass.ds(k, 1), 0, :]).then_inc(index_in[par], 16)
                if norm:
                    q = 1 - par
                    waits(sp, norm_step, k * NS - 2 * NS)
                    g = C.gate_tab[bass.ds(k - 1, 1), :, :, :].rearrange("b p f j -> (b p) f j")
                    sp.dma_start(gate[:, q, 0, :], g[:, layer, :]).then_inc(norm_in[q], 16)
                    sp.dma_start(gate[:, q, 1, :], g[:, 2, :]).then_inc(norm_in[q], 16)
                    sp.dma_start(mask[:, q, :, :].rearrange("s f e -> s (f e)"),
                                 C.mask_tab[bass.ds(k * BATCH - BATCH, BATCH), :]).then_inc(norm_in[q], 16)
                    sp.dma_start(carry_tab[:, q, :, :].rearrange("a f j -> a (f j)"),
                                 C.carry_tab[bass.ds(k - 1, 1), :, :].rearrange("b f j -> b (f j)")
                                 ).then_inc(norm_in[q], 16)
                if logits:
                    for g in range(GPB):
                        waits(sp, hot_ready, k * GPB + (g - 1))
                        sp.dma_start(row_sb[:, g % 2, :, :, :].rearrange("p s f e -> p (s f e)"),
                                     over_partitions(C.row_tab[bass.ds(k * BATCH + g * GROUP, GROUP), :]
                                                     .rearrange("(a s) w -> a (s w)", a=1))
                                     ).then_inc(rows_in[g % 2], 16)
                        if norm and g == 1:
                            sums_tables(k, 1 - par)
                elif par == 0:
                    sp.wait_ge(hot_ready, NBATCH * GPB - 1)
                    sp.dma_start(row_sb[:, 0, :, :, :].rearrange("p s f e -> p (s f e)"),
                                 over_partitions(C.row_tab[0:GROUP, :].rearrange("(a s) w -> a (s w)", a=1))
                                 ).then_inc(rows_in[0], 16)
                    sums_tables(k, 1 - par)
            run_batches(sp, emit)

        @block.gpsimd
        def _(pool):
            pool.memset(carried[:, :, :], NEG).then_inc(cleared, 1)

            def emit(k0, par, logits, norm, sums):
                if not logits:
                    return
                k = k0 + par
                pool.wait_ge(index_in[par], k0 * 16 + 32)
                for g in range(GPB):
                    wait_alone(pool, msg_ready, k * GPB + (g - 1), passed)
                    for j in range(GROUP):
                        n = g % 2 * GROUP + j
                        pool.indirect_dma_start(
                            got[:, g % 2, j, :, :].rearrange("p f d -> p (f d)"), None, C.source_tab,
                            bass.IndirectOffsetOnAxis(ap=index[:, par, g * GROUP + j:g * GROUP + j + 1], axis=0)
                        ).then_inc(got_in[n], 16)
            run_batches(pool, emit)

        @block.tensor
        def _(pe):
            def turn_logits(k, g, norm):
                pe.wait_ge(lrelu_ready, k * GPB + (g + 1))
                if g == 0:
                    waits(pe, norm_step, (k - 1) * NS + 1 if norm else 0)
                for j in range(GROUP):
                    n = g * GROUP + j
                    mm = pe.matmul(logit_ps[:, :], C.a2_slide[:, BATCH - 1 - n:2 * BATCH - 1 - n],
                                   lrelu[:, g % 2, j, :], start=(n == 0), stop=(n == BATCH - 1),
                                   skip_group_check=True)
                mm.then_inc(logit_ready, 1)

            def emit(k0, par, logits, norm, sums):
                k = k0 + par
                q = 1 - par
                if logits:
                    wait_alone(pe, index_in[par], k0 * 16 + 32, passed)
                for g in range(GPB):
                    grp = k * GPB + g
                    if logits:
                        place = fetch_places(pe, blk_q[:, par, :], g * GROUP, BLOCKS * 3 * D)
                        pe.wait_ge(hot_ready, grp + 1)
                        waits(pe, lrelu_ready, grp - 1)
                        for n, pack in enumerate(RELP):
                            pe.matmul(z_ps[g % 2][:, :], C.rel_tab[:, n, :],
                                      hot[:, g % 2, pack, :, :].rearrange("p j e -> p (j e)"),
                                      start=(n == 0), stop=False, skip_group_check=True)
                        for j in range(GROUP):
                            for s in range(3):
                                pe.matmul(z_ps[g % 2][:, j * P:(j + 1) * P], node_q[:, bass.ds(place[j] + s * D, D)],
                                          hot[:, g % 2, 3, j, :], start=False, stop=False, skip_group_check=True)
                        for j in range(GROUP):
                            pe.wait_ge(got_in[g % 2 * GROUP + j], k0 * (16 * GPB // 2)
                                       + (par * GPB // 2 + g // 2 + 1) * 16)
                            last_mm = pe.matmul(z_ps[g % 2][:, j * P:(j + 1) * P], got[:, g % 2, j, 0, :],
                                                C.ident[:, :], start=False, stop=True, skip_group_check=True)
                        last_mm.then_inc(z_ready, 1)
                    if logits and g > 0:
                        turn_logits(k, g - 1, norm)
                    if norm and g == 1:
                        wait_alone(pe, norm_step, k * NS + (4 - NS), passed)
                        pe.matmul(small_ps[0:1, 0, :], before[:, P - 1:P], C.ident[0:BATCH, 0:BATCH],
                                  start=True, stop=True).then_inc(norm_turned, 1)
                    if norm and g == 2:
                        wait_alone(pe, norm_step, k * NS + (6 - NS), passed)
                        pe.matmul(small_ps[0:BATCH, 1, 0:1], carried[0:1, q, 0:BATCH], C.ones[0:1, 0:1],
                                  start=True, stop=True).then_inc(norm_turned, 1)
                    if sums:
                        pe.wait_ge(sel_ready, grp + (1 - 2 * GPB))
                        pe.wait_ge(msg_scaled, grp + (1 - 2 * GPB))
                        for j in range(GROUP):
                            if j % 2 == 0:
                                waits(pe, step_added, k * BATCH + (g * GROUP + j - 2 * BATCH - 2))
                            mm = pe.matmul(sum_ps[j // 2][:, j % 2, 0:AW], sel[:, g % 2, j, :],
                                           msg[:, par, g * GROUP + j, :], start=True, stop=True)
                            if j % 2 == 1:
                                mm.then_inc(pair_summed, 1)
                    if logits:
                        waits(pe, msg_ready, grp - 1)
                        for j in range(GROUP):
                            for n, pack in enumerate(RELP):
                                mm = pe.matmul(rel_ps[g % 2][:, j * P:(j + 1) * P], hot[:, g % 2, pack, j, :],
                                               C.gate_rel[:, n, :], start=(n == 0), stop=(n == len(RELP) - 1))
                        mm.then_inc(rel_ready, 1)
                    if norm and g == 3:
                        pe.wait_ge(norm_step, k * NS + (10 - NS))
                        wait_alone(pe, prob_ready, k, passed)
                        pe.matmul(small_ps[:, 2, :], prob[:, :], C.ident[0:BATCH, 0:BATCH], start=True, stop=True)
                        pe.matmul(small_ps[:, 3, :], C.ones[0:BATCH, :], diag[:, :], start=True, stop=True
                                  ).then_inc(norm_turned, 1)
                    if logits and g == GPB - 1:
                        turn_logits(k, g, norm)
            run_batches(pe, emit)

        @block.scalar
        def _(act):
            def emit(k0, par, logits, norm, sums):
                k = k0 + par
                q = 1 - par
                for g in range(GPB):
                    if sums:
                        if g == 0:
                            act.wait_ge(norm_step, k * NS - NS)
                            waits(act, step_added, k * BATCH - 4 * BATCH)
                            act.activation(shrink[:, par, :], shrink_log[:, :], ACT.Exp).then_inc(shrink_ready, 1)
                        for j in range(GROUP):
                            n = g * GROUP + j
                            act.activation(msg[:, par, n, 0:D], msg[:, par, n, 0:D], ACT.Copy,
                                           scale=wgt[:, par, 0, n:n + 1])
                        act.activation(msg[:, par, g * GROUP:(g + 1) * GROUP, D],
                                       wgt[:, par, 1, g * GROUP:(g + 1) * GROUP], ACT.Copy).then_inc(msg_scaled, 1)
                    if logits:
                        act.wait_ge(z_ready, k * GPB + (g + 1))
                        waits(act, logit_ready, k * GPB + (g - 1))
                        act.activation(lrelu[:, g % 2, :, :].rearrange("p j e -> p (j e)"), z_ps[g % 2][:, :],
                                       ACT.Copy, scale=0.2).then_inc(z_scaled, 1)
                    if norm and g == 3:
                        act.wait_ge(norm_step, k * NS + (10 - NS))
                        act.activation(prob[:, :], diff[:, :], ACT.Exp).then_inc(prob_ready, 1)
            run_batches(act, emit)

        @block.vector
        def _(dve):
            dve.memset(C.acc[:, :, :], 0.0).then_inc(cleared, 1)
            dve.wait_ge(cleared, 2)

            def one_hots(k0, par, g):
                dve.wait_ge(rows_in[g % 2], k0 * (16 * GPB // 2) + (par * GPB // 2 + g // 2 + 1) * 16)
                waits(dve, rel_ready, (k0 + par) * GPB + (g - 1))
                types = row_sb[:, g % 2, :, 0, :]
                nodes = row_sb[:, g % 2, :, 1, :]
                for pack in range(3):
                    dve.tensor_scalar(hot[:, g % 2, pack, :, :], types, C.iota_part[:, pack:pack + 1], None,
                                      ALU.is_equal)
                dve.tensor_scalar(hot[:, g % 2, 3, :, :], nodes, C.iota_part[:, 0:1], None, ALU.is_equal
                                  ).then_inc(hot_ready, 1)

            def selectors(k0, par, g):
                at = par if g < GPB else 1 - par
                if g % GPB == 0:
                    dve.wait_ge(sums_in[at], k0 * 16 + (32 if par == 1 else 0))
                n = g % GPB * GROUP
                waits(dve, pair_summed, (k0 + par - 2) * (BATCH // 2) + (g - 1) * (GROUP // 2))
                dve.tensor_tensor(sel[:, g % 2, :, :], C.iota_free[:, :].unsqueeze(1).to_broadcast([P, GROUP, P]),
                                  dstc[:, at, n:n + GROUP].unsqueeze(2).to_broadcast([P, GROUP, P]),
                                  ALU.is_equal).then_inc(sel_ready, 1)

            one_hots(0, 0, 0)

            def emit(k0, par, logits, norm, sums):
                k = k0 + par
                q = 1 - par

                def step(ins, n, lag=1):
                    ins.then_inc(norm_step, 1)
                    dve.wait_ge(norm_step, k * NS + (n - lag * NS))

                for g in range(GPB):
                    grp = k * GPB + g
                    if sums and g == 0:
                        dve.wait_ge(norm_turned, k * 3 - 3)
                        step(dve.tensor_copy(wgt[:, par, 1, :], small_ps[:, 2, :]), 11, 2)
                        step(dve.tensor_tensor(wgt[:, par, 0, :], wgt[:, par, 1, :], gate[:, par, 0, :], ALU.mult),
                             12, 2)
                        step(dve.tensor_tensor(shrink_log[:, :], small_ps[:, 3, :], gate[:, par, 1, :], ALU.mult),
                             13, 2)
                    if logits:
                        one_hots(k0, par, g + 1)
                    if norm and g == 0:
                        dve.wait_ge(norm_in[q], k0 * 32 + 64 * par)
                        dve.wait_ge(logit_ready, k * GPB)
                        step(dve.tensor_scalar(logit[:, :], logit_ps[:, :], C.a2_bias[0:BATCH, 0:1], None,
                                               ALU.add), 1)
                    if logits:
                        dve.wait_ge(z_scaled, grp + 1)
                        act_z = lrelu[:, g % 2, :, :].rearrange("p j e -> p (j e)")
                        dve.tensor_tensor(act_z, z_ps[g % 2][:, :], act_z, ALU.max).then_inc(lrelu_ready, 1)
                    if sums:
                        place = fetch_places(dve, blk_acc[:, par, :], g * GROUP, BLOCKS * AW)
                        before_it = [dve.snap(k * BATCH + (g * GROUP + j - 2 * BATCH)) if not isinstance(k, int) else
                                     k * BATCH + (g * GROUP + j - 2 * BATCH) for j in range(GROUP)]
                        if g == 0:
                            dve.wait_ge(shrink_ready, k - 1)
                        for j in range(GROUP):
                            n = g * GROUP + j
                            if j % 2 == 0:
                                dve.wait_ge(pair_summed, k * (BATCH // 2) + (n - 2 * BATCH) // 2 + 1)
                            waits(dve, step_added, before_it[j])
                            a = acc[:, bass.ds(place[j], AW)]
                            dve.scalar_tensor_tensor(out=a, in0=a, scalar=shrink[:, par, n:n + 1],
                                                     in1=sum_ps[j // 2][:, j % 2, 0:AW], op0=ALU.mult,
                                                     op1=ALU.add).then_inc(step_added, 1)
                    if logits:
                        dve.wait_ge(rel_ready, grp + 1)
                        dve.tensor_tensor(msg[:, par, g * GROUP:(g + 1) * GROUP, 0:D], got[:, g % 2, :, 1, :],
                                          rel_ps[g % 2][:, :].rearrange("p (j d) -> p j d", d=D), ALU.mult
                                          ).then_inc(msg_ready, 1)
                    if norm if g == GPB - 1 else sums:
                        selectors(k0, par, g + 1)
                    if norm and g == 0:
                        step(dve.tensor_tensor_scan(before[:, :], mask[:, q, 0, :], logit[:, :], NEG,
                                                    ALU.add, ALU.max), 2)
                        step(dve.tensor_tensor_scan(after[:, ::-1], mask[:, q, 1, ::-1], logit[:, ::-1], NEG,
                                                    ALU.add, ALU.max), 3)
                        step(dve.tensor_tensor(top[:, :], before[:, :], after[:, :], ALU.max), 4)
                    if norm and g == 1:
                        dve.tensor_copy(carried[:, q, 0:1], carried[:, par, BATCH:BATCH + 1])
                        dve.wait_ge(norm_turned, k * 3 - 2)
                        step(dve.tensor_tensor(last[:, :], small_ps[0:1, 0, :], carry_tab[:, q, 1, :], ALU.add), 5)
                        step(dve.tensor_tensor_scan(carried[:, q, 1:BATCH + 1], carry_tab[:, q, 0, :], last[:, :],
                                                    carried[:, q, 0:1], ALU.add, ALU.max), 6)
                    if norm and g == 2:
                        dve.wait_ge(norm_turned, k * 3 - 1)
                        step(dve.tensor_copy(carried_c[:, :], small_ps[0:BATCH, 1, 0:1]), 7)
                        step(dve.scalar_tensor_tensor(out=top[:, :], in0=mask[:, q, 2, :], scalar=carried_c[:, 0:1],
                                                      in1=top[:, :], op0=ALU.add, op1=ALU.max), 8)
                        step(dve.tensor_tensor(delta[:, :], carried_c[:, :], top[:, 0:1], ALU.subtract), 9)
                        dve.tensor_scalar(diag[:, :], C.ident[0:BATCH, 0:BATCH], delta[:, 0:1], None, ALU.mult)
                        step(dve.tensor_tensor(diff[:, :], logit[:, :], top[:, :], ALU.subtract), 10)
            run_batches(dve, emit)


def combine(nc, C, layer):
    with ExitStack() as st:
        K = Kit(nc, st, f"m{layer}_")
        inv = K.sb("inv", [P, BLOCKS])
        own = K.sb("own", [P, 2, 7, D])
        chunk = 7
        loaded = [K.sem(f"loaded{i}") for i in range(2)]
        inverted = K.sem("inverted")
        scaled = K.sem("scaled")
        added = K.sem("added")
        clipped = K.sem("clipped")
        block = K.block()
        rounds = BLOCKS // chunk
        own_v = C.own_tab.rearrange("(r i p) d -> r p i d", p=P, i=chunk)

        @block.sync
        def _(sp):
            for r in range(rounds):
                if r >= 2:
                    sp.wait_ge(added, r - 1)
                sp.dma_start(own[:, r % 2, :, :], own_v[r]).then_inc(loaded[r % 2], 16)

        @block.vector
        def _(dve):
            dve.tensor_scalar(inv[:, :], C.acc[:, 0:BLOCKS, D], 1e-16, None, ALU.add).then_inc(inverted, 1)
            dve.wait_ge(inverted, 1)
            dve.reciprocal(inv[:, :], inv[:, :]).then_inc(inverted, 1)
            dve.wait_ge(inverted, 2)
            for r in range(rounds):
                a = C.acc[:, r * chunk:(r + 1) * chunk, 0:D]
                dve.tensor_tensor(a, a, inv[:, r * chunk:(r + 1) * chunk].unsqueeze(2)
                                  .to_broadcast([P, chunk, D]), ALU.mult).then_inc(scaled, 1)
                dve.wait_ge(scaled, r + 1)
                dve.wait_ge(loaded[r % 2], 16 * (r // 2 + 1))
                dve.tensor_tensor(a, a, own[:, r % 2, :, :], ALU.add).then_inc(added, 1)

        @block.scalar
        def _(act):
            for r in range(rounds):
                act.wait_ge(added, r + 1)
                a = C.acc[:, r * chunk:(r + 1) * chunk, 0:D]
                act.activation(a, a, ACT.Relu).then_inc(clipped, 1)


def neighbour_sums(nc, C):
    with ExitStack() as st:
        K = Kit(nc, st, "s_")
        depth = 2
        index = K.sb("index", [P, 2, BATCH], I32)
        blk = K.sb("blk", [1, 2, BATCH], I32)
        dstc = K.sb("dstc", [P, 2, BATCH])
        got = K.sb("got", [P, GPB, GROUP, AW])
        sel = K.sb("sel", [P, 2, GROUP, P])
        sum_ps = [K.ps(f"sum_ps{i}", [P, 2, 2 * P]) for i in range(2)]
        tabs_in = [K.sem(f"tabs_in{i}") for i in range(2)]
        got_in = [K.gather_sem(C.root, f"got_in{i}") for i in range(BATCH)]
        cleared = K.sem("cleared")
        passed = K.sem("passed")
        sel_ready = K.sem("sel_ready")
        pair_summed = K.sem("pair_summed")
        step_added = K.sem("step_added")
        block = K.block()
        acc = C.acc[:, :, :].rearrange("p b w -> p (b w)")

        def batches(engine, emit):
            for par in range(2):
                emit(0, par)
            with engine.Fori(1, NBATCH // 2) as pair:
                for par in range(2):
                    emit(pair * 2, par)

        @block.sync
        def _(sp):
            def emit(k0, par):
                k = k0 + par
                waits(sp, step_added, k * BATCH - BATCH)
                sp.dma_start(index[:, par, :], C.index_tab[bass.ds(k, 1), :, :]
                             .rearrange("b p j -> (b p) j")).then_inc(tabs_in[par], 16)
                sp.dma_start(dstc[:, par, :], C.dst_tab[bass.ds(k, 1), :, :]
                             .rearrange("b p j -> (b p) j")).then_inc(tabs_in[par], 16)
                sp.dma_start(blk[0:1, par, :], C.block_tab[bass.ds(k, 1), 1, :]).then_inc(tabs_in[par], 16)
            batches(sp, emit)

        @block.gpsimd
        def _(pool):
            pool.memset(got[:, :, :, D], 1.0).then_inc(cleared, 1)

            def emit(k0, par):
                k = k0 + par
                pool.wait_ge(tabs_in[par], k0 * 24 + 48)
                for g in range(GPB):
                    wait_alone(pool, pair_summed, k * (BATCH // 2) + (g * GROUP - BATCH + GROUP) // 2, passed)
                    for j in range(GROUP):
                        n = g * GROUP + j
                        pool.indirect_dma_start(
                            got[:, g, j, 0:D], None, C.h_tab,
                            bass.IndirectOffsetOnAxis(ap=index[:, par, n:n + 1], axis=0)).then_inc(got_in[n], 16)
            batches(pool, emit)

        @block.tensor
        def _(pe):
            pe.wait_ge(cleared, 2)

            def emit(k0, par):
                k = k0 + par
                for g in range(GPB):
                    pe.wait_ge(sel_ready, k * GPB + (g + 1))
                    for j in range(GROUP):
                        n = g * GROUP + j
                        pe.wait_ge(got_in[n], k * 16 + 16)
                        if j % 2 == 0:
                            waits(pe, step_added, k * BATCH + (n - 2))
                        mm = pe.matmul(sum_ps[j // 2][:, j % 2, 0:AW], sel[:, g % 2, j, :], got[:, g, j, :],
                                       start=True, stop=True)
                        if j % 2 == 1:
                            mm.then_inc(pair_summed, 1)
            batches(pe, emit)

        @block.vector
        def _(dve):
            dve.memset(C.acc[:, :, :], 0.0).then_inc(cleared, 1)
            dve.wait_ge(cleared, 2)

            def emit(k0, par):
                k = k0 + par
                dve.wait_ge(tabs_in[par], k0 * 24 + 48)
                for g in range(GPB):
                    waits(dve, pair_summed, k * (BATCH // 2) + (g * GROUP - GROUP) // 2)
                    dve.tensor_tensor(sel[:, g % 2, :, :], C.iota_free[:, :].unsqueeze(1).to_broadcast([P, GROUP, P]),
                                      dstc[:, par, g * GROUP:(g + 1) * GROUP].unsqueeze(2).to_broadcast([P, GROUP, P]),
                                      ALU.is_equal).then_inc(sel_ready, 1)
                    place = fetch_places(dve, blk[:, par, :], g * GROUP, BLOCKS * AW)
                    for j in range(GROUP):
                        n = g * GROUP + j
                        if j % 2 == 0:
                            dve.wait_ge(pair_summed, k * (BATCH // 2) + (n // 2 + 1))
                        waits(dve, step_added, k * BATCH + n)
                        a = acc[:, bass.ds(place[j], AW)]
                        dve.tensor_tensor(a, a, sum_ps[j // 2][:, j % 2, 0:AW], ALU.add).then_inc(step_added, 1)
            batches(dve, emit)


def finish(nc, C, w1, b1, out):
    with ExitStack() as st:
        K = Kit(nc, st, "f_")
        w = K.sb("w", [P, D])
        bias = K.sb("bias", [P, D])
        inv = K.sb("inv", [P, BLOCKS])
        h = K.sb("h", [P, BLOCKS // 2, D])
        skip = K.sb("skip", [P, BLOCKS, D])
        x_now = K.sb("x_now", [P, 2, D])
        xt = K.sb("xt", [P, 2, P])
        lin = K.sb("lin", [P, 2, D])
        xt_ps = [K.ps(f"xt_ps{i}", [P, P]) for i in range(2)]
        out_ps = [K.ps(f"out_ps{i}", [P, D]) for i in range(2)]
        loaded = K.sem("loaded")
        h_in = K.sem("h_in")
        skip_in = K.sem("skip_in")
        inverted = K.sem("inverted")
        scaled = K.sem("scaled")
        added = K.sem("added")
        staged = K.sem("staged")
        turned = K.sem("turned")
        copied = K.sem("copied")
        projected = K.sem("projected")
        biased = K.sem("biased")
        finished = K.sem("finished")
        stored = K.sem("stored")
        half = BLOCKS // 2
        h_v = C.h_tab.rearrange("(r i p) d -> r p i d", p=P, i=half)
        block = K.block()

        @block.sync
        def _(sp):
            sp.dma_start(w[:, :], w1[:, :]).then_inc(loaded, 16)
            sp.dma_start(bias[:, :], over_partitions(row(b1))).then_inc(loaded, 16)
            sp.dma_start(h[:, :, :], h_v[0]).then_inc(h_in, 16)
            sp.dma_start(skip[:, :, :], C.skip_tab.rearrange("(i p) d -> p i d", p=P)).then_inc(skip_in, 16)
            sp.wait_ge(added, 1)
            sp.dma_start(h[:, :, :], h_v[1]).then_inc(h_in, 16)
            sp.wait_ge(finished, BLOCKS)
            sp.dma_start(out[0:FULL_BLOCKS * P, :].rearrange("(i p) d -> p i d", p=P), skip[:, 0:FULL_BLOCKS, :]
                         ).then_inc(stored, 16)
            sp.dma_start(out[FULL_BLOCKS * P:NODES, :], skip[0:TAIL_NODES, FULL_BLOCKS, :]).then_inc(stored, 16)
            sp.wait_ge(stored, 32)

        @block.tensor
        def _(pe):
            pe.wait_ge(loaded, 32)
            pe.wait_ge(staged, 1)
            pe.transpose(xt_ps[0][:, :], x_now[:, 0, :], C.ident[:, :]).then_inc(turned, 1)
            with pe.Fori(0, BLOCKS // 2) as pair:
                i = pair * 2
                for n in range(2):
                    pe.wait_ge(staged, i + (n + 2))
                    pe.transpose(xt_ps[1 - n][:, :], x_now[:, 1 - n, :], C.ident[:, :]).then_inc(turned, 1)
                    pe.wait_ge(copied, i + (n + 1))
                    pe.wait_ge(biased, i + (n + 1))
                    pe.matmul(out_ps[n][:, :], xt[:, n, :], w[:, :], start=True, stop=True).then_inc(projected, 1)

        @block.scalar
        def _(act):
            act.wait_ge(added, 2)
            act.activation(x_now[:, 0, :], C.acc[:, 0, 0:D], ACT.Copy).then_inc(staged, 1)
            with act.Fori(0, BLOCKS // 2) as pair:
                i = pair * 2
                for n in range(2):
                    act.activation(x_now[:, 1 - n, :], C.acc[:, bass.ds(i + (n + 1), 1), 0:D]
                                   .rearrange("p a d -> p (a d)"), ACT.Copy).then_inc(staged, 1)
                    act.wait_ge(turned, i + (n + 1))
                    act.wait_ge(biased, i + (n + 1))
                    act.activation(xt[:, n, :], xt_ps[n][:, :], ACT.Copy).then_inc(copied, 1)

        @block.vector
        def _(dve):
            dve.sem_inc(biased, 2)
            dve.tensor_scalar(inv[:, :], C.acc[:, 0:BLOCKS, D], 1.0, None, ALU.max).then_inc(inverted, 1)
            dve.wait_ge(inverted, 1)
            dve.reciprocal(inv[:, :], inv[:, :]).then_inc(inverted, 1)
            dve.wait_ge(inverted, 2)
            for r in range(2):
                a = C.acc[:, r * half:(r + 1) * half, 0:D]
                dve.tensor_tensor(a, a, inv[:, r * half:(r + 1) * half].unsqueeze(2)
                                  .to_broadcast([P, half, D]), ALU.mult).then_inc(scaled, 1)
                dve.wait_ge(scaled, r + 1)
                dve.wait_ge(h_in, 16 * (r + 1))
                dve.tensor_tensor(a, a, h[:, :, :], ALU.add).then_inc(added, 1)
            dve.wait_ge(loaded, 32)
            dve.wait_ge(skip_in, 16)
            with dve.Fori(0, BLOCKS // 2) as pair:
                i = pair * 2
                for n in range(2):
                    dve.wait_ge(projected, i + (n + 1))
                    dve.tensor_tensor(lin[:, n, :], out_ps[n][:, :], bias[:, :], ALU.add).then_inc(biased, 1)
                    dve.wait_ge(biased, i + (n + 3))
                    s = skip[:, bass.ds(i + n, 1), :].rearrange("p a d -> p (a d)")
                    dve.scalar_tensor_tensor(out=s, in0=lin[:, n, :], scalar=0.0, in1=s, op0=ALU.max,
                                             op1=ALU.add).then_inc(finished, 1)


def gnn(nc, x, src, dst, etype, weight, rel_emb, wv, bv, w0, b0, a1w, a1b, a2w, a2b, gw, gb, w1, b1, out):
    class C:
        pass

    with ExitStack() as st:
        K = Kit(nc, st)
        C.root = K

        def dram(name, shape, dt=F32):
            return nc.dram_tensor(name, shape, dt, kind="Internal").ap()

        C.edge_tab = dram("edge_tab", [STEPS, 4 * P], I32)
        C.facts_tab = dram("facts_tab", [4, STEPS + BATCH])
        C.row_tab = dram("row_tab", [STEPS, 2 * P], BF16)
        C.mask_tab = dram("mask_tab", [STEPS, 3 * P])
        C.index_tab = dram("index_tab", [NBATCH, P, BATCH], I32)
        C.dst_tab = dram("dst_tab", [NBATCH, P, BATCH])
        C.gate_tab = dram("gate_tab", [NBATCH, P, 3, BATCH])
        C.carry_tab = dram("carry_tab", [NBATCH, 2, BATCH])
        C.block_tab = dram("block_tab", [NBATCH, 2, BATCH], I32)
        C.source_tab = dram("source_tab", [BLOCKS * P, 2 * D])
        C.own_tab = dram("own_tab", [BLOCKS * P, D])
        C.h_tab = dram("h_tab", [BLOCKS * P, D])
        C.skip_tab = dram("skip_tab", [BLOCKS * P, D])

        C.ident = K.sb("ident", [P, P])
        C.ones = K.sb("ones", [P, P])
        C.iota_free = K.sb("iota_free", [P, P])
        C.iota_part = K.sb("iota_part", [P, 3])
        make_constants(nc, C)
        plan_steps(nc, C, src, dst, etype, weight, gw, gb)
        C.acc = K.sb("acc", [P, BLOCKS + 1, AW])
        layer_norm(nc, C, "l0_", x, False)
        with ExitStack() as att:
            A = Kit(nc, att)
            C.node_q = A.sb("node_q", [P, BLOCKS + 1, 3, D], BF16)
            C.rel_tab = A.sb("rel_tab", [P, len(RELP), D], BF16)
            C.gate_rel = A.sb("gate_rel", [P, len(RELP), D], BF16)
            C.a2_slide = A.sb("a2_slide", [P, 2 * BATCH - 1])
            C.a2_bias = A.sb("a2_bias", [P, 1])
            for layer in range(LAYERS):
                relation_tables(nc, C, layer, rel_emb, a1w, a1b, a2w, a2b)
                node_tables(nc, C, layer, a1w, wv, bv, w0, b0)
                attention(nc, C, layer)
                combine(nc, C, layer)
        layer_norm(nc, C, "l1_", x, True)
        neighbour_sums(nc, C)
        finish(nc, C, w1, b1, out)


_INS = ["x", "src", "dst", "edge_type_200", "edge_weight", "L0_gnn_rel_emb", "L0_gnn_Wv_w", "L0_gnn_Wv_b",
        "L0_gnn_W0_w", "L0_gnn_W0_b", "L0_gnn_A1_w", "L0_gnn_A1_b", "L0_gnn_A2_w", "L0_gnn_A2_b",
        "L0_gnn_G_w", "L0_gnn_G_b", "L1_gnn_W", "L1_gnn_b"]


def kernel(**inputs):
    import numpy as np
    from concourse import bacc
    from concourse.bass_utils import run_bass_kernel_spmd

    nc = bacc.Bacc("TRN2", target_bir_lowering=False, num_devices=1)
    arrays, args = {}, []
    for name in _INS:
        a = np.ascontiguousarray(inputs[name])
        arrays[f"in_{name}"] = a
        args.append(nc.dram_tensor(f"in_{name}", a.shape, mybir.dt.from_np(a.dtype), kind="ExternalInput").ap())
    args.append(nc.dram_tensor("out_0", (NODES, D), F32, kind="ExternalOutput").ap())
    gnn(nc, *args)
    r = run_bass_kernel_spmd(nc, [arrays], core_ids=[0])
    return r.results[0]["out_0"]
```

```python
from contextlib import ExitStack

import concourse.bass as bass
from concourse import mybir

F32 = mybir.dt.float32
BF16 = mybir.dt.bfloat16
I32 = mybir.dt.int32
ALU = mybir.AluOpType
ACT = mybir.ActivationFunctionType
AX = mybir.AxisListType
ENG = mybir.EngineType

P = 128
D = 128
NODES = 12500
EDGES = 200000
RELS = 200
LAYERS = 2
BLOCKS = -(-NODES // P)
FULL_BLOCKS = NODES // P
TAIL_NODES = NODES - FULL_BLOCKS * P
EDGE_TILES = -(-EDGES // P)
FULL_TILES = EDGES // P
TAIL_EDGES = EDGES - FULL_TILES * P
CHUNKS = -(-(EDGE_TILES + BLOCKS - 1) // P)
STEPS = CHUNKS * P
BATCH = 16
GROUP = 4
GPB = BATCH // GROUP
SPLITS = 3
HIGH = RELS - P
MID0 = P - HIGH
RELP = (0, 0, 0, 1, 2)
NBATCH = STEPS // BATCH
PAD_DST = BLOCKS * P
AW = D + 1
NEG = -1.0e30
EPS = 1e-5


class Kit:

    def __init__(self, nc, stack, tag=""):
        self.nc, self.stack, self.tag = nc, stack, tag
        self.sems = []

    def sb(self, name, shape, dt=F32):
        return self.stack.enter_context(self.nc.sbuf_tensor(self.tag + name, shape, dt))

    def ps(self, name, shape):
        size = 1
        for n in shape[1:]:
            size *= n
        bank = self.stack.enter_context(self.nc.psum_tensor(self.tag + name, [P, 512], F32))
        flat = bank[0:shape[0], 0:size]
        if len(shape) == 3:
            return flat.rearrange("p (a b) -> p a b", a=shape[1])
        return flat

    def two_banks(self, name, a, b):
        banks = self.stack.enter_context(self.nc.psum_tensor(self.tag + name, [P, 1024], F32))
        return banks[:, :].rearrange("p (a b) -> p a b", a=a, b=b)

    def sem(self, name):
        self.sems.append(self.stack.enter_context(self.nc.semaphore(self.tag + name)))
        return self.sems[-1]

    def gather_sem(self, root, name):
        return root.stack.enter_context(self.nc.semaphore(self.tag + name))

    def block(self):
        self.stack.callback(self.clear)
        return self.stack.enter_context(self.nc.Block())

    def clear(self):
        with self.nc.Block() as block:
            @block.gpsimd
            def _(pool):
                for sem in self.sems:
                    pool.sem_clear(sem)


def over_partitions(ap):
    return ap.partition_broadcast(P)


def row(ap):
    return ap.rearrange("(a n) -> a n", a=1)


def make_constants(nc, C):
    with ExitStack() as st:
        K = Kit(nc, st, "c_")
        iota_i = K.sb("iota_i", [P, P], I32)
        part_i = K.sb("part_i", [P, 1], I32)
        part = K.sb("part", [P, 3])
        link = K.sem("link")
        filled = K.sem("filled")
        made = K.sem("made")
        block = K.block()

        @block.gpsimd
        def _(pool):
            pool.memset(C.ident[:, :], 0.0).then_inc(filled, 1)
            pool.wait_ge(filled, 1)
            pool.affine_select(out=C.ident[:, :], in_=C.ident[:, :], compare_op=ALU.not_equal, fill=1.0,
                               base=0, pattern=[[-1, P]], channel_multiplier=1).then_inc(made, 1)
            pool.memset(C.ones[:, :], 1.0).then_inc(made, 1)
            pool.iota(iota_i[:, :], [[1, P]], 0, 0).then_inc(made, 1)
            pool.iota(part_i[:, :], [[0, 1]], 0, 1).then_inc(made, 1)

        @block.vector
        def _(dve):
            dve.wait_ge(made, 4)
            dve.tensor_copy(C.iota_free[:, :], iota_i[:, :])
            dve.tensor_copy(C.iota_part[:, 0:1], part_i[:, :]).then_inc(link, 1)
            dve.wait_ge(link, 1)
            p = C.iota_part[:, 0:1]
            dve.tensor_scalar(part[:, 0:1], p, float(HIGH), float(-HIGH), ALU.is_ge, ALU.mult)
            dve.tensor_scalar(part[:, 1:2], p, float(HIGH - MID0), float(HIGH), ALU.is_lt, ALU.mult)
            dve.tensor_scalar(part[:, 2:3], p, float(2 * HIGH - MID0), float(-2 * RELS), ALU.is_ge, ALU.mult
                              ).then_inc(link, 1)
            dve.wait_ge(link, 2)
            dve.tensor_tensor(part[:, 1:2], part[:, 1:2], part[:, 2:3], ALU.add).then_inc(link, 1)
            dve.wait_ge(link, 3)
            dve.scalar_tensor_tensor(out=C.iota_part[:, 1:2], in0=p, scalar=float(P), in1=part[:, 0:1],
                                     op0=ALU.add, op1=ALU.add)
            dve.scalar_tensor_tensor(out=C.iota_part[:, 2:3], in0=p, scalar=float(P - (HIGH - MID0)),
                                     in1=part[:, 1:2], op0=ALU.add, op1=ALU.add)


def plan_steps(nc, C, src, dst, etype, weight, gw, gb):
    with ExitStack() as st:
        K = Kit(nc, st, "p_")
        edges = K.sb("edges", [P, CHUNKS, 4, P], I32)
        steps = K.sb("steps", [P, CHUNKS, 4, P], I32)
        ends_f = K.sb("ends_f", [P, 2, CHUNKS])
        start_i = K.sb("start_i", [P, BLOCKS + 1], I32)
        start = K.sb("start", [P, BLOCKS + 1])
        below = K.sb("below", [P, 2, BLOCKS])
        count = K.sb("count", [P, 2, BLOCKS])
        npair = K.sb("npair", [P, BLOCKS])
        pair_end = K.sb("pair_end", [P, BLOCKS])
        shift = K.sb("shift", [P, BLOCKS])
        step_i = K.sb("step_i", [P, CHUNKS], I32)
        step_f = K.sb("step_f", [P, CHUNKS])
        table = K.sb("table", [P, CHUNKS, BLOCKS])
        facts = K.sb("facts", [P, 4, CHUNKS])
        tile_i = K.sb("tile_i", [P, CHUNKS], I32)
        base = K.sb("base", [P, CHUNKS])
        dst_g = K.sb("dst_g", [P, CHUNKS, P])
        dst_b = K.sb("dst_b", [P, CHUNKS, P])
        src_f = K.sb("src_f", [P, CHUNKS, P])
        masks = K.sb("masks", [P, CHUNKS, 3, P])
        rows = K.sb("rows", [P, CHUNKS, 2, P], BF16)
        col_i = K.sb("col_i", [P, 2, P], I32)
        col_f = K.sb("col_f", [P, 2, P])
        wcol = K.sb("wcol", [P, 2, P])
        gf = K.sb("gf", [P, 2, 3, P])
        gwb = K.sb("gwb", [P, 2 * LAYERS])
        facts_t = K.sb("facts_t", [4 * CHUNKS, P])
        now = K.sb("now", [NBATCH, 4, BATCH])
        nxt = K.sb("nxt", [NBATCH, 3, BATCH])
        flags = K.sb("flags", [NBATCH, 4, BATCH])
        ag = K.sb("ag", [NBATCH, 2, BATCH])
        blk_i = K.sb("blk_i", [NBATCH, 2, BATCH], I32)
        zero = K.sb("zero", [4, BATCH])
        count_ps = K.ps("count_ps", [P, 2 * BLOCKS])
        facts_ps = K.ps("facts_ps", [4 * CHUNKS, P])
        turned_ps = [K.ps(f"turned_ps{i}", [P, 3, P]) for i in range(2)]
        first_ps = [K.ps(f"first_ps{i}", [P, P]) for i in range(2)]

        padded = K.sem("padded")
        loaded = K.sem("loaded")
        stored = K.sem("stored")
        counted = K.sem("counted")
        link = K.sem("link")
        summed = K.sem("summed")
        facts_ready = K.sem("facts_ready")
        facts_turned = K.sem("facts_turned")
        facts_copied = K.sem("facts_copied")
        facts_stored = K.sem("facts_stored")
        facts_back = K.sem("facts_back")
        gathered = K.gather_sem(C.root, "gathered")
        rows_ready = K.sem("rows_ready")
        rows_stored = K.sem("rows_stored")
        turned = K.sem("turned")
        copied = K.sem("copied")
        first_done = K.sem("first_done")
        gated = K.sem("gated")
        selected = K.sem("selected")
        gate_in = K.sem("gate_in")
        cols_stored = [K.sem(f"cols_stored{i}") for i in range(2)]
        last_ready = K.sem("last_ready")
        block = K.block()

        full_c = FULL_TILES // P
        rest = FULL_TILES - full_c * P
        fields = [src, dst, etype, weight.bitcast(I32)]

        @block.gpsimd
        def _(pool):
            pool.memset(edges[:, full_c:CHUNKS, :, :], 0).then_inc(padded, 1)
            pool.wait_ge(padded, 1)
            pool.memset(edges[:, full_c:CHUNKS, 1, :], PAD_DST).then_inc(padded, 1)
            pool.memset(zero[:, :], 0.0).then_inc(padded, 1)
            pool.iota(start_i[:, :], [[P, BLOCKS + 1]], 0, 0).then_inc(counted, 1)
            pool.iota(step_i[:, :], [[P, CHUNKS]], 0, 1).then_inc(counted, 1)
            pool.wait_ge(facts_ready, 1)
            pool.wait_ge(stored, 16)
            for c in range(CHUNKS):
                pool.indirect_dma_start(steps[:, c, :, :].rearrange("p f e -> p (f e)"), None, C.edge_tab,
                                        bass.IndirectOffsetOnAxis(ap=tile_i[:, c:c + 1], axis=0)
                                        ).then_inc(gathered, 16)

        @block.sync
        def _(sp):
            sp.wait_ge(padded, 3)
            for f, a in enumerate(fields):
                sp.dma_start(edges[:, 0:full_c, f, :],
                             a[0:full_c * P * P].rearrange("(c p e) -> p c e", p=P, e=P)).then_inc(loaded, 16)
                sp.dma_start(edges[0:rest, full_c, f, :],
                             a[full_c * P * P:FULL_TILES * P].rearrange("(p e) -> p e", e=P)).then_inc(loaded, 16)
                sp.dma_start(edges[rest:rest + 1, full_c, f, 0:TAIL_EDGES],
                             row(a[FULL_TILES * P:EDGES])).then_inc(loaded, 16)
            for i in range(LAYERS):
                sp.dma_start(gwb[:, 2 * i:2 * i + 1], over_partitions(row(gw[i:i + 1]))).then_inc(gate_in, 16)
                sp.dma_start(gwb[:, 2 * i + 1:2 * i + 2], over_partitions(row(gb[i:i + 1]))).then_inc(gate_in, 16)
            sp.dma_start(C.facts_tab[:, STEPS:STEPS + BATCH], zero[:, :]).then_inc(facts_stored, 16)
            sp.wait_ge(loaded, 16 * 3 * len(fields))
            sp.dma_start(C.edge_tab.rearrange("(c p) w -> p c w", p=P),
                         edges[:, :, :, :].rearrange("p c f e -> p c (f e)")).then_inc(stored, 16)
            sp.wait_ge(facts_copied, 1)
            for f in range(4):
                sp.dma_start(row(C.facts_tab[f, 0:STEPS]).rearrange("a (c p) -> (a c) p", p=P),
                             facts_t[f * CHUNKS:(f + 1) * CHUNKS, :]).then_inc(facts_stored, 16)
            sp.wait_ge(facts_stored, 16 * 5)
            for f in range(4):
                sp.dma_start(now[:, f, :], C.facts_tab[f, 0:STEPS].rearrange("(b j) -> b j", j=BATCH)
                             ).then_inc(facts_back, 16)
            for f in range(3):
                sp.dma_start(nxt[:, f, :], C.facts_tab[f, 1:STEPS + 1].rearrange("(b j) -> b j", j=BATCH)
                             ).then_inc(facts_back, 16)
            sp.wait_ge(rows_ready, 1)
            sp.dma_start(C.row_tab.rearrange("(c p) w -> p c w", p=P),
                         rows[:, :, :, :].rearrange("p c f e -> p c (f e)")).then_inc(rows_stored, 16)
            sp.dma_start(C.mask_tab.rearrange("(c p) w -> p c w", p=P),
                         masks[:, :, :, :].rearrange("p c f e -> p c (f e)")).then_inc(rows_stored, 16)
            bpc = P // BATCH
            for c in range(CHUNKS):
                sp.wait_ge(copied, 3 * (c + 1))
                sp.wait_ge(gated, LAYERS * (c + 1))
                sp.wait_ge(selected, c + 1)
                done = cols_stored[c % 2]
                bs = slice(c * bpc, (c + 1) * bpc)
                sp.dma_start(C.index_tab[bs, :, :].rearrange("b p j -> p b j"),
                             col_i[:, c % 2, :].rearrange("p (b j) -> p b j", j=BATCH)).then_inc(done, 16)
                sp.dma_start(C.dst_tab[bs, :, :].rearrange("b p j -> p b j"),
                             col_f[:, c % 2, :].rearrange("p (b j) -> p b j", j=BATCH)).then_inc(done, 16)
                for f in range(3):
                    sp.dma_start(C.gate_tab[bs, :, f, :].rearrange("b p j -> p b j"),
                                 gf[:, c % 2, f, :].rearrange("p (b j) -> p b j", j=BATCH)).then_inc(done, 16)
            sp.wait_ge(last_ready, 1)
            sp.dma_start(C.carry_tab.rearrange("b f j -> b (f j)"),
                         ag[:, :, :].rearrange("b f j -> b (f j)")).then_inc(rows_stored, 16)
            sp.dma_start(C.block_tab.rearrange("b f j -> b (f j)"),
                         blk_i[:, :, :].rearrange("b f j -> b (f j)")).then_inc(rows_stored, 16)
            sp.wait_ge(rows_stored, 64)
            for n in range(2):
                sp.wait_ge(cols_stored[n], 16 * 5 * ((CHUNKS + 1 - n) // 2))

        @block.tensor
        def _(pe):
            pe.wait_ge(summed, 1)
            pe.matmul(count_ps[:, :], C.ones[:, :], below[:, :, :].rearrange("p f b -> p (f b)"),
                      start=True, stop=True).then_inc(turned, 1)
            pe.wait_ge(facts_ready, 2)
            pe.transpose(facts_ps[:, :], facts[:, :, :].rearrange("p f c -> p (f c)"), C.ident[:, :]
                         ).then_inc(facts_turned, 1)
            pe.wait_ge(rows_ready, 1)
            for c in range(CHUNKS):
                if c >= 2:
                    pe.wait_ge(copied, 3 * (c - 1))
                pe.transpose(turned_ps[c % 2][:, 0, :], src_f[:, c, :], C.ident[:, :])
                pe.transpose(turned_ps[c % 2][:, 1, :], dst_b[:, c, :], C.ident[:, :])
                pe.transpose(turned_ps[c % 2][:, 2, :], steps[:, c, 3, :].bitcast(F32), C.ident[:, :]
                             ).then_inc(turned, 1)
                pe.wait_ge(copied, 3 * (c + 1))
                if c >= 2:
                    pe.wait_ge(selected, c - 1)
                pe.matmul(first_ps[c % 2][:, :], C.ones[0:1, :], col_f[0:1, c % 2, :],
                          start=True, stop=True).then_inc(first_done, 1)

        @block.scalar
        def _(act):
            act.wait_ge(gate_in, 16 * 2 * LAYERS)
            for c in range(CHUNKS):
                act.wait_ge(copied, 3 * (c + 1))
                if c >= 2:
                    act.wait_ge(cols_stored[c % 2], 16 * 5 * (c // 2))
                for i in range(LAYERS):
                    act.activation(gf[:, c % 2, i, :], wcol[:, c % 2, :], ACT.Sigmoid,
                                   scale=gwb[:, 2 * i:2 * i + 1], bias=gwb[:, 2 * i + 1:2 * i + 2]
                                   ).then_inc(gated, 1)

        @block.vector
        def _(dve):
            chain = [0]

            def done(ins):
                chain[0] += 1
                ins.then_inc(link, 1)
                dve.wait_ge(link, chain[0])

            dve.wait_ge(counted, 2)
            dve.wait_ge(loaded, 16 * 3 * len(fields))
            dve.tensor_copy(start[:, :], start_i[:, :])
            dve.tensor_copy(step_f[:, :], step_i[:, :])
            dve.tensor_copy(ends_f[:, 0, :], edges[:, :, 1, 0])
            done(dve.tensor_copy(ends_f[:, 1, :], edges[:, :, 1, P - 1]))
            for f, (at, e) in enumerate(((0, 1), (1, 0))):
                for c in range(CHUNKS):
                    edge = ends_f[:, e, c:c + 1]
                    if c == 0:
                        done(dve.tensor_scalar(below[:, f, :], start[:, at:at + BLOCKS], edge, None, ALU.is_gt))
                    else:
                        done(dve.scalar_tensor_tensor(out=below[:, f, :], in0=start[:, at:at + BLOCKS],
                                                      scalar=edge, in1=below[:, f, :], op0=ALU.is_gt, op1=ALU.add))
            dve.sem_inc(summed, 1)
            dve.wait_ge(turned, 1)
            done(dve.tensor_copy(count[:, :, :].rearrange("p f b -> p (f b)"), count_ps[:, :]))
            done(dve.tensor_tensor(npair[:, :], count[:, 1, :], count[:, 0, :], ALU.subtract))
            done(dve.tensor_tensor_scan(pair_end[:, :], C.ones[:, 0:BLOCKS], npair[:, :], 0.0, ALU.mult, ALU.add))
            done(dve.tensor_tensor(shift[:, :], count[:, 0, :], pair_end[:, :], ALU.subtract))
            done(dve.tensor_tensor(shift[:, :], shift[:, :], npair[:, :], ALU.add))
            grid = [P, CHUNKS, BLOCKS]
            done(dve.tensor_tensor(table[:, :, :], pair_end[:, :].unsqueeze(1).to_broadcast(grid),
                                   step_f[:, :].unsqueeze(2).to_broadcast(grid), ALU.is_le))
            done(dve.tensor_reduce(facts[:, 3, :], table[:, :, :], AX.X, ALU.add))
            done(dve.tensor_scalar(base[:, :], facts[:, 3, :], float(P), None, ALU.mult))
            done(dve.tensor_tensor(table[:, :, :], start[:, 0:BLOCKS].unsqueeze(1).to_broadcast(grid),
                                   base[:, :].unsqueeze(2).to_broadcast(grid), ALU.is_equal))
            done(dve.tensor_tensor(table[:, :, :], table[:, :, :],
                                   shift[:, :].unsqueeze(1).to_broadcast(grid), ALU.mult))
            done(dve.tensor_reduce(facts[:, 0, :], table[:, :, :], AX.X, ALU.add))
            done(dve.tensor_tensor(facts[:, 0, :], facts[:, 0, :], step_f[:, :], ALU.add))
            done(dve.tensor_scalar(facts[:, 0, :], facts[:, 0, :], float(EDGE_TILES - 1), None, ALU.min))
            dve.tensor_copy(tile_i[:, :], facts[:, 0, :]).then_inc(facts_ready, 1)
            dve.wait_ge(gathered, 16 * CHUNKS)
            dve.tensor_copy(src_f[:, :, :], steps[:, :, 0, :])
            done(dve.tensor_copy(dst_g[:, :, :], steps[:, :, 1, :]))
            dve.tensor_copy(facts[:, 1, :], dst_g[:, :, 0])
            dve.tensor_copy(facts[:, 2, :], dst_g[:, :, P - 1]).then_inc(facts_ready, 1)
            done(dve.tensor_tensor(dst_b[:, :, :], dst_g[:, :, :],
                                   base[:, :].unsqueeze(2).to_broadcast([P, CHUNKS, P]), ALU.subtract))
            dve.tensor_copy(rows[:, :, 0, :], steps[:, :, 2, :])
            dve.tensor_copy(rows[:, :, 1, :], dst_b[:, :, :])
            dve.memset(masks[:, :, 0, 0:1], 0.0)
            dve.memset(masks[:, :, 1, P - 1:P], 0.0)
            dve.tensor_tensor(masks[:, :, 0, 1:P], dst_g[:, :, 1:P], dst_g[:, :, 0:P - 1], ALU.not_equal)
            dve.tensor_tensor(masks[:, :, 1, 0:P - 1], dst_g[:, :, 0:P - 1], dst_g[:, :, 1:P], ALU.not_equal)
            done(dve.tensor_tensor(masks[:, :, 2, :], dst_g[:, :, :],
                                   dst_g[:, :, 0:1].to_broadcast([P, CHUNKS, P]), ALU.not_equal))
            flat = masks[:, :, :, :].rearrange("p c f e -> p (c f e)")
            dve.tensor_scalar(flat, flat, NEG, None, ALU.mult).then_inc(rows_ready, 1)
            dve.wait_ge(facts_turned, 1)
            dve.tensor_copy(facts_t[:, :], facts_ps[:, :]).then_inc(facts_copied, 1)
            for c in range(CHUNKS):
                dve.wait_ge(turned, c + 2)
                if c >= 2:
                    dve.wait_ge(cols_stored[c % 2], 16 * 5 * (c // 2))
                    dve.wait_ge(gated, LAYERS * (c - 1))
                dve.tensor_copy(col_i[:, c % 2, :], turned_ps[c % 2][:, 0, :]).then_inc(copied, 1)
                dve.tensor_copy(col_f[:, c % 2, :], turned_ps[c % 2][:, 1, :]).then_inc(copied, 1)
                dve.tensor_copy(wcol[:, c % 2, :], turned_ps[c % 2][:, 2, :]).then_inc(copied, 1)
                dve.wait_ge(first_done, c + 1)
                dve.tensor_scalar(gf[:, c % 2, 2, :], first_ps[c % 2][:, :], C.iota_part[:, 0:1], None,
                                  ALU.is_equal).then_inc(selected, 1)
            dve.wait_ge(facts_back, 16 * 7)
            same, goes, one = flags[:, 0, :], flags[:, 1, :], flags[:, 2, :]
            dve.tensor_scalar(blk_i[:, 0, :], now[:, 3, :], float(3 * D), None, ALU.mult)
            dve.tensor_scalar(blk_i[:, 1, :], now[:, 3, :], float(AW), None, ALU.mult)
            dve.tensor_tensor(same, now[:, 0, :], nxt[:, 0, :], ALU.is_equal)
            dve.tensor_tensor(goes, now[:, 2, :], nxt[:, 1, :], ALU.is_equal)
            dve.tensor_tensor(one, now[:, 1, :], now[:, 2, :], ALU.is_equal)
            done(dve.tensor_tensor(flags[:, 3, :], now[:, 0, :], nxt[:, 0, :], ALU.not_equal))
            done(dve.tensor_tensor(goes, goes, flags[:, 3, :], ALU.mult))
            done(dve.tensor_tensor(one, one, goes, ALU.mult))
            done(dve.tensor_tensor(same, same, one, ALU.max))
            dve.tensor_scalar(ag[:, 0, :], same, -NEG, NEG, ALU.mult, ALU.add)
            dve.tensor_scalar(ag[:, 1, :], goes, -NEG, NEG, ALU.mult, ALU.add).then_inc(last_ready, 1)


def load_node_rows(sp, acc, x, sem):
    sp.dma_start(acc[:, 0:FULL_BLOCKS, 0:D], x[0:FULL_BLOCKS * P, :].rearrange("(i p) d -> p i d", p=P)
                 ).then_inc(sem, 16)
    sp.dma_start(acc[0:TAIL_NODES, FULL_BLOCKS, 0:D], x[FULL_BLOCKS * P:NODES, :]).then_inc(sem, 16)


def layer_norm(nc, C, tag, x, skip):
    with ExitStack() as st:
        K = Kit(nc, st, tag)
        stats = K.sb("stats", [P, BLOCKS, 6])
        mv = K.sb("mv", [P, BLOCKS, 2])
        dev = K.sb("dev", [P, BLOCKS])
        rstd = K.sb("rstd", [P, BLOCKS])
        other = K.sb("other", [P, BLOCKS if skip else 1, D])
        loaded = K.sem("loaded")
        ready = K.sem("ready")
        added = K.sem("added")
        counted = K.sem("counted")
        aggregated = K.sem("aggregated")
        shifted = K.sem("shifted")
        rooted = K.sem("rooted")
        inverted = K.sem("inverted")
        centred = K.sem("centred")
        scaled = K.sem("scaled")
        clipped = K.sem("clipped")
        stored = K.sem("stored")
        acc = C.acc
        block = K.block()

        @block.gpsimd
        def _(pool):
            if skip:
                pool.memset(other[:, FULL_BLOCKS, :], 0.0).then_inc(ready, 1)
            else:
                pool.memset(acc[:, FULL_BLOCKS:BLOCKS + 1, :], 0.0).then_inc(ready, 1)

        @block.sync
        def _(sp):
            sp.wait_ge(ready, 1)
            load_node_rows(sp, other if skip else acc, x, loaded)
            if skip:
                sp.wait_ge(added, BLOCKS // 7)
                sp.dma_start(C.skip_tab.rearrange("(i p) d -> p i d", p=P), other[:, :, :]).then_inc(stored, 16)
                sp.wait_ge(clipped, BLOCKS // 7)
                sp.dma_start(C.h_tab.rearrange("(i p) d -> p i d", p=P), acc[:, 0:BLOCKS, 0:D]).then_inc(stored, 16)
                sp.wait_ge(stored, 32)

        per = 7

        @block.vector
        def _(dve):
            tgt = other if skip else acc
            with dve.Fori(0, BLOCKS // per) as r:
                dve.wait_ge(loaded, 32)
                part = tgt[:, bass.ds(r * per, per), 0:D]
                if skip:
                    dve.tensor_tensor(part, part, acc[:, bass.ds(r * per, per), 0:D], ALU.add).then_inc(added, 1)
                    dve.wait_ge(added, r + 1)
                for i in range(per):
                    dve.bn_stats(stats[:, bass.ds(r * per + i, 1), :].rearrange("p a s -> p (a s)"),
                                 tgt[:, bass.ds(r * per + i, 1), 0:D].rearrange("p a d -> p (a d)")
                                 ).then_inc(counted, 1)
            dve.wait_ge(counted, BLOCKS)
            for i in range(BLOCKS):
                dve.bn_aggr(mv[:, i, :], stats[:, i, :]).then_inc(aggregated, 1)
            dve.wait_ge(aggregated, BLOCKS)
            dve.tensor_scalar(dev[:, :], mv[:, :, 1], EPS, None, ALU.add).then_inc(shifted, 1)
            dve.wait_ge(rooted, 1)
            dve.reciprocal(rstd[:, :], dev[:, :]).then_inc(inverted, 1)
            dve.wait_ge(inverted, 1)
            for r in range(BLOCKS // per):
                rs = slice(r * per, (r + 1) * per)
                dve.tensor_tensor(acc[:, rs, 0:D], tgt[:, rs, 0:D], mv[:, rs, 0:1].to_broadcast([P, per, D]),
                                  ALU.subtract).then_inc(centred, 1)
                dve.wait_ge(centred, r + 1)
                dve.tensor_tensor(acc[:, rs, 0:D], acc[:, rs, 0:D],
                                  rstd[:, rs].unsqueeze(2).to_broadcast([P, per, D]), ALU.mult).then_inc(scaled, 1)

        @block.scalar
        def _(act):
            act.wait_ge(shifted, 1)
            act.activation(dev[:, :], dev[:, :], ACT.Sqrt).then_inc(rooted, 1)
            for r in range(BLOCKS // per):
                act.wait_ge(scaled, r + 1)
                part = acc[:, r * per:(r + 1) * per, 0:D]
                act.activation(part, part, ACT.Relu).then_inc(clipped, 1)


def split3(dve, scratch, src, hi, mid, lo, done):
    done(dve.tensor_copy(hi, src))
    done(dve.tensor_tensor(scratch, src, hi, ALU.subtract))
    done(dve.tensor_copy(mid, scratch))
    done(dve.tensor_tensor(lo, scratch, mid, ALU.subtract))


def relation_tables(nc, C, layer, rel_emb, a1w, a1b, a2w, a2b):
    with ExitStack() as st:
        K = Kit(nc, st, f"r{layer}_")
        rel = K.sb("rel", [P, 2, D])
        rel_t = K.sb("rel_t", [P, 2, P])
        w = K.sb("w", [P, D])
        b = K.sb("b", [P, D])
        signs = K.sb("signs", [P, D])
        tab = K.sb("tab", [P, 2, D])
        scratch = K.sb("scratch", [P, 2, D])
        parts = K.sb("parts", [P, 2, 2, 3, D], BF16)
        split = K.sem("split")
        packed = K.sem("packed")
        t_ps = K.ps("t_ps", [P, 2, P])
        r_ps = K.ps("r_ps", [P, 2, D])
        cleared = K.sem("cleared")
        loaded = K.sem("loaded")
        turned = K.sem("turned")
        copied = K.sem("copied")
        product = K.sem("product")
        link = K.sem("link")
        block = K.block()

        @block.gpsimd
        def _(pool):
            pool.memset(rel[:, :, :], 0.0).then_inc(cleared, 1)
            pool.memset(C.rel_tabs[:, 4, :, :], 0.0).then_inc(cleared, 1)

        @block.sync
        def _(sp):
            sp.wait_ge(cleared, 2)
            sp.dma_start(rel[:, 0, :], rel_emb[0:P, :]).then_inc(loaded, 16)
            sp.dma_start(rel[0:RELS - P, 1, :], rel_emb[P:RELS, :]).then_inc(loaded, 16)
            sp.dma_start(w[:, :], a1w[layer, D:2 * D, :]).then_inc(loaded, 16)
            sp.dma_start(b[:, :], over_partitions(row(a1b[layer, :]))).then_inc(loaded, 16)
            sp.dma_start(C.a2_row[:, :], over_partitions(row(a2w[layer, :]))).then_inc(loaded, 16)
            sp.dma_start(C.a2_bias[:, :], over_partitions(row(a2b[layer:layer + 1]))).then_inc(loaded, 16)
            sp.wait_ge(split, 1)
            for n, tab in enumerate((C.rel_tabs[:, :, 1, :], C.rel_tabs[:, :, 0, :])):
                hi, mid, lo = (parts[:, n, 1, s, :] for s in range(3))
                for dst, src in ((tab[0:HIGH, 3, :], hi[0:HIGH, :]), (tab[HIGH:P, 3, :], mid[0:MID0, :]),
                                 (tab[0:HIGH - MID0, 4, :], mid[MID0:HIGH, :]),
                                 (tab[HIGH - MID0:2 * HIGH - MID0, 4, :], lo[0:HIGH, :])):
                    sp.dma_start(dst, src).then_inc(packed, 16)
            sp.wait_ge(packed, 128)

        @block.tensor
        def _(pe):
            pe.wait_ge(loaded, 96)
            for c in range(2):
                pe.transpose(t_ps[:, c, :], rel[:, c, :], C.ident[:, :]).then_inc(turned, 1)
            pe.wait_ge(copied, 1)
            for c in range(2):
                pe.matmul(r_ps[:, c, :], rel_t[:, c, :], w[:, :], start=True, stop=True).then_inc(product, 1)

        @block.vector
        def _(dve):
            chain = [0]

            def done(ins):
                chain[0] += 1
                ins.then_inc(link, 1)
                dve.wait_ge(link, chain[0])

            dve.wait_ge(turned, 2)
            dve.tensor_copy(rel_t[:, :, :], t_ps[:, :, :]).then_inc(copied, 1)
            dve.wait_ge(loaded, 96)
            split3(dve, scratch[:, :, :], rel[:, :, :], *(parts[:, 0, :, s, :] for s in range(3)), done)
            dve.wait_ge(product, 2)
            done(dve.tensor_tensor(tab[:, :, :], r_ps[:, :, :],
                                   b[:, :].unsqueeze(1).to_broadcast([P, 2, D]), ALU.add))
            done(dve.tensor_tensor(tab[:, :, :], tab[:, :, :],
                                   C.a2_row[:, :].unsqueeze(1).to_broadcast([P, 2, D]), ALU.mult))
            done(dve.tensor_scalar(signs[:, :], C.a2_row[:, :], 0.0, 0.8, ALU.is_ge, ALU.mult))
            done(dve.tensor_scalar(C.a2_sign[:, :], signs[:, :], -0.4, None, ALU.add))
            split3(dve, scratch[:, :, :], tab[:, :, :], *(parts[:, 1, :, s, :] for s in range(3)), done)
            dve.tensor_copy(C.rel_tabs[:, 0:3, 1, :], parts[:, 0, 0, :, :])
            dve.tensor_copy(C.rel_tabs[:, 0:3, 0, :], parts[:, 1, 0, :, :]).then_inc(split, 1)


def node_tables(nc, C, layer, a1w, wv, bv, w0, b0):
    with ExitStack() as st:
        K = Kit(nc, st, f"n{layer}_")
        w = K.sb("w", [P, 4, D])
        bias = K.sb("bias", [P, 4, D])
        x_now = K.sb("x_now", [P, 2, D])
        xt = K.sb("xt", [P, 2, P])
        out = K.sb("out", [P, 4, 4, D])
        rest = K.sb("rest", [P, 2, D])
        xt_ps = [K.ps(f"xt_ps{i}", [P, P]) for i in range(2)]
        out_ps = [K.ps(f"out_ps{i}", [P, 4 * D]) for i in range(2)]
        cleared = K.sem("cleared")
        loaded = K.sem("loaded")
        staged = K.sem("staged")
        turned = K.sem("turned")
        copied = K.sem("copied")
        projected = K.sem("projected")
        biased = K.sem("biased")
        split_step = K.sem("split_step")
        stored = [K.sem(f"stored{i}") for i in range(4)]
        folded = K.sem("folded")
        block = K.block()
        own = C.own_tab.rearrange("(i p) d -> i p d", p=P)
        sources = C.source_tab.rearrange("(i p) d -> i p d", p=P)

        @block.sync
        def _(sp):
            sp.wait_ge(cleared, 1)
            sp.dma_start(w[:, 0, :], a1w[layer, 0:D, :]).then_inc(loaded, 16)
            sp.dma_start(w[:, 1, :], wv[layer, :, :]).then_inc(loaded, 16)
            sp.dma_start(w[:, 2, :], a1w[layer, 2 * D:3 * D, :]).then_inc(loaded, 16)
            sp.dma_start(w[:, 3, :], w0[layer, :, :]).then_inc(loaded, 16)
            sp.dma_start(bias[:, 1, :], over_partitions(row(bv[layer, :]))).then_inc(loaded, 16)
            sp.dma_start(bias[:, 3, :], over_partitions(row(b0[layer, :]))).then_inc(loaded, 16)

            def store(i, at):
                for n in range(2):
                    sp.wait_ge(biased, i + (n + 3))
                    sp.dma_start(sources[bass.ds(i + n, 1), :, :].rearrange("a p d -> (a p) d"),
                                 out[:, at + n, 0:2, :].rearrange("p f d -> p (f d)")).then_inc(stored[at + n], 16)
                    sp.dma_start(own[bass.ds(i + n, 1), :, :].rearrange("a p d -> (a p) d"),
                                 out[:, at + n, 3, :]).then_inc(stored[at + n], 16)

            store(0, 0)
            with sp.Fori(0, BLOCKS // 4) as two_pairs:
                i = two_pairs * 4
                store(i + 2, 2)
                store(i + 4, 0)
            for n in range(2):
                sp.wait_ge(stored[n], 32 * (BLOCKS // 4 + 1))
                sp.wait_ge(stored[2 + n], 32 * (BLOCKS // 4 + 1))

        @block.gpsimd
        def _(pool):
            pool.memset(bias[:, :, :], 0.0).then_inc(cleared, 1)
            pool.memset(C.node_q[:, BLOCKS, :, :], 0.0)

        @block.tensor
        def _(pe):
            pe.sem_inc(projected, 2)
            pe.wait_ge(loaded, 96)
            pe.wait_ge(folded, 1)
            pe.wait_ge(staged, 1)
            pe.transpose(xt_ps[0][:, :], x_now[:, 0, :], C.ident[:, :]).then_inc(turned, 1)
            with pe.Fori(0, BLOCKS // 2) as pair:
                i = pair * 2
                for n in range(2):
                    pe.wait_ge(staged, i + (n + 2))
                    pe.transpose(xt_ps[1 - n][:, :], x_now[:, 1 - n, :], C.ident[:, :]).then_inc(turned, 1)
                    pe.wait_ge(copied, i + (n + 1))
                    pe.wait_ge(biased, i + (n + 1))
                    pe.matmul(out_ps[n][:, :], xt[:, n, :], w[:, :, :].rearrange("p f d -> p (f d)"),
                              start=True, stop=True).then_inc(projected, 1)

        @block.scalar
        def _(act):
            act.activation(x_now[:, 0, :], C.acc[:, 0, 0:D], ACT.Copy).then_inc(staged, 1)
            with act.Fori(0, BLOCKS // 2) as pair:
                i = pair * 2
                for n in range(2):
                    act.activation(x_now[:, 1 - n, :], C.acc[:, bass.ds(i + (n + 1), 1), 0:D]
                                   .rearrange("p a d -> p (a d)"), ACT.Copy).then_inc(staged, 1)
                    act.wait_ge(turned, i + (n + 1))
                    act.wait_ge(projected, i + (n + 1))
                    act.activation(xt[:, n, :], xt_ps[n][:, :], ACT.Copy).then_inc(copied, 1)

        @block.vector
        def _(dve):
            dve.sem_inc(biased, 2)
            for n in range(2):
                dve.sem_inc(stored[2 + n], 32)
            dve.wait_ge(loaded, 96)
            dve.tensor_tensor(w[:, 0:4:2, :], w[:, 0:4:2, :], C.a2_row[:, :].unsqueeze(1).to_broadcast([P, 2, D]),
                              ALU.mult).then_inc(folded, 1)

            def high(i, at):
                dve.wait_ge(biased, i + 4)
                dve.tensor_copy(C.node_q[:, bass.ds(i, 2), 0, :], out[:, at:at + 2, 2, :]).then_inc(split_step, 1)

            def remainder(i, at):
                dve.wait_ge(split_step, i * 2 + 1)
                dve.tensor_tensor(rest[:, :, :], out[:, at:at + 2, 2, :], C.node_q[:, bass.ds(i, 2), 0, :],
                                  ALU.subtract).then_inc(split_step, 1)

            def middle(i):
                dve.wait_ge(split_step, i * 2 + 2)
                dve.tensor_copy(C.node_q[:, bass.ds(i, 2), 1, :], rest[:, :, :]).then_inc(split_step, 1)

            def low(i):
                dve.wait_ge(split_step, i * 2 + 3)
                dve.tensor_tensor(C.node_q[:, bass.ds(i, 2), 2, :], rest[:, :, :], C.node_q[:, bass.ds(i, 2), 1, :],
                                  ALU.subtract).then_inc(split_step, 1)

            def add_bias(i, n, at, used):
                dve.wait_ge(projected, i + (n + 3))
                waits(dve, stored[at + n], used)
                dve.tensor_tensor(out[:, at + n, :, :], out_ps[n][:, :].rearrange("p (f d) -> p f d", d=D),
                                  bias[:, :, :], ALU.add).then_inc(biased, 1)

            def emit(i, at, used):
                add_bias(i, 0, at, used)
                remainder(i - 2, 2 - at)
                add_bias(i, 1, at, used)
                middle(i - 2)
                high(i, at)
                low(i - 2)

            assert BLOCKS % 4 == 2
            add_bias(0, 0, 0, 0)
            add_bias(0, 1, 0, 0)
            high(0, 0)
            with dve.Fori(0, BLOCKS // 4) as two_pairs:
                i = two_pairs * 4
                emit(i + 2, 2, two_pairs * 32 + 32)
                emit(i + 4, 0, two_pairs * 32 + 32)
            remainder(BLOCKS - 2, 0)
            middle(BLOCKS - 2)
            low(BLOCKS - 2)


def fetch_places(engine, tab, at, most):
    _, vals = engine.bass.values_load_multi_w_load_instructions(
        tab[0:1, at:at + GROUP], engines=[engine.engine], min_val=0, max_val=most,
        skip_runtime_bounds_check_because="plan_steps counts at most BLOCKS pair ends")
    return vals


def waits(engine, sem, value):
    if not isinstance(value, int) or value > 0:
        engine.wait_ge(sem, value)


def wait_alone(engine, sem, value, passed):
    if isinstance(value, int):
        waits(engine, sem, value)
        return
    engine.wait_ge(sem, value)
    engine.sem_inc(passed, 1)


def run_batches(engine, emit):
    for k0 in (0, 2):
        for par in range(2):
            k = k0 + par
            emit(k0, par, True, k >= 1, k >= 2)
    with engine.Fori(2, NBATCH // 2) as pair:
        for par in range(2):
            emit(pair * 2, par, True, True, True)
    emit(NBATCH, 0, False, True, True)
    emit(NBATCH, 1, False, False, True)


def attention(nc, C, layer):
    with ExitStack() as st:
        K = Kit(nc, st, f"a{layer}_")
        index = K.sb("index", [P, 2, BATCH], I32)
        blk_q = K.sb("blk_q", [1, 2, BATCH], I32)
        blk_acc = K.sb("blk_acc", [1, 2, BATCH], I32)
        gate = K.sb("gate", [P, 2, 2, BATCH])
        mask = K.sb("mask", [BATCH, 2, 3, P])
        carry_tab = K.sb("carry_tab", [1, 2, 2, BATCH])
        dstc = K.sb("dstc", [P, 2, BATCH])
        row_sb = K.sb("row_sb", [P, 2, GROUP, 2, P], BF16)
        got = K.sb("got", [P, 2, GROUP, 2, D])
        hot = K.sb("hot", [P, 2, 4, GROUP, P], BF16)
        bent = K.sb("bent", [P, GROUP, D])
        unread = K.sb("unread", [P, 2, GROUP, D], BF16)
        straight_sum = K.sb("straight_sum", [P, 2, BATCH])
        bent_sum = K.sb("bent_sum", [P, 2, BATCH])
        sel = K.sb("sel", [P, 2, GROUP, P])
        msg = K.sb("msg", [P, 2, BATCH, AW])
        logit = K.sb("logit", [BATCH, P])
        before = K.sb("before", [BATCH, P])
        after = K.sb("after", [BATCH, P])
        top = K.sb("top", [BATCH, P])
        diff = K.sb("diff", [BATCH, P])
        prob = K.sb("prob", [BATCH, P])
        last = K.sb("last", [1, BATCH])
        carried = K.sb("carried", [1, 2, BATCH + 1])
        carried_c = K.sb("carried_c", [BATCH, 1])
        delta = K.sb("delta", [BATCH, 1])
        diag = K.sb("diag", [BATCH, BATCH])
        wgt = K.sb("wgt", [P, 2, 2, BATCH])
        shrink_log = K.sb("shrink_log", [P, BATCH])
        shrink = K.sb("shrink", [P, 2, BATCH])
        z_ps = [K.two_banks(f"z_ps{i}", GROUP, 2 * D) for i in range(2)]
        logit_ps = K.ps("logit_ps", [BATCH, P])
        small_ps = K.ps("small_ps", [P, 4, BATCH])
        sum_ps = [K.ps(f"sum_ps{i}", [P, 2, 2 * P]) for i in range(2)]

        index_in = [K.sem(f"index_in{i}") for i in range(2)]
        norm_in = [K.sem(f"norm_in{i}") for i in range(2)]
        sums_in = [K.sem(f"sums_in{i}") for i in range(2)]
        rows_in = [K.sem(f"rows_in{i}") for i in range(2)]
        got_in = [K.gather_sem(C.root, f"got_in{i}") for i in range(2 * GROUP)]
        cleared = K.sem("cleared")
        passed = K.sem("passed")
        hot_ready = K.sem("hot_ready")
        z_ready = K.sem("z_ready")
        straight_summed = K.sem("straight_summed")
        bare_ready = K.sem("bare_ready")
        bent_ready = K.sem("bent_ready")
        bent_summed = K.sem("bent_summed")
        logit_ready = K.sem("logit_ready")
        msg_ready = K.sem("msg_ready")
        sel_ready = K.sem("sel_ready")
        msg_scaled = K.sem("msg_scaled")
        pair_summed = K.sem("pair_summed")
        step_added = K.sem("step_added")
        norm_step = K.sem("norm_step")
        norm_turned = K.sem("norm_turned")
        prob_ready = K.sem("prob_ready")
        shrink_ready = K.sem("shrink_ready")
        NS = 14
        block = K.block()
        node_q = C.node_q[:, :, :, :].rearrange("p b s d -> p (b s d)")
        acc = C.acc[:, :, :].rearrange("p b w -> p (b w)")

        @block.sync
        def _(sp):
            def sums_tables(k, q):
                waits(sp, step_added, k * BATCH - 2 * BATCH)
                sp.dma_start(dstc[:, q, :], C.dst_tab[bass.ds(k - 1, 1), :, :]
                             .rearrange("b p j -> (b p) j")).then_inc(sums_in[q], 16)
                sp.dma_start(blk_acc[0:1, q, :], C.block_tab[bass.ds(k - 1, 1), 1, :]).then_inc(sums_in[q], 16)

            def emit(k0, par, logits, norm, sums):
                k = k0 + par
                if logits:
                    waits(sp, msg_ready, k * GPB - GPB)
                    sp.dma_start(index[:, par, :], C.index_tab[bass.ds(k, 1), :, :]
                                 .rearrange("b p j -> (b p) j")).then_inc(index_in[par], 16)
                    sp.dma_start(blk_q[0:1, par, :], C.block_tab[bass.ds(k, 1), 0, :]).then_inc(index_in[par], 16)
                if norm:
                    q = 1 - par
                    waits(sp, norm_step, k * NS - 2 * NS)
                    g = C.gate_tab[bass.ds(k - 1, 1), :, :, :].rearrange("b p f j -> (b p) f j")
                    sp.dma_start(gate[:, q, 0, :], g[:, layer, :]).then_inc(norm_in[q], 16)
                    sp.dma_start(gate[:, q, 1, :], g[:, 2, :]).then_inc(norm_in[q], 16)
                    sp.dma_start(mask[:, q, :, :].rearrange("s f e -> s (f e)"),
                                 C.mask_tab[bass.ds(k * BATCH - BATCH, BATCH), :]).then_inc(norm_in[q], 16)
                    sp.dma_start(carry_tab[:, q, :, :].rearrange("a f j -> a (f j)"),
                                 C.carry_tab[bass.ds(k - 1, 1), :, :].rearrange("b f j -> b (f j)")
                                 ).then_inc(norm_in[q], 16)
                if logits:
                    for g in range(GPB):
                        waits(sp, hot_ready, k * GPB + (g - 1))
                        sp.dma_start(row_sb[:, g % 2, :, :, :].rearrange("p s f e -> p (s f e)"),
                                     over_partitions(C.row_tab[bass.ds(k * BATCH + g * GROUP, GROUP), :]
                                                     .rearrange("(a s) w -> a (s w)", a=1))
                                     ).then_inc(rows_in[g % 2], 16)
                        if norm and g == 1:
                            sums_tables(k, 1 - par)
                elif par == 0:
                    sp.wait_ge(hot_ready, NBATCH * GPB - 1)
                    sp.dma_start(row_sb[:, 0, :, :, :].rearrange("p s f e -> p (s f e)"),
                                 over_partitions(C.row_tab[0:GROUP, :].rearrange("(a s) w -> a (s w)", a=1))
                                 ).then_inc(rows_in[0], 16)
                    sums_tables(k, 1 - par)
            run_batches(sp, emit)

        @block.gpsimd
        def _(pool):
            pool.memset(carried[:, :, :], NEG).then_inc(cleared, 1)

            def emit(k0, par, logits, norm, sums):
                if not logits:
                    return
                k = k0 + par
                pool.wait_ge(index_in[par], k0 * 16 + 32)
                for g in range(GPB):
                    wait_alone(pool, msg_ready, k * GPB + (g - 1), passed)
                    for j in range(GROUP):
                        n = g % 2 * GROUP + j
                        pool.indirect_dma_start(
                            got[:, g % 2, j, :, :].rearrange("p f d -> p (f d)"), None, C.source_tab,
                            bass.IndirectOffsetOnAxis(ap=index[:, par, g * GROUP + j:g * GROUP + j + 1], axis=0)
                        ).then_inc(got_in[n], 16)
            run_batches(pool, emit)

        @block.tensor
        def _(pe):
            def emit(k0, par, logits, norm, sums):
                k = k0 + par
                q = 1 - par
                if logits:
                    wait_alone(pe, index_in[par], k0 * 16 + 32, passed)

                def add_up(g):
                    pe.wait_ge(sel_ready, k * GPB + (g + 1 - 2 * GPB))
                    pe.wait_ge(msg_scaled, k * GPB + (g + 1 - 2 * GPB))
                    for j in range(GROUP):
                        if j % 2 == 0:
                            waits(pe, step_added, k * BATCH + (g * GROUP + j - 2 * BATCH - 2))
                        mm = pe.matmul(sum_ps[j // 2][:, j % 2, 0:AW], sel[:, g % 2, j, :],
                                       msg[:, par, g * GROUP + j, :], start=True, stop=True)
                        if j % 2 == 1:
                            mm.then_inc(pair_summed, 1)

                for g in range(GPB):
                    grp = k * GPB + g
                    if logits:
                        place = fetch_places(pe, blk_q[:, par, :], g * GROUP, BLOCKS * 3 * D)
                        pe.wait_ge(hot_ready, grp + 1)
                        waits(pe, msg_ready, grp - 1)
                        for j in range(GROUP):
                            for n, pack in enumerate(RELP):
                                pe.matmul(z_ps[g % 2][:, j, :], hot[:, g % 2, pack, j, :],
                                          C.rel_tabs[:, n, :, :].rearrange("p f d -> p (f d)"),
                                          start=(n == 0 and j % 2 == 0), stop=False, skip_group_check=True)
                            for s in range(3):
                                pe.matmul(z_ps[g % 2][:, j, 0:D], hot[:, g % 2, 3, j, :],
                                          node_q[:, bass.ds(place[j] + s * D, D)],
                                          start=False, stop=False, skip_group_check=True)
                        for j in range(GROUP):
                            pe.wait_ge(got_in[g % 2 * GROUP + j], k0 * (16 * GPB // 2)
                                       + (par * GPB // 2 + g // 2 + 1) * 16)
                            last_mm = pe.matmul(z_ps[g % 2][:, j, 0:D], C.ident[:, :], got[:, g % 2, j, 0, :],
                                                start=False, stop=True, skip_group_check=True)
                        last_mm.then_inc(z_ready, 1)
                    if sums:
                        add_up(g)
                    if norm and g == 0:
                        wait_alone(pe, bent_summed, k * GPB, passed)
                        pe.matmul(logit_ps[:, :], straight_sum[:, q, :], C.ident[:, :], start=True, stop=False)
                        pe.matmul(logit_ps[:, :], bent_sum[:, q, :], C.ident[:, :], start=False, stop=True
                                  ).then_inc(logit_ready, 1)
                    if norm and g == 1:
                        wait_alone(pe, norm_step, k * NS + (4 - NS), passed)
                        pe.matmul(small_ps[0:1, 0, :], before[:, P - 1:P], C.ident[0:BATCH, 0:BATCH],
                                  start=True, stop=True).then_inc(norm_turned, 1)
                    if norm and g == 2:
                        wait_alone(pe, norm_step, k * NS + (6 - NS), passed)
                        pe.matmul(small_ps[0:BATCH, 1, 0:1], carried[0:1, q, 0:BATCH], C.ones[0:1, 0:1],
                                  start=True, stop=True).then_inc(norm_turned, 1)
                    if norm and g == 3:
                        pe.wait_ge(norm_step, k * NS + (11 - NS))
                        wait_alone(pe, prob_ready, k, passed)
                        pe.matmul(small_ps[:, 2, :], prob[:, :], C.ident[0:BATCH, 0:BATCH], start=True, stop=True)
                        pe.matmul(small_ps[:, 3, :], C.ones[0:BATCH, :], diag[:, :], start=True, stop=True
                                  ).then_inc(norm_turned, 1)
            run_batches(pe, emit)

        @block.scalar
        def _(act):
            def emit(k0, par, logits, norm, sums):
                k = k0 + par
                q = 1 - par

                def scale_group(g):
                    for j in range(GROUP):
                        n = g * GROUP + j
                        act.activation(msg[:, par, n, 0:D], msg[:, par, n, 0:D], ACT.Copy,
                                       scale=wgt[:, par, 0, n:n + 1])
                    act.activation(msg[:, par, g * GROUP:(g + 1) * GROUP, D],
                                   wgt[:, par, 1, g * GROUP:(g + 1) * GROUP], ACT.Copy).then_inc(msg_scaled, 1)

                def sum_bent(at, g):
                    for j in range(GROUP):
                        n = g * GROUP + j
                        total = act.activation(bent[:, j, :], bent[:, j, :], ACT.Copy,
                                               accum_out=bent_sum[:, at, n:n + 1])
                    total.then_inc(bent_summed, 1)

                for g in range(GPB):
                    if norm and g == 0:
                        act.wait_ge(bent_ready, k * GPB)
                        sum_bent(q, GPB - 1)
                    if logits and g > 0:
                        act.wait_ge(bent_ready, k * GPB + g)
                        sum_bent(par, g - 1)
                    if sums and g == 0:
                        act.wait_ge(norm_step, k * NS - (NS + 1))
                    if sums:
                        scale_group(g)
                    if sums and g == 0:
                        act.wait_ge(norm_step, k * NS - NS)
                        waits(act, step_added, k * BATCH - 4 * BATCH)
                        act.activation(shrink[:, par, :], shrink_log[:, :], ACT.Exp).then_inc(shrink_ready, 1)
                    if norm and g == 3:
                        act.wait_ge(norm_step, k * NS + (10 - NS))
                        act.activation(prob[:, :], diff[:, :], ACT.Exp).then_inc(prob_ready, 1)
                    if logits:
                        act.wait_ge(z_ready, k * GPB + (g + 1))
                        waits(act, bent_summed, k * GPB + g)
                        act.activation(bent[:, :, :], z_ps[g % 2][:, :, 0:D], ACT.Abs).then_inc(bare_ready, 1)
                        for j in range(GROUP):
                            n = g * GROUP + j
                            total = act.activation(unread[:, g % 2, j, :], z_ps[g % 2][:, j, 0:D], ACT.Copy, scale=0.6,
                                                   accum_out=straight_sum[:, par, n:n + 1])
                        total.then_inc(straight_summed, 1)
            run_batches(act, emit)

        @block.vector
        def _(dve):
            dve.memset(C.acc[:, :, :], 0.0).then_inc(cleared, 1)
            dve.wait_ge(cleared, 2)

            def one_hots(k0, par, g, pack):
                if pack == 0:
                    dve.wait_ge(rows_in[g % 2], k0 * (16 * GPB // 2) + (par * GPB // 2 + g // 2 + 1) * 16)
                    waits(dve, z_ready, (k0 + par) * GPB + (g - 1))
                keys = row_sb[:, g % 2, :, pack // 3, :]
                hots = dve.tensor_scalar(hot[:, g % 2, pack, :, :], keys, C.iota_part[:, pack % 3:pack % 3 + 1],
                                         None, ALU.is_equal)
                if pack == 3:
                    hots.then_inc(hot_ready, 1)

            def selectors(k0, par, g):
                if g == 0:
                    dve.wait_ge(sums_in[par], k0 * 16)
                n = g * GROUP
                waits(dve, pair_summed, (k0 + par - 2) * (BATCH // 2) + (g - 1) * (GROUP // 2))
                dve.tensor_tensor(sel[:, g % 2, :, :], C.iota_free[:, :].unsqueeze(1).to_broadcast([P, GROUP, P]),
                                  dstc[:, par, n:n + GROUP].unsqueeze(2).to_broadcast([P, GROUP, P]),
                                  ALU.is_equal).then_inc(sel_ready, 1)

            for pack in range(4):
                one_hots(0, 0, 0, pack)

            def emit(k0, par, logits, norm, sums):
                k = k0 + par
                q = 1 - par

                def add_step(k, par, g, j, place):
                    n = g * GROUP + j
                    if n == 0:
                        dve.wait_ge(shrink_ready, k - 1)
                    if j % 2 == 0:
                        dve.wait_ge(pair_summed, k * (BATCH // 2) + (n - 2 * BATCH) // 2 + 1)
                    waits(dve, step_added, k * BATCH + (n - 2 * BATCH))
                    a = acc[:, bass.ds(place[j], AW)]
                    dve.scalar_tensor_tensor(out=a, in0=a, scalar=shrink[:, par, n:n + 1],
                                             in1=sum_ps[j // 2][:, j % 2, 0:AW], op0=ALU.mult,
                                             op1=ALU.add).then_inc(step_added, 1)

                def bend(g):
                    dve.wait_ge(bare_ready, k * GPB + (g + 1))
                    dve.tensor_tensor(bent[:, :, :], bent[:, :, :],
                                      C.a2_sign[:, :].unsqueeze(1).to_broadcast([P, GROUP, D]), ALU.mult
                                      ).then_inc(bent_ready, 1)

                def weigh(g):
                    if sums:
                        dve.wait_ge(pair_summed, k * (BATCH // 2) + ((g + 1) * (GROUP // 2) - BATCH))
                    dve.wait_ge(straight_summed, k * GPB + (g + 1))
                    dve.tensor_tensor(msg[:, par, g * GROUP:(g + 1) * GROUP, 0:D], got[:, g % 2, :, 1, :],
                                      z_ps[g % 2][:, :, D:2 * D], ALU.mult).then_inc(msg_ready, 1)

                def done(n, lag=1):
                    dve.wait_ge(norm_step, k * NS + (n - lag * NS))

                if sums:
                    selectors(k0, par, 0)
                add_last = sums and not (isinstance(k, int) and k == 2)
                if add_last:
                    place = fetch_places(dve, blk_acc[:, q, :], BATCH - GROUP, BLOCKS * AW)
                for j in range(GROUP):
                    if sums and j == 0:
                        dve.wait_ge(norm_turned, k * 3 - 3)
                        dve.tensor_copy(wgt[:, par, 1, :], small_ps[:, 2, :]).then_inc(norm_step, 1)
                    if logits:
                        one_hots(k0, par, 1, j)
                    if sums and j == 0:
                        done(12, 2)
                        dve.tensor_tensor(wgt[:, par, 0, :], wgt[:, par, 1, :], gate[:, par, 0, :], ALU.mult
                                          ).then_inc(norm_step, 1)
                    if sums and j == 2:
                        dve.tensor_tensor(shrink_log[:, :], small_ps[:, 3, :], gate[:, par, 1, :], ALU.mult
                                          ).then_inc(norm_step, 1)
                    if add_last:
                        add_step(k - 1, q, GPB - 1, j, place)
                if logits:
                    bend(0)
                if norm:
                    dve.wait_ge(norm_in[q], k0 * 32 + 64 * par)
                    dve.wait_ge(logit_ready, k)
                    dve.tensor_scalar(logit[:, :], logit_ps[:, :], C.a2_bias[0:BATCH, 0:1], None, ALU.add
                                      ).then_inc(norm_step, 1)
                if logits:
                    weigh(0)
                if norm:
                    done(1)
                    dve.tensor_tensor_scan(before[:, :], mask[:, q, 0, :], logit[:, :], NEG, ALU.add, ALU.max
                                           ).then_inc(norm_step, 1)
                    dve.tensor_tensor_scan(after[:, ::-1], mask[:, q, 1, ::-1], logit[:, ::-1], NEG,
                                           ALU.add, ALU.max).then_inc(norm_step, 1)

                for g in range(1, GPB):
                    if sums:
                        selectors(k0, par, g)
                        place = fetch_places(dve, blk_acc[:, par, :], g * GROUP - GROUP, BLOCKS * AW)
                    for j in range(GROUP):
                        if sums:
                            add_step(k, par, g - 1, j, place)
                        if logits:
                            one_hots(k0, par, g + 1, j)
                        if norm and g == 1 and j == 0:
                            done(3)
                            dve.tensor_tensor(top[:, :], before[:, :], after[:, :], ALU.max
                                              ).then_inc(norm_step, 1)
                        if norm and g == 3 and j == 0:
                            done(8)
                            dve.tensor_tensor(delta[:, :], carried_c[:, :], top[:, 0:1], ALU.subtract
                                              ).then_inc(norm_step, 1)
                            dve.tensor_tensor(diff[:, :], logit[:, :], top[:, :], ALU.subtract
                                              ).then_inc(norm_step, 1)
                        if norm and g == 3 and j == 1:
                            done(9)
                            dve.tensor_scalar(diag[:, :], C.ident[0:BATCH, 0:BATCH], delta[:, 0:1], None, ALU.mult
                                              ).then_inc(norm_step, 1)
                    if logits:
                        bend(g)
                    if norm and g == 1:
                        dve.tensor_copy(carried[:, q, 0:1], carried[:, par, BATCH:BATCH + 1])
                        dve.wait_ge(norm_turned, k * 3 - 2)
                        dve.tensor_tensor(last[:, :], small_ps[0:1, 0, :], carry_tab[:, q, 1, :], ALU.add
                                          ).then_inc(norm_step, 1)
                    if norm and g == 2:
                        dve.wait_ge(norm_turned, k * 3 - 1)
                        dve.tensor_copy(carried_c[:, :], small_ps[0:BATCH, 1, 0:1]).then_inc(norm_step, 1)
                    if logits:
                        weigh(g)
                    if norm and g == 1:
                        done(5)
                        dve.tensor_tensor_scan(carried[:, q, 1:BATCH + 1], carry_tab[:, q, 0, :], last[:, :],
                                               carried[:, q, 0:1], ALU.add, ALU.max).then_inc(norm_step, 1)
                    if norm and g == 2:
                        done(7)
                        dve.scalar_tensor_tensor(out=top[:, :], in0=mask[:, q, 2, :], scalar=carried_c[:, 0:1],
                                                 in1=top[:, :], op0=ALU.add, op1=ALU.max).then_inc(norm_step, 1)
                if not norm and not logits:
                    place = fetch_places(dve, blk_acc[:, par, :], BATCH - GROUP, BLOCKS * AW)
                    for j in range(GROUP):
                        add_step(k, par, GPB - 1, j, place)
            run_batches(dve, emit)


def combine(nc, C, layer):
    with ExitStack() as st:
        K = Kit(nc, st, f"m{layer}_")
        inv = K.sb("inv", [P, BLOCKS])
        own = K.sb("own", [P, 2, 7, D])
        chunk = 7
        loaded = [K.sem(f"loaded{i}") for i in range(2)]
        inverted = K.sem("inverted")
        scaled = K.sem("scaled")
        added = K.sem("added")
        clipped = K.sem("clipped")
        block = K.block()
        rounds = BLOCKS // chunk
        own_v = C.own_tab.rearrange("(r i p) d -> r p i d", p=P, i=chunk)

        @block.sync
        def _(sp):
            for r in range(rounds):
                if r >= 2:
                    sp.wait_ge(added, r - 1)
                sp.dma_start(own[:, r % 2, :, :], own_v[r]).then_inc(loaded[r % 2], 16)

        @block.vector
        def _(dve):
            dve.tensor_scalar(inv[:, :], C.acc[:, 0:BLOCKS, D], 1e-16, None, ALU.add).then_inc(inverted, 1)
            dve.wait_ge(inverted, 1)
            dve.reciprocal(inv[:, :], inv[:, :]).then_inc(inverted, 1)
            dve.wait_ge(inverted, 2)
            for r in range(rounds):
                a = C.acc[:, r * chunk:(r + 1) * chunk, 0:D]
                dve.tensor_tensor(a, a, inv[:, r * chunk:(r + 1) * chunk].unsqueeze(2)
                                  .to_broadcast([P, chunk, D]), ALU.mult).then_inc(scaled, 1)
                dve.wait_ge(scaled, r + 1)
                dve.wait_ge(loaded[r % 2], 16 * (r // 2 + 1))
                dve.tensor_tensor(a, a, own[:, r % 2, :, :], ALU.add).then_inc(added, 1)

        @block.scalar
        def _(act):
            for r in range(rounds):
                act.wait_ge(added, r + 1)
                a = C.acc[:, r * chunk:(r + 1) * chunk, 0:D]
                act.activation(a, a, ACT.Relu).then_inc(clipped, 1)


def neighbour_sums(nc, C):
    with ExitStack() as st:
        K = Kit(nc, st, "s_")
        depth = 2
        index = K.sb("index", [P, 2, BATCH], I32)
        blk = K.sb("blk", [1, 2, BATCH], I32)
        dstc = K.sb("dstc", [P, 2, BATCH])
        got = K.sb("got", [P, GPB, GROUP, AW])
        sel = K.sb("sel", [P, 2, GROUP, P])
        sum_ps = [K.ps(f"sum_ps{i}", [P, 2, 2 * P]) for i in range(2)]
        tabs_in = [K.sem(f"tabs_in{i}") for i in range(2)]
        got_in = [K.gather_sem(C.root, f"got_in{i}") for i in range(BATCH)]
        cleared = K.sem("cleared")
        passed = K.sem("passed")
        sel_ready = K.sem("sel_ready")
        pair_summed = K.sem("pair_summed")
        step_added = K.sem("step_added")
        block = K.block()
        acc = C.acc[:, :, :].rearrange("p b w -> p (b w)")

        def batches(engine, emit):
            for par in range(2):
                emit(0, par)
            with engine.Fori(1, NBATCH // 2) as pair:
                for par in range(2):
                    emit(pair * 2, par)

        @block.sync
        def _(sp):
            def emit(k0, par):
                k = k0 + par
                waits(sp, step_added, k * BATCH - BATCH)
                sp.dma_start(index[:, par, :], C.index_tab[bass.ds(k, 1), :, :]
                             .rearrange("b p j -> (b p) j")).then_inc(tabs_in[par], 16)
                sp.dma_start(dstc[:, par, :], C.dst_tab[bass.ds(k, 1), :, :]
                             .rearrange("b p j -> (b p) j")).then_inc(tabs_in[par], 16)
                sp.dma_start(blk[0:1, par, :], C.block_tab[bass.ds(k, 1), 1, :]).then_inc(tabs_in[par], 16)
            batches(sp, emit)

        @block.gpsimd
        def _(pool):
            pool.memset(got[:, :, :, D], 1.0).then_inc(cleared, 1)

            def emit(k0, par):
                k = k0 + par
                pool.wait_ge(tabs_in[par], k0 * 24 + 48)
                for g in range(GPB):
                    wait_alone(pool, pair_summed, k * (BATCH // 2) + (g * GROUP - BATCH + GROUP) // 2, passed)
                    for j in range(GROUP):
                        n = g * GROUP + j
                        pool.indirect_dma_start(
                            got[:, g, j, 0:D], None, C.h_tab,
                            bass.IndirectOffsetOnAxis(ap=index[:, par, n:n + 1], axis=0)).then_inc(got_in[n], 16)
            batches(pool, emit)

        @block.tensor
        def _(pe):
            pe.wait_ge(cleared, 2)

            def emit(k0, par):
                k = k0 + par
                for g in range(GPB):
                    pe.wait_ge(sel_ready, k * GPB + (g + 1))
                    for j in range(GROUP):
                        n = g * GROUP + j
                        pe.wait_ge(got_in[n], k * 16 + 16)
                        if j % 2 == 0:
                            waits(pe, step_added, k * BATCH + (n - 2))
                        mm = pe.matmul(sum_ps[j // 2][:, j % 2, 0:AW], sel[:, g % 2, j, :], got[:, g, j, :],
                                       start=True, stop=True)
                        if j % 2 == 1:
                            mm.then_inc(pair_summed, 1)
            batches(pe, emit)

        @block.vector
        def _(dve):
            dve.memset(C.acc[:, :, :], 0.0).then_inc(cleared, 1)
            dve.wait_ge(cleared, 2)

            def emit(k0, par):
                k = k0 + par
                dve.wait_ge(tabs_in[par], k0 * 24 + 48)
                for g in range(GPB):
                    waits(dve, pair_summed, k * (BATCH // 2) + (g * GROUP - GROUP) // 2)
                    dve.tensor_tensor(sel[:, g % 2, :, :], C.iota_free[:, :].unsqueeze(1).to_broadcast([P, GROUP, P]),
                                      dstc[:, par, g * GROUP:(g + 1) * GROUP].unsqueeze(2).to_broadcast([P, GROUP, P]),
                                      ALU.is_equal).then_inc(sel_ready, 1)
                    place = fetch_places(dve, blk[:, par, :], g * GROUP, BLOCKS * AW)
                    for j in range(GROUP):
                        n = g * GROUP + j
                        if j % 2 == 0:
                            dve.wait_ge(pair_summed, k * (BATCH // 2) + (n // 2 + 1))
                        waits(dve, step_added, k * BATCH + n)
                        a = acc[:, bass.ds(place[j], AW)]
                        dve.tensor_tensor(a, a, sum_ps[j // 2][:, j % 2, 0:AW], ALU.add).then_inc(step_added, 1)
            batches(dve, emit)


def finish(nc, C, w1, b1, out):
    with ExitStack() as st:
        K = Kit(nc, st, "f_")
        w = K.sb("w", [P, D])
        bias = K.sb("bias", [P, D])
        inv = K.sb("inv", [P, BLOCKS])
        h = K.sb("h", [P, BLOCKS // 2, D])
        skip = K.sb("skip", [P, BLOCKS, D])
        x_now = K.sb("x_now", [P, 2, D])
        xt = K.sb("xt", [P, 2, P])
        lin = K.sb("lin", [P, 2, D])
        xt_ps = [K.ps(f"xt_ps{i}", [P, P]) for i in range(2)]
        out_ps = [K.ps(f"out_ps{i}", [P, D]) for i in range(2)]
        loaded = K.sem("loaded")
        h_in = K.sem("h_in")
        skip_in = K.sem("skip_in")
        inverted = K.sem("inverted")
        scaled = K.sem("scaled")
        added = K.sem("added")
        staged = K.sem("staged")
        turned = K.sem("turned")
        copied = K.sem("copied")
        projected = K.sem("projected")
        biased = K.sem("biased")
        finished = K.sem("finished")
        stored = K.sem("stored")
        half = BLOCKS // 2
        h_v = C.h_tab.rearrange("(r i p) d -> r p i d", p=P, i=half)
        block = K.block()

        @block.sync
        def _(sp):
            sp.dma_start(w[:, :], w1[:, :]).then_inc(loaded, 16)
            sp.dma_start(bias[:, :], over_partitions(row(b1))).then_inc(loaded, 16)
            sp.dma_start(h[:, :, :], h_v[0]).then_inc(h_in, 16)
            sp.dma_start(skip[:, :, :], C.skip_tab.rearrange("(i p) d -> p i d", p=P)).then_inc(skip_in, 16)
            sp.wait_ge(added, 1)
            sp.dma_start(h[:, :, :], h_v[1]).then_inc(h_in, 16)
            sp.wait_ge(finished, BLOCKS)
            sp.dma_start(out[0:FULL_BLOCKS * P, :].rearrange("(i p) d -> p i d", p=P), skip[:, 0:FULL_BLOCKS, :]
                         ).then_inc(stored, 16)
            sp.dma_start(out[FULL_BLOCKS * P:NODES, :], skip[0:TAIL_NODES, FULL_BLOCKS, :]).then_inc(stored, 16)
            sp.wait_ge(stored, 32)

        @block.tensor
        def _(pe):
            pe.wait_ge(loaded, 32)
            pe.wait_ge(staged, 1)
            pe.transpose(xt_ps[0][:, :], x_now[:, 0, :], C.ident[:, :]).then_inc(turned, 1)
            with pe.Fori(0, BLOCKS // 2) as pair:
                i = pair * 2
                for n in range(2):
                    pe.wait_ge(staged, i + (n + 2))
                    pe.transpose(xt_ps[1 - n][:, :], x_now[:, 1 - n, :], C.ident[:, :]).then_inc(turned, 1)
                    pe.wait_ge(copied, i + (n + 1))
                    pe.wait_ge(biased, i + (n + 1))
                    pe.matmul(out_ps[n][:, :], xt[:, n, :], w[:, :], start=True, stop=True).then_inc(projected, 1)

        @block.scalar
        def _(act):
            act.wait_ge(added, 2)
            act.activation(x_now[:, 0, :], C.acc[:, 0, 0:D], ACT.Copy).then_inc(staged, 1)
            with act.Fori(0, BLOCKS // 2) as pair:
                i = pair * 2
                for n in range(2):
                    act.activation(x_now[:, 1 - n, :], C.acc[:, bass.ds(i + (n + 1), 1), 0:D]
                                   .rearrange("p a d -> p (a d)"), ACT.Copy).then_inc(staged, 1)
                    act.wait_ge(turned, i + (n + 1))
                    act.wait_ge(biased, i + (n + 1))
                    act.activation(xt[:, n, :], xt_ps[n][:, :], ACT.Copy).then_inc(copied, 1)

        @block.vector
        def _(dve):
            dve.sem_inc(biased, 2)
            dve.tensor_scalar(inv[:, :], C.acc[:, 0:BLOCKS, D], 1.0, None, ALU.max).then_inc(inverted, 1)
            dve.wait_ge(inverted, 1)
            dve.reciprocal(inv[:, :], inv[:, :]).then_inc(inverted, 1)
            dve.wait_ge(inverted, 2)
            for r in range(2):
                a = C.acc[:, r * half:(r + 1) * half, 0:D]
                dve.tensor_tensor(a, a, inv[:, r * half:(r + 1) * half].unsqueeze(2)
                                  .to_broadcast([P, half, D]), ALU.mult).then_inc(scaled, 1)
                dve.wait_ge(scaled, r + 1)
                dve.wait_ge(h_in, 16 * (r + 1))
                dve.tensor_tensor(a, a, h[:, :, :], ALU.add).then_inc(added, 1)
            dve.wait_ge(loaded, 32)
            dve.wait_ge(skip_in, 16)
            with dve.Fori(0, BLOCKS // 2) as pair:
                i = pair * 2
                for n in range(2):
                    dve.wait_ge(projected, i + (n + 1))
                    dve.tensor_tensor(lin[:, n, :], out_ps[n][:, :], bias[:, :], ALU.add).then_inc(biased, 1)
                    dve.wait_ge(biased, i + (n + 3))
                    s = skip[:, bass.ds(i + n, 1), :].rearrange("p a d -> p (a d)")
                    dve.scalar_tensor_tensor(out=s, in0=lin[:, n, :], scalar=0.0, in1=s, op0=ALU.max,
                                             op1=ALU.add).then_inc(finished, 1)


def gnn(nc, x, src, dst, etype, weight, rel_emb, wv, bv, w0, b0, a1w, a1b, a2w, a2b, gw, gb, w1, b1, out):
    class C:
        pass

    with ExitStack() as st:
        K = Kit(nc, st)
        C.root = K

        def dram(name, shape, dt=F32):
            return nc.dram_tensor(name, shape, dt, kind="Internal").ap()

        C.edge_tab = dram("edge_tab", [STEPS, 4 * P], I32)
        C.facts_tab = dram("facts_tab", [4, STEPS + BATCH])
        C.row_tab = dram("row_tab", [STEPS, 2 * P], BF16)
        C.mask_tab = dram("mask_tab", [STEPS, 3 * P])
        C.index_tab = dram("index_tab", [NBATCH, P, BATCH], I32)
        C.dst_tab = dram("dst_tab", [NBATCH, P, BATCH])
        C.gate_tab = dram("gate_tab", [NBATCH, P, 3, BATCH])
        C.carry_tab = dram("carry_tab", [NBATCH, 2, BATCH])
        C.block_tab = dram("block_tab", [NBATCH, 2, BATCH], I32)
        C.source_tab = dram("source_tab", [BLOCKS * P, 2 * D])
        C.own_tab = dram("own_tab", [BLOCKS * P, D])
        C.h_tab = dram("h_tab", [BLOCKS * P, D])
        C.skip_tab = dram("skip_tab", [BLOCKS * P, D])

        C.ident = K.sb("ident", [P, P])
        C.ones = K.sb("ones", [P, P])
        C.iota_free = K.sb("iota_free", [P, P])
        C.iota_part = K.sb("iota_part", [P, 3])
        make_constants(nc, C)
        plan_steps(nc, C, src, dst, etype, weight, gw, gb)
        C.acc = K.sb("acc", [P, BLOCKS + 1, AW])
        layer_norm(nc, C, "l0_", x, False)
        with ExitStack() as att:
            A = Kit(nc, att)
            C.node_q = A.sb("node_q", [P, BLOCKS + 1, 3, D], BF16)
            C.rel_tabs = A.sb("rel_tabs", [P, len(RELP), 2, D], BF16)
            C.a2_row = A.sb("a2_row", [P, D])
            C.a2_sign = A.sb("a2_sign", [P, D])
            C.a2_bias = A.sb("a2_bias", [P, 1])
            for layer in range(LAYERS):
                relation_tables(nc, C, layer, rel_emb, a1w, a1b, a2w, a2b)
                node_tables(nc, C, layer, a1w, wv, bv, w0, b0)
                attention(nc, C, layer)
                combine(nc, C, layer)
        layer_norm(nc, C, "l1_", x, True)
        neighbour_sums(nc, C)
        finish(nc, C, w1, b1, out)


_INS = ["x", "src", "dst", "edge_type_200", "edge_weight", "L0_gnn_rel_emb", "L0_gnn_Wv_w", "L0_gnn_Wv_b",
        "L0_gnn_W0_w", "L0_gnn_W0_b", "L0_gnn_A1_w", "L0_gnn_A1_b", "L0_gnn_A2_w", "L0_gnn_A2_b",
        "L0_gnn_G_w", "L0_gnn_G_b", "L1_gnn_W", "L1_gnn_b"]


def kernel(**inputs):
    import numpy as np
    from concourse import bacc
    from concourse.bass_utils import run_bass_kernel_spmd

    nc = bacc.Bacc("TRN2", target_bir_lowering=False, num_devices=1)
    arrays, args = {}, []
    for name in _INS:
        a = np.ascontiguousarray(inputs[name])
        arrays[f"in_{name}"] = a
        args.append(nc.dram_tensor(f"in_{name}", a.shape, mybir.dt.from_np(a.dtype), kind="ExternalInput").ap())
    args.append(nc.dram_tensor("out_0", (NODES, D), F32, kind="ExternalOutput").ap())
    gnn(nc, *args)
    r = run_bass_kernel_spmd(nc, [arrays], core_ids=[0])
    return r.results[0]["out_0"]
```
